# Optimizing a Trainium2 kernel written in Bass

```python
import numpy as np
import jax
import jax.numpy as jnp

def _softmax(x, axis=-1):
    return jax.nn.softmax(x, axis=axis)

def _gelu(x):
    return jax.nn.gelu(x, approximate=True)

def _silu(x):
    return jax.nn.silu(x)

def _sigmoid(x):
    return jax.nn.sigmoid(x)

def _layernorm(x, axis=-1, eps=1e-05):
    m = jnp.mean(x, axis=axis, keepdims=True)
    v = jnp.var(x, axis=axis, keepdims=True)
    return (x - m) / jnp.sqrt(v + eps)

def _scatter_add(tgt, idx, src, axis=0):
    return tgt.at[idx].add(src)

def _segment_sum(src, seg, n):
    return jax.ops.segment_sum(src, seg, n)
kernel_name = 'mk_gnn_ffn_d1_gnn_r8_13c8d2'

def setup_inputs(seed: int=0):
    np.random.seed(seed)
    _w = jnp.asarray

    def _rec_inputs():
        import jax
        import jax.numpy as jnp
        _gk = jax.random.key(seed)
        x = -0.0006008 + 1.001 * jax.random.normal(jax.random.fold_in(_gk, 1), (6250, 256), jnp.float32)
        src = jax.random.randint(jax.random.fold_in(_gk, 2), (100000,), 0, 6250, jnp.int32)
        dst = jnp.minimum((6250 * jax.random.uniform(jax.random.fold_in(_gk, 3), (100000,)) ** 2.0).astype(jnp.int32), 49999)
        _o = jnp.argsort(dst, stable=True)
        src = src[_o]
        dst = dst[_o]
        return (x, src, dst)
    x, src, dst = _rec_inputs()

    def _L0_gnn_setup():
        import jax, jax.numpy as jnp
        import numpy as np
        N = 1250
        E = 40000
        D = 256
        key = jax.random.key(seed)
        ks = jax.random.split(key, 10)
        s = 1.0 / np.sqrt(D)
        return {'x0': jax.random.normal(ks[0], (N, D), jnp.float32), 'edge_index': jax.random.randint(ks[1], (2, E), 0, N, jnp.int32), 'W1': jax.random.normal(ks[2], (D, D), jnp.float32) * s, 'b1': jax.random.normal(ks[3], (D,), jnp.float32) * s, 'W2': jax.random.normal(ks[4], (D, D), jnp.float32) * s, 'b2': jax.random.normal(ks[5], (D,), jnp.float32) * s, 'wa1': jax.random.normal(ks[6], (D,), jnp.float32) * s, 'ba1': jax.random.normal(ks[7], (1,), jnp.float32) * s, 'wa2': jax.random.normal(ks[8], (D,), jnp.float32) * s, 'ba2': jax.random.normal(ks[9], (1,), jnp.float32) * s}
    _L0_gnn_all = _L0_gnn_setup()
    _L0_gnn_in = {k: v for k, v in _L0_gnn_all.items() if k in ('W1', 'b1', 'W2', 'b2', 'wa1', 'ba1', 'wa2', 'ba2')}
    del _L0_gnn_all

    def _L0_ffn_setup():
        import jax, jax.numpy as jnp
        import numpy as np
        TOP_K = 2
        key = jax.random.key(seed)
        ks = jax.random.split(key, 4)
        B, L, D, H, E = (8, 512, 256, 1024, 8)
        s = 0.02
        return {'x': jax.random.normal(ks[0], (B, L, D), jnp.float32), 'Wg': jax.random.normal(ks[1], (D, E), jnp.float32) * s, 'bg': jnp.zeros((E,), jnp.float32), 'W1': jax.random.normal(ks[2], (E, D, H), jnp.float32) * s, 'b1': jnp.zeros((E, H), jnp.float32), 'W2': jax.random.normal(ks[3], (E, H, D), jnp.float32) * s, 'b2': jnp.zeros((E, D), jnp.float32)}
    _L0_ffn_all = _L0_ffn_setup()
    _L0_ffn_in = {k: v for k, v in _L0_ffn_all.items() if k in ('Wg', 'bg', 'W1', 'b1', 'W2', 'b2')}
    del _L0_ffn_all
    return {'x': x, 'src': src, 'dst': dst, 'L0_gnn_W1': _L0_gnn_in['W1'], 'L0_gnn_b1': _L0_gnn_in['b1'], 'L0_gnn_W2': _L0_gnn_in['W2'], 'L0_gnn_b2': _L0_gnn_in['b2'], 'L0_gnn_wa1': _L0_gnn_in['wa1'], 'L0_gnn_ba1': _L0_gnn_in['ba1'], 'L0_gnn_wa2': _L0_gnn_in['wa2'], 'L0_gnn_ba2': _L0_gnn_in['ba2'], 'L0_ffn_Wg': _L0_ffn_in['Wg'], 'L0_ffn_bg': _L0_ffn_in['bg'], 'L0_ffn_W1': _L0_ffn_in['W1'], 'L0_ffn_b1': _L0_ffn_in['b1'], 'L0_ffn_W2': _L0_ffn_in['W2'], 'L0_ffn_b2': _L0_ffn_in['b2']}

def reference(x, src, dst, L0_gnn_W1, L0_gnn_b1, L0_gnn_W2, L0_gnn_b2, L0_gnn_wa1, L0_gnn_ba1, L0_gnn_wa2, L0_gnn_ba2, L0_ffn_Wg, L0_ffn_bg, L0_ffn_W1, L0_ffn_b1, L0_ffn_W2, L0_ffn_b2):
    import jax
    import jax.numpy as jnp

    def _L0_gnn_ref(x0, edge_index, W1, b1, W2, b2, wa1, ba1, wa2, ba2):
        import jax, jax.numpy as jnp
        import numpy as np
        N = 1250
        E = 40000
        D = 256
        n = x0.shape[0]
        leaky = lambda v: jax.nn.leaky_relu(v, 0.2)
        x0_i = leaky(x0 @ W1 + b1)
        x0_j = leaky(x0 @ W2 + b2)
        a1 = x0_i @ wa1 + ba1[0]
        a2 = x0_j @ wa2 + ba2[0]
        row, col = (edge_index[0], edge_index[1])
        att = jax.nn.sigmoid(a1[row] + a2[col])
        msg = att[:, None] * x0_j[col]
        out = jax.ops.segment_sum(msg, row, num_segments=n)
        return out + x0

    def _L0_ffn_ref(x, Wg, bg, W1, b1, W2, b2):
        import jax, jax.numpy as jnp
        import numpy as np
        TOP_K = 2
        B, L, D = x.shape
        E = W1.shape[0]
        xf = x.reshape(-1, D)
        gate_logits = xf @ Wg + bg
        top_w, top_i = jax.lax.top_k(gate_logits, TOP_K)
        top_w = jax.nn.softmax(top_w, axis=-1)
        w_dense = jnp.sum(jax.nn.one_hot(top_i, E, dtype=xf.dtype) * top_w[..., None], axis=1)
        out = jnp.zeros_like(xf)
        for e in range(E):
            h = jax.nn.gelu(xf @ W1[e] + b1[e], approximate=False)
            out = out + w_dense[:, e:e + 1] * (h @ W2[e] + b2[e])
        return out.reshape(B, L, D)
    edge_index = jnp.stack([src, dst])
    x = x + _L0_gnn_ref(_layernorm(x, axis=-1), edge_index, L0_gnn_W1, L0_gnn_b1, L0_gnn_W2, L0_gnn_b2, L0_gnn_wa1, L0_gnn_ba1, L0_gnn_wa2, L0_gnn_ba2)
    x = x + _L0_ffn_ref(_layernorm(x, axis=-1)[None], L0_ffn_Wg, L0_ffn_bg, L0_ffn_W1, L0_ffn_b1, L0_ffn_W2, L0_ffn_b2)[0]
    return x

_drawn_inputs = setup_inputs


def setup_inputs(seed=0):
    import zlib

    import numpy as np

    out = dict(_drawn_inputs(seed))
    spreads = {'L0_ffn_bg': (0.0, 0.697), 'L0_ffn_b1': (0.0, 0.8), 'L0_ffn_b2': (0.0, 0.486)}
    factors = {'L0_gnn_b1': 6.461, 'L0_ffn_W1': 3.17, 'L0_ffn_W2': 2.947}
    for name, (base, spread) in spreads.items():
        noise = np.random.default_rng([zlib.crc32(name.encode()), seed]).standard_normal(out[name].shape)
        drawn = base * np.exp(spread * noise) if base else spread * noise
        out[name] = jnp.asarray(drawn.astype(out[name].dtype))
    for name, factor in factors.items():
        out[name] = (out[name] * factor).astype(out[name].dtype)
    return out
```

```python
from contextlib import ExitStack

import concourse.bass as bass
from concourse import mybir

ALU = mybir.AluOpType
ACT = mybir.ActivationFunctionType
AX_X = mybir.AxisListType.X
F32 = mybir.dt.float32
F16 = mybir.dt.float16
BF16 = mybir.dt.bfloat16
I32 = mybir.dt.int32
U16 = mybir.dt.uint16
U32 = mybir.dt.uint32

P = 128
EPS = 1e-5
SLOPE = 0.2
TOP_K = 2
FFN_ROWS = 256
GROUP = 8
BODY = 16
HALF = BODY // 2
SORTS_PER_BODY = 3


def ceil_div(a, b):
    return -(-a // b)


def gnn_moe_kernel(nc, x, src, dst, g_w1, g_b1, g_w2, g_b2, wa1, ba1, wa2, ba2,
                   w_gate, b_gate, f_w1, f_b1, f_w2, f_b2, out):
    N, D = x.shape
    (E,) = src.shape
    X, _, H = f_w1.shape
    KD, KH = D // P, H // P
    REAL = ceil_div(N, P)
    LAST = N - (REAL - 1) * P
    NB = ceil_div(REAL, 2) * 2
    EC = ceil_div(E, P)
    FULL = E // P
    TAIL = E - FULL * P
    COLS = ceil_div(EC, GROUP) * GROUP

    def tiles_for(cols):
        return (cols * P + REAL * (P - 1)) // P

    WA = 304
    WB = COLS - WA
    WB_REAL = EC - WA
    TA = ceil_div(tiles_for(WA), BODY) * BODY
    TB = ceil_div(tiles_for(WB_REAL), BODY) * BODY
    TMAX = max(TA, TB)
    SORT_BODIES = WB // GROUP // SORTS_PER_BODY
    assert WB % (GROUP * SORTS_PER_BODY) == 0 and SORT_BODIES <= TA // BODY
    assert TB % 2 == 0 and TB // 2 <= 512 and TA <= 512 and max(WA, WB) <= 512
    PARTS = ((0, WA, TA), (WA, WB, TB))
    CUTS = (((0, TA),), ((0, TB // 2), (TB // 2, TB)))
    FT = (TOP_K * N + X * (FFN_ROWS - 1)) // FFN_ROWS
    DEAD = 1 << 14
    ROW = D + 1

    table = nc.dram_tensor("table", (NB * P, ROW), F32).ap()
    xs = nc.dram_tensor("xs", (FT * FFN_ROWS, D), F32).ap()
    os = nc.dram_tensor("os", (FT * FFN_ROWS, D), F32).ap()

    with ExitStack() as ctx:
        def sb(name, shape, dt=F32):
            return ctx.enter_context(nc.sbuf_tensor(name, shape, dt))

        def sem(name):
            return ctx.enter_context(nc.semaphore(name))

        banks = [ctx.enter_context(nc.psum_tensor(f"bank{i}", [P, 512], F32)) for i in range(8)]

        acc = sb("acc", [P, NB, D])
        ident = sb("ident", [P, P])
        ones = sb("ones", [P, P])
        iota_f32 = sb("iota_f32", [P, P])
        iota_1 = sb("iota_1", [P, P])
        iota_16 = sb("iota_16", [P, TMAX], F16)
        below = sb("below", [P, P])
        mean2 = sb("mean2", [P, NB])
        spread = sb("spread", [P, NB])
        rstd = sb("rstd", [P, NB])
        shift = sb("shift", [P, NB])
        row_f = sb("row_f", [P, TMAX])
        part = [dict(
            sender=sb(f"sender{n}", [P, t], I32), receiver=sb(f"receiver{n}", [P, t]),
            block=sb(f"block{n}", [P, t], I32)) for n, (_, _, t) in enumerate(PARTS)]
        a1row = sb("a1row", [P, NB, P])
        ring = sb("ring", [P, BODY, ROW])
        gate = sb("gate", [P, 4, P])
        lhs = sb("lhs", [P, 4, P])
        places = sb("places", [P, 2, HALF], I32)


        ARENA = 19 * 1024 + 512
        arena = sb("arena", [P, ARENA])
        used = [0]

        def cut(shape, dt=F32):
            n = 1
            for m in shape:
                n *= m
            words = ceil_div(n * (2 if dt in (F16, BF16) else 4), 32) * 8
            a = arena[:, used[0]:used[0] + words]
            used[0] += words
            assert used[0] <= ARENA, used[0]
            a = (a if dt == F32 else a.bitcast(dt))[:, 0:n]
            if len(shape) == 2:
                a = a.rearrange("p (a b) -> p a b", a=shape[0])
            if len(shape) == 3:
                a = a.rearrange("p (a b c) -> p a b c", a=shape[0], b=shape[1])
            return a

        tmp_i = cut([COLS], I32)
        src_i = cut([COLS], I32)
        dst_i = cut([COLS], I32)
        block16 = cut([COLS], BF16)
        v1_16 = cut([COLS], F16)
        v2_16 = cut([COLS], F16)
        posl_16 = cut([COLS], F16)
        post_f = cut([COLS])
        pos_f = cut([COLS])
        unit = cut([2 * P], BF16)
        iota_m = cut([P, GROUP], F16)
        after_sort = used[0]
        sel = cut([NB, P], BF16)
        below16 = cut([P], BF16)
        mask = [cut([COLS], BF16) for _ in range(2)]
        a1flat = a1row[:, :, :].rearrange("p b m -> p (b m)")
        count_f, scan_f, ones_row = (a1flat[:, n * COLS:(n + 1) * COLS] for n in range(3))
        carry_i, digit_i = (a1flat[:, n * COLS:(n + 1) * COLS].bitcast(I32) for n in (3, 4))
        carry = [cut([COLS], BF16) for _ in range(3)]
        first_rows = cut([P], F16)
        after = cut([TMAX], F16)
        small = cut([16])
        small_i = cut([16], I32)
        wcat = cut([KD, 2 * D])
        bcat = cut([2 * D])
        wa = cut([2, D])
        ba = cut([2])
        xn = cut([2, D])
        xt = cut([2, KD, P])
        xij = cut([2, 2, ROW])
        junk = cut([2, D])
        a1diag = cut([4, P])
        used[0] = after_sort
        hot = [cut([P, GROUP], F16) for _ in range(2)]
        hot1 = [cut([P, GROUP], F16) for _ in range(2)]
        hot2 = [cut([P, GROUP], F16) for _ in range(2)]
        tile_hot = [cut([GROUP, TMAX], F16) for _ in range(2)]
        out_v1 = cut([TMAX])
        out_v2 = cut([TMAX], I32)
        out_hi = cut([TMAX], I32)
        used[0] = 0
        W1 = [cut([KD, H]) for _ in range(2)]
        W2 = [cut([KH, D]) for _ in range(2)]
        b2all = cut([X, D])
        hT = [cut([KH, FFN_ROWS]) for _ in range(2)]
        xg = [cut([2, D]) for _ in range(2)]
        xgT = [cut([KD, FFN_ROWS]) for _ in range(2)]
        yo = [cut([2, D]) for _ in range(2)]
        back = cut([4, 2, D])

        b1T = sb("b1T", [P, X * KH])
        b1raw = sb("b1raw", [X * KH, P])
        wg = sb("wg", [P, KD, X])
        bg = sb("bg", [P, X])
        yn = ring[:, :, :].rearrange("p a b -> p (a b)")[:, 0:8 * D].rearrange("p (a b) -> p a b", a=8)
        ynT = gate[:, :, :]
        logits = sb("logits", [P, NB, X])
        stats = logits[:, :, 0:6]
        top = sb("top", [P, TOP_K, NB])
        hit = sb("hit", [P, NB, X])
        lead = sb("lead", [P, NB, X])
        diff = sb("diff", [P, NB])
        wk = [sb(f"wk{k}", [P, NB]) for k in range(TOP_K)]
        idx = [sb(f"idx{k}", [P, NB]) for k in range(TOP_K)]
        eh = [sb(f"eh{k}", [P, X, NB]) for k in range(TOP_K)]
        ehs = sb("ehs", [P, X, NB])
        esc = sb("esc", [P, X, NB])
        valid = sb("valid", [P, NB])
        etot = sb("etot", [P, X])
        et = sb("et", [P, 6, X])
        eti = sb("eti", [P, X], I32)
        posk_f = sb("posk_f", [P, NB])
        posk = sb("posk", [P, NB, TOP_K], I32)
        placesk = sb("placesk", [P, 4, TOP_K], I32)
        zeros = ring[:, :, :].rearrange("p a b -> p (a b)")[:, 0:4 * D]
        ecmp = sb("ecmp", [P, FT, X])
        esum = sb("esum", [P, FT])
        expert = sb("expert", [P, FT], I32)
        a1col = sb("a1col", [P, NB])

        def chain(eng, name):
            s, n = sem(name), [0]

            def link(ins):
                n[0] += 1
                ins.then_inc(s, 1)
                eng.wait_ge(s, n[0])
            return link


        def flat(ap):
            return ap.rearrange("p a b -> p (a b)")

        s_dummy = sem("carries_pool_waits")
        s_dve = sem("carries_dve_waits")
        s_pe = sem("carries_pe_waits")

        s_const = sem("constants_ready")
        s_x = [sem(f"x_loaded{n}") for n in range(5)]
        s_w = sem("weights_loaded")
        s_e = sem("edges_loaded")
        XG = [0, 12, 24, 36, REAL - 1]

        with nc.Block() as block:
            @block.vector
            def _(dve):
                nc.vector.memset(src_i[:, FULL:COLS], DEAD)
                nc.vector.memset(dst_i[:, FULL:COLS], 0)
                nc.vector.memset(acc[:, REAL - 1:NB, :], 0.0)
                nc.vector.memset(ones[:, :], 1.0)
                nc.vector.memset(zeros, 0.0)
                nc.vector.memset(ones_row, 1.0)
                nc.vector.memset(unit, 0.0)
                nc.vector.memset(pos_f, -1.0).then_inc(s_const, 1)
                dve.wait_ge(s_const, 1)
                nc.vector.memset(unit[:, P:P + 1], 1.0).then_inc(s_const, 1)

            @block.sync
            def _(sp):
                sp.wait_ge(s_const, 2)
                for dram, tile in ((src, src_i), (dst, dst_i)):
                    sp.dma_start(tile[:, 0:FULL], dram[0:FULL * P].rearrange("(p j) -> p j", p=P)).then_inc(s_e, 16)
                    sp.dma_start(tile[0:TAIL, FULL:FULL + 1],
                                 dram[FULL * P:E].rearrange("(p j) -> p j", j=1)).then_inc(s_e, 16)
                for n in range(4):
                    a, b = XG[n], XG[n + 1]
                    sp.dma_start(acc[:, a:b, :], x[a * P:b * P, :].rearrange("(b p) d -> p b d", p=P)).then_inc(s_x[n], 16)
                sp.dma_start(acc[0:LAST, REAL - 1, :], x[(REAL - 1) * P:N, :]).then_inc(s_x[4], 16)

            @block.scalar
            def _(act):
                for n, (w, b, wv, bv) in enumerate(((g_w2, g_b2, wa2, ba2), (g_w1, g_b1, wa1, ba1))):
                    act.dma_start(wcat[:, :, n * D:(n + 1) * D], w.rearrange("(k p) n -> p k n", p=P)).then_inc(s_w, 16)
                    act.dma_start(bcat[0:1, n * D:(n + 1) * D], b.rearrange("(a n) -> a n", a=1)).then_inc(s_w, 16)
                    act.dma_start(wa[:, n, :], wv.partition_broadcast(P)).then_inc(s_w, 16)
                    act.dma_start(ba[:, n:n + 1], bv.partition_broadcast(P)).then_inc(s_w, 16)
                act.dma_start(wg[:, :, :], w_gate.rearrange("(k p) e -> p k e", p=P)).then_inc(s_w, 16)
                act.dma_start(bg[:, :], b_gate.partition_broadcast(P)).then_inc(s_w, 16)
                act.dma_start(b1raw[:, :], f_b1.rearrange("e (k p) -> (e k) p", p=P)).then_inc(s_w, 16)

            @block.gpsimd
            def _(pool):
                link = chain(pool, "pool_constants")
                nc.gpsimd.memset(sel, 1.0)
                nc.gpsimd.memset(first_rows, 1.0)
                nc.gpsimd.memset(below[:, :], 1.0)
                nc.gpsimd.memset(below16, 1.0)
                nc.gpsimd.memset(valid[:, :], 1.0)
                nc.gpsimd.memset(ident[:, :], 1.0)
                link(nc.gpsimd.iota(tmp_i, [[1, COLS]], base=0, channel_multiplier=0))
                nc.gpsimd.tensor_copy(iota_16[:, :], tmp_i[:, 0:TMAX])
                nc.gpsimd.tensor_copy(row_f[:, :], tmp_i[:, 0:TMAX])
                nc.gpsimd.tensor_copy(iota_m, tmp_i[:, 0:P].unsqueeze(2).to_broadcast([P, P, GROUP]))
                nc.gpsimd.tensor_copy(iota_1[:, :], tmp_i[:, 1:P + 1])
                nc.gpsimd.affine_select(out=sel, in_=sel, pattern=[[-1, NB], [0, P]], base=0, channel_multiplier=1,
                                        compare_op=ALU.is_equal, fill=0.0)
                nc.gpsimd.affine_select(out=first_rows, in_=first_rows, pattern=[[0, P]], base=REAL - 1,
                                        channel_multiplier=-1, compare_op=ALU.is_gt, fill=0.0)
                nc.gpsimd.affine_select(out=below[:, :], in_=below[:, :], pattern=[[1, P]], base=0,
                                        channel_multiplier=-1, compare_op=ALU.is_gt, fill=0.0)
                nc.gpsimd.affine_select(out=below16, in_=below16, pattern=[[1, P]], base=0,
                                        channel_multiplier=-1, compare_op=ALU.is_gt, fill=0.0)
                nc.gpsimd.affine_select(out=valid[:, :], in_=valid[:, :], pattern=[[-P, NB]], base=N,
                                        channel_multiplier=-1, compare_op=ALU.is_gt, fill=0.0)
                link(nc.gpsimd.affine_select(out=ident[:, :], in_=ident[:, :], pattern=[[-1, P]], base=0,
                                             channel_multiplier=1, compare_op=ALU.is_equal, fill=0.0))

        s_mask = sem("mask_ready")
        s_counted = sem("mask_counted")
        s_cnt = sem("counts_ready")
        s_tiles = sem("tiles_ready")
        s_base = sem("bases_ready")
        s_cmp = sem("ends_compared")
        s_blk = sem("tile_blocks_ready")
        s_carry = sem("carries_ready")
        s_rank = sem("ranks_ready")
        s_ranked = sem("ranks_taken")
        s_bn = sem("moments_taken")
        s_var = sem("variance_ready")
        s_sd = sem("deviation_ready")
        s_xn = sem("xn_ready")
        s_acc = sem("xn_added")
        s_xnT = sem("xn_transposed")
        s_xt = sem("xt_ready")
        s_lin = sem("linear_ready")
        s_xij = sem("xij_ready")
        s_dot = sem("dots_ready")
        s_a2 = sem("table_row_ready")
        s_tab = [sem(f"table_stored{u}") for u in range(2)]
        s_diag = sem("a1_spread")
        s_a1r = sem("a1_row_copied")
        s_a1b = sem("a1_broadcast")
        s_a1c = sem("a1row_ready")
        s_xs0 = sem("xs_zeroed")
        s_zero = sem("zeros_ready")
        RANK_CUTS = ((0, WA), (WA, COLS))

        def moments(dve, link, done):
            with dve.Fori(0, NB) as b:
                nc.vector.bn_stats(flat(stats[:, bass.ds(b, 1), :]), flat(acc[:, bass.ds(b, 1), :])).then_inc(s_bn, 1)
            dve.wait_ge(s_bn, NB * (done + 1))
            nc.vector.tensor_tensor(mean2[:, :], stats[:, :, 1], stats[:, :, 4], ALU.add)
            nc.vector.tensor_tensor(rstd[:, :], stats[:, :, 2], stats[:, :, 5], ALU.add)
            link(nc.vector.tensor_tensor(spread[:, :], stats[:, :, 1], stats[:, :, 4], ALU.subtract))
            link(nc.vector.scalar_tensor_tensor(out=spread[:, :], in0=spread[:, :], scalar=0.25, in1=spread[:, :],
                                                op0=ALU.mult, op1=ALU.mult))
            link(nc.vector.scalar_tensor_tensor(out=rstd[:, :], in0=rstd[:, :], scalar=1.0 / D, in1=spread[:, :],
                                                op0=ALU.mult, op1=ALU.add))
            nc.vector.tensor_scalar(rstd[:, :], rstd[:, :], EPS, None, ALU.add).then_inc(s_var, 1)
            dve.wait_ge(s_sd, done + 1)
            link(nc.vector.reciprocal(rstd[:, :], rstd[:, :]))
            link(nc.vector.scalar_tensor_tensor(out=shift[:, :], in0=mean2[:, :], scalar=-0.5, in1=rstd[:, :],
                                                op0=ALU.mult, op1=ALU.mult))

        with nc.Block() as block:
            @block.gpsimd
            def _(pool):
                pool.sem_inc(s_acc, 2)
                with pool.Fori(0, NB // 2) as b_2:
                    b = b_2 * 2
                    for u in range(2):
                        pool.wait_ge(s_xn, b + (u + 1))
                        a = acc[:, bass.ds(b + u, 1), :].rearrange("p b d -> p (b d)")
                        nc.gpsimd.tensor_tensor(a, a, xn[:, u, :], ALU.add).then_inc(s_acc, 1)

            @block.vector
            def _(dve):
                link = chain(dve, "dve_keys")
                shift_and = nc.vector.tensor_scalar
                dve.sem_inc(s_ranked, 2)
                dve.sem_inc(s_xij, 2)
                dve.wait_ge(s_e, 64)
                link(shift_and(tmp_i, src_i, 7, None, ALU.arith_shift_right))
                link(nc.vector.tensor_copy(block16, tmp_i))
                link(shift_and(tmp_i, dst_i, 3, None, ALU.arith_shift_right))
                link(nc.vector.tensor_scalar(v1_16, tmp_i, 1.0, None, ALU.add))
                link(shift_and(src_i, src_i, P - 1, None, ALU.bitwise_and))
                link(shift_and(dst_i, dst_i, 7, 7, ALU.bitwise_and, ALU.arith_shift_left))
                link(nc.vector.tensor_tensor(v2_16, src_i, dst_i, ALU.add))

                def make_mask(b, slot):
                    nc.vector.tensor_scalar(mask[slot], block16, b, None, ALU.is_equal).then_inc(s_mask, 1)

                with dve.Fori(0, NB // 2) as b_2:
                    b = b_2 * 2
                    for u in range(2):
                        dve.wait_ge(s_counted, b + (u + 1))
                        make_mask(row_f[:, bass.ds(b + u, 1)], u)
                dve.wait_ge(s_cnt, 1)
                nc.vector.tensor_copy(count_f[:, WA:COLS], banks[1][:, 0:WB])
                link(nc.vector.tensor_copy(count_f[:, 0:WA], banks[0][:, 0:WA]))
                for n, (c0, w, t) in enumerate(PARTS):
                    link(nc.vector.tensor_tensor_scan(out=scan_f[:, c0:c0 + w], data0=ones_row[:, 0:w],
                                                      data1=count_f[:, c0:c0 + w], initial=0.0,
                                                      op0=ALU.mult, op1=ALU.add))
                    link(nc.vector.tensor_scalar(small_i[:, n:n + 1], scan_f[:, c0 + w - 1:c0 + w], float(P - 1), None, ALU.add))
                    link(shift_and(small_i[:, n:n + 1], small_i[:, n:n + 1], 7, None, ALU.arith_shift_right))
                    link(nc.vector.tensor_copy(small[:, n:n + 1], small_i[:, n:n + 1]))
                nc.vector.memset(small[:, 15:16], 0.0).then_inc(s_tiles, 1)
                link(nc.vector.tensor_tensor(scan_f, scan_f, count_f, ALU.subtract))
                dve.wait_ge(s_base, 1)
                link(nc.vector.tensor_copy(small[:, 2:4], banks[6][:, 0:2]))
                link(nc.vector.tensor_tensor(small[:, 4:6], small[:, 2:4], small[:, 0:2], ALU.add))
                link(nc.vector.tensor_scalar(small[:, 6:8], small[:, 2:4], float(P), None, ALU.mult))
                for n, (c0, w, t) in enumerate(PARTS):
                    link(nc.vector.tensor_scalar(carry_i[:, c0:c0 + w], scan_f[:, c0:c0 + w], small[:, 6 + n:7 + n],
                                                 None, ALU.add))
                for d in range(3):
                    link(shift_and(digit_i, carry_i, 127 << (7 * d), None, ALU.bitwise_and))
                    link(nc.vector.tensor_copy(carry[d], digit_i))
                nc.vector.memset(small[:, 14:15], 0.0).then_inc(s_carry, 1)
                for n, (c0, w, t) in enumerate(PARTS):
                    nc.vector.tensor_scalar(after[:, 0:t], row_f[:, 0:t], small[:, 4 + n:5 + n], None,
                                            ALU.is_ge).then_inc(s_cmp, 1)
                    dve.wait_ge(s_blk, n + 1)
                    for k, (a, z) in enumerate(CUTS[n]):
                        link(nc.vector.tensor_copy(part[n]["block"][:, a:z], banks[6 + k][:, 0:z - a]))

                def take(k, slot):
                    dve.wait_ge(s_rank, k)
                    dve.wait_ge(s_mask, k + NB)
                    dve.sem_inc(s_dve, 1)
                    for c, (a, z) in enumerate(RANK_CUTS):
                        last = nc.vector.copy_predicated(pos_f[:, a:z], mask[slot][:, a:z].bitcast(U16),
                                                         banks[2 + 2 * slot + c][:, 0:z - a])
                    last.then_inc(s_ranked, 1)
                    dve.wait_ge(s_ranked, k + 2)

                make_mask(row_f[:, 0:1], 0)
                with dve.Fori(0, (NB - 2) // 2) as b_2:
                    b = b_2 * 2
                    make_mask(row_f[:, bass.ds(b + 1, 1)], 1)
                    take(b + 1, 0)
                    make_mask(row_f[:, bass.ds(b + 2, 1)], 0)
                    take(b + 2, 1)
                make_mask(row_f[:, NB - 1:NB], 1)
                take(NB - 1, 0)
                take(NB, 1)
                link(nc.vector.tensor_copy(tmp_i, pos_f))
                link(shift_and(src_i, tmp_i, P - 1, None, ALU.bitwise_and))
                link(shift_and(dst_i, tmp_i, 7, None, ALU.arith_shift_right))
                link(nc.vector.tensor_copy(posl_16, src_i))
                link(nc.vector.tensor_copy(post_f, dst_i))

                for n in range(5):
                    dve.wait_ge(s_x[n], 16)
                dve.wait_ge(s_w, 176)
                moments(dve, link, 0)
                nc.vector.memset(small[:, 13:14], 0.0).then_inc(s_zero, 1)

                def normalize(b, u):
                    dve.wait_ge(s_acc, b + (u + 1))
                    dve.wait_ge(s_xnT, b + (u + 1))
                    nc.vector.tensor_scalar(xn[:, u, :], flat(acc[:, bass.ds(b + u, 1), :]), rstd[:, bass.ds(b + u, 1)],
                                            shift[:, bass.ds(b + u, 1)], ALU.mult, ALU.add).then_inc(s_xn, 1)

                def rows(b, u):
                    dve.wait_ge(s_lin, b + (u + 1))
                    dve.wait_ge(s_dot, b + (u + 1))
                    o = banks[u][:, :].rearrange("p (s d) -> p s d", s=2)
                    nc.vector.tensor_scalar(junk, o, SLOPE, None, ALU.mult).then_inc(s_diag, 1)
                    dve.wait_ge(s_diag, 4 * b + (4 * u + 1))
                    nc.vector.tensor_tensor(xij[:, u, :, 0:D], o, junk, ALU.max).then_inc(s_diag, 1)
                    dve.wait_ge(s_diag, 4 * b + (4 * u + 2))
                    for side in range(2):
                        nc.vector.tensor_tensor_reduce(out=junk[:, side, :], in0=xij[:, u, side, 0:D], in1=wa[:, side, :],
                                                       scale=1.0, scalar=ba[:, side:side + 1], op0=ALU.mult, op1=ALU.add,
                                                       accum_out=xij[:, u, side, D:ROW]).then_inc(s_diag, 1)
                    dve.wait_ge(s_diag, 4 * b + (4 * u + 4))
                    nc.vector.tensor_copy(a1col[:, bass.ds(b + u, 1)], xij[:, u, 1, D:ROW]).then_inc(s_xij, 1)

                with dve.Fori(0, NB // 2) as b_2:
                    b = b_2 * 2
                    for u in range(2):
                        normalize(b, u)
                    for u in range(2):
                        rows(b, u)
                dve.wait_ge(s_xij, NB + 2)
                with dve.Fori(0, NB // 2) as b_2:
                    b = b_2 * 2
                    for u in range(2):
                        dve.wait_ge(s_a1b, b + (u + 1))
                        nc.vector.tensor_scalar(a1diag[:, u, :], ident[:, :], a1col[:, bass.ds(b + u, 1)], None,
                                                ALU.mult).then_inc(s_a1c, 1)

            @block.scalar
            def _(act):
                act.sem_inc(s_xt, 2)
                act.sem_inc(s_a1r, 2)
                act.wait_ge(s_var, 1)
                nc.scalar.activation(rstd[:, :], rstd[:, :], ACT.Sqrt).then_inc(s_sd, 1)
                with act.Fori(0, NB // 2) as b_2:
                    b = b_2 * 2
                    for u in range(2):
                        act.wait_ge(s_xnT, b + (u + 3))
                        nc.scalar.copy(xt[:, u, :, :], banks[2 + u][:, 0:KD * P].rearrange("p (k m) -> p k m", k=KD)).then_inc(s_xt, 1)
                with act.Fori(0, NB // 2) as b_2:
                    b = b_2 * 2
                    for u in range(2):
                        act.wait_ge(s_a1b, b + (u + 3))
                        nc.scalar.copy(flat(a1row[:, bass.ds(b + u, 1), :]), banks[4 + u][:, 0:P]).then_inc(s_a1r, 1)

            @block.tensor
            def _(pe):
                pe.sem_inc(s_counted, 2)
                pe.sem_inc(s_xnT, 2)
                pe.sem_inc(s_a1b, 2)
                for c, (a, z) in enumerate(RANK_CUTS):
                    nc.tensor.matmul(banks[c][:, 0:z - a], unit[:, 0:P], iota_16[:, 0:z - a], start=True, stop=False)
                with pe.Fori(0, NB // 2) as b_2:
                    b = b_2 * 2
                    for u in range(2):
                        pe.wait_ge(s_mask, b + (u + 1))
                        pe.sem_inc(s_pe, 1)
                        for c, (a, z) in enumerate(RANK_CUTS):
                            mm = nc.tensor.matmul(banks[c][:, 0:z - a], unit[:, bass.ds(P - u - b, P)], mask[u][:, a:z],
                                                  start=False, stop=False)
                        mm.then_inc(s_counted, 1)
                for c, (a, z) in enumerate(RANK_CUTS):
                    mm = nc.tensor.matmul(banks[c][:, 0:z - a], unit[:, 0:P], iota_16[:, 0:z - a], start=False, stop=True)
                mm.then_inc(s_cnt, 1)
                pe.wait_ge(s_tiles, 1)
                nc.tensor.matmul(banks[6][:, 0:2], below[:, :], small[:, 0:2], start=True, stop=True).then_inc(s_base, 1)
                pe.wait_ge(s_carry, 1)
                for n, (c0, w, t) in enumerate(PARTS):
                    pe.wait_ge(s_cmp, n + 1)
                    for k, (a, z) in enumerate(CUTS[n]):
                        mm = nc.tensor.matmul(banks[6 + k][:, 0:z - a], first_rows, after[:, a:z], start=True, stop=True)
                    mm.then_inc(s_blk, 1)
                with pe.Fori(0, NB // 2) as b_2:
                    b = b_2 * 2
                    for u in range(2):
                        pe.wait_ge(s_mask, b + (NB + u + 1))
                        pe.wait_ge(s_ranked, b + (u + 1))
                        for c, (a, z) in enumerate(RANK_CUTS):
                            o = banks[2 + 2 * u + c][:, 0:z - a]
                            nc.tensor.matmul(o, below16, mask[u][:, a:z], start=True, stop=False)
                            for d in range(3):
                                mm = nc.tensor.matmul(o, flat(sel[:, bass.ds(b + u, 1), :]), carry[d][:, a:z],
                                                      start=False, stop=(d == 2))
                        mm.then_inc(s_rank, 1)
                pe.wait_ge(s_ranked, NB + 2)
                with pe.Fori(0, NB // 2) as b_2:
                    b = b_2 * 2
                    for u in range(2):
                        pe.wait_ge(s_xn, b + (u + 1))
                        pe.wait_ge(s_xt, b + (u + 1))
                        for k in range(KD):
                            mm = nc.tensor.transpose(banks[2 + u][:, k * P:(k + 1) * P], xn[:, u, k * P:(k + 1) * P], ident[:, :])
                        mm.then_inc(s_xnT, 1)
                    for u in range(2):
                        pe.wait_ge(s_xt, b + (u + 3))
                        pe.wait_ge(s_xij, b + (u + 1))
                        for k in range(KD):
                            nc.tensor.matmul(banks[u][:, :], xt[:, u, k, :], wcat[:, k, :], start=(k == 0), stop=False)
                        nc.tensor.matmul(banks[u][:, :], ones[0:1, :], bcat[0:1, :], start=False, stop=True).then_inc(s_lin, 1)
                pe.wait_ge(s_blk, len(PARTS))
                with pe.Fori(0, NB // 2) as b_2:
                    b = b_2 * 2
                    for u in range(2):
                        pe.wait_ge(s_a1c, b + (u + 1))
                        pe.wait_ge(s_a1r, b + (u + 1))
                        nc.tensor.matmul(banks[4 + u][:, 0:P], ones[:, :], a1diag[:, u, :], start=True, stop=True).then_inc(s_a1b, 1)

            @block.sync
            def _(sp):
                per = FT * FFN_ROWS // P * D // (4 * D)
                sp.dma_start(xs.rearrange("(p a r) d -> p a (r d)", p=P, a=per),
                             zeros.unsqueeze(1).to_broadcast([P, per, 4 * D])).then_inc(s_xs0, 16)
                sp.sem_inc(s_dot, 2)
                with sp.Fori(0, NB // 2) as b_2:
                    b = b_2 * 2
                    for u in range(2):
                        sp.wait_ge(s_xij, b + (u + 3))
                        sp.dma_start(table[bass.ds((b + u) * P, P), :], xij[:, u, 0, :]).then_inc(s_tab[u], 16)
                    for u in range(2):
                        sp.wait_ge(s_tab[u], 8 * b + 16)
                        sp.sem_inc(s_dot, 1)
                sp.wait_ge(s_xs0, 16)

        s_hot = sem("one_hots_ready")
        s_lone = sem("plain_one_hot_ready")
        s_moved = sem("one_hots_used")
        s_sorted = sem("sorted")
        s_opened = sem("sort_banks_opened")
        SORT_BANKS = ((0, 1), (2, 4))

        def one_hots(dve, n, g, slot):
            c0, w, t = PARTS[n]
            done = PARTS[0][1] // GROUP if n else 0
            at = g + (done + 1)
            cols = g * GROUP + (c0)
            dve.wait_ge(s_moved, at)

            def rep(a):
                return a[:, bass.ds(cols, GROUP)].unsqueeze(1).to_broadcast([P, P, GROUP])
            nc.vector.tensor_tensor(hot[slot], iota_m, rep(posl_16), ALU.is_equal).then_inc(s_lone, 1)
            for c in range(GROUP):
                nc.vector.tensor_scalar(tile_hot[slot][:, c, 0:t], iota_16[:, 0:t], post_f[:, bass.ds(cols + c, 1)], None,
                                        ALU.is_equal)
            dve.wait_ge(s_lone, at)
            nc.vector.tensor_tensor(hot1[slot], hot[slot], rep(v1_16), ALU.mult)
            nc.vector.tensor_tensor(hot2[slot], hot[slot], rep(v2_16), ALU.mult).then_inc(s_hot, 1)

        def move(pe, n, g, slot):
            done = PARTS[0][1] // GROUP if n else 0
            pe.wait_ge(s_hot, g + (done + 1))
            for c in range(GROUP):
                for v, h in enumerate((hot1, hot2)):
                    for k, (a, z) in enumerate(CUTS[n]):
                        mm = nc.tensor.matmul(banks[SORT_BANKS[n][v] + k][:, 0:z - a], h[slot][:, :, c],
                                              tile_hot[slot][:, c, a:z], start=False, stop=False)
            mm.then_inc(s_moved, 1)

        def open_or_close(n, first):
            for v in range(2):
                for k, (a, z) in enumerate(CUTS[n]):
                    mm = nc.tensor.matmul(banks[SORT_BANKS[n][v] + k][:, 0:z - a], unit[:, 0:P], iota_16[:, 0:z - a],
                                          start=first, stop=not first)
            mm.then_inc(s_opened if first else s_sorted, 1)

        def decode(dve, link, n):
            dve.wait_ge(s_sorted, n + 1)
            t = PARTS[n][2]
            for k, (a, z) in enumerate(CUTS[n]):
                link(nc.vector.tensor_copy(out_v1[:, a:z], banks[SORT_BANKS[n][0] + k][:, 0:z - a]))
                link(nc.vector.tensor_copy(out_v2[:, a:z], banks[SORT_BANKS[n][1] + k][:, 0:z - a]))
            link(nc.vector.tensor_scalar(out_hi[:, 0:t], out_v2[:, 0:t], 7, None, ALU.arith_shift_right))
            link(nc.vector.tensor_scalar(out_v2[:, 0:t], out_v2[:, 0:t], P - 1, None, ALU.bitwise_and))
            link(nc.vector.scalar_tensor_tensor(out=part[n]["receiver"][:, :], in0=out_v1[:, 0:t], scalar=1.0,
                                                in1=out_v2[:, 0:t], op0=ALU.min, op1=ALU.add))
            link(nc.vector.tensor_scalar(out_v1[:, 0:t], out_v1[:, 0:t], -1.0, 0.0, ALU.add, ALU.max))
            link(nc.vector.scalar_tensor_tensor(out=part[n]["sender"][:, :], in0=out_v1[:, 0:t], scalar=8.0,
                                                in1=out_hi[:, 0:t], op0=ALU.mult, op1=ALU.add))

        with nc.Block() as block:
            @block.vector
            def _(dve):
                link = chain(dve, "dve_decode0")
                with dve.Fori(0, (WA // GROUP) // 2) as g_2:
                    g = g_2 * 2
                    for u in range(2):
                        one_hots(dve, 0, g + u, u)
                decode(dve, link, 0)

            @block.tensor
            def _(pe):
                pe.sem_inc(s_moved, 2)
                open_or_close(0, True)
                with pe.Fori(0, (WA // GROUP) // 2) as g_2:
                    g = g_2 * 2
                    for u in range(2):
                        move(pe, 0, g + u, u)
                open_or_close(0, False)

        s_place = sem("places_staged")
        s_row = [sem(f"rows_gathered{h}") for h in range(2)]
        s_gate = sem("gates_ready")
        s_lhs = sem("gated_one_hots_ready")
        s_sum = sem("tile_sums_ready")
        s_add = sem("tile_sums_added")

        sums = [banks[n] for n in (0, 1, 6, 7)]

        def gather(pool, n, i, done):
            for h in range(2):
                at = i * 2 + (h + done // HALF)
                t0 = i * BODY + h * HALF
                pool.wait_ge(s_sum, t0 + (done + HALF))
                pool.sem_inc(s_dummy, 1)
                nc.gpsimd.tensor_copy(places[:, h, :], part[n]["sender"][:, bass.ds(t0, HALF)]).then_inc(s_place, 1)
                pool.wait_ge(s_place, at + 1)
                pool.sem_inc(s_dummy, 1)
                for u in range(HALF):
                    pool.indirect_dma_start(out=ring[:, h * HALF + u, :], out_offset=None, in_=table[:, :],
                                            in_offset=bass.IndirectOffsetOnAxis(ap=places[:, h, u:u + 1], axis=0)
                                            ).then_inc(s_row[h], 16)

        def gates(act, n, i, done):
            for h in range(2):
                t0 = i * BODY + h * HALF
                blocks = [act.value_load(part[n]["block"][0:1, bass.ds(t0 + u, 1)], min_val=0, max_val=NB - 1)
                          for u in range(HALF)]
                act.wait_ge(s_row[h], i * (16 * HALF) + (16 * HALF * (done // BODY + 1)))
                for u in range(HALF):
                    act.wait_ge(s_lhs, t0 + (done + u + 1))
                    nc.scalar.activation(gate[:, u % 4, :], flat(a1row[:, bass.ds(blocks[u], 1), :]), ACT.Sigmoid,
                                         bias=ring[:, h * HALF + u, D:ROW]).then_inc(s_gate, 1)

        def lhs_and_add(dve, n, i, done, between):
            for h in range(2):
                t0 = i * BODY + h * HALF
                blocks = [dve.value_load(part[n]["block"][0:1, bass.ds(t0 + u, 1)], min_val=0, max_val=NB - 1)
                          for u in range(HALF)]

                def make(u):
                    dve.wait_ge(s_gate, t0 + (done + u + 1))
                    dve.wait_ge(s_sum, t0 + (done + u + 13))
                    nc.vector.scalar_tensor_tensor(out=lhs[:, u % 4, :], in0=iota_1[:, :],
                                                   scalar=part[n]["receiver"][:, bass.ds(t0 + u, 1)], in1=gate[:, u % 4, :],
                                                   op0=ALU.is_equal, op1=ALU.mult).then_inc(s_lhs, 1)

                def add(u):
                    dve.wait_ge(s_sum, t0 + (done + u + 17))
                    dve.wait_ge(s_add, t0 + (done + u + 4))
                    a = flat(acc[:, bass.ds(blocks[u], 1), :])
                    nc.vector.tensor_tensor(a, a, sums[u % 4][:, 0:D], ALU.add).then_inc(s_add, 1)
                make(0)
                make(1)
                for u in range(HALF):
                    if u + 2 < HALF:
                        make(u + 2)
                    add(u)
                    between(h * HALF + u)

        def tile_sums(pe, n, i, done, between):
            for h in range(2):
                t0 = i * BODY + h * HALF
                for u in range(HALF):
                    pe.wait_ge(s_lhs, t0 + (done + u + 5))
                    pe.wait_ge(s_add, t0 + (done + u + 1))
                    nc.tensor.matmul(sums[u % 4][:, 0:D], lhs[:, u % 4, :],
                                     ring[:, h * HALF + u, 0:D], start=True, stop=True).then_inc(s_sum, 1)
                    between(h * HALF + u)

        SORT_AT = {2: 0, 7: 1, 12: 2}
        GROUPS_B = WB // GROUP

        with nc.Block() as block:
            @block.gpsimd
            def _(pool):
                with pool.Fori(0, TA // BODY) as i:
                    gather(pool, 0, i, 0)

            @block.scalar
            def _(act):
                with act.Fori(0, TA // BODY) as i:
                    gates(act, 0, i, 0)

            @block.vector
            def _(dve):
                link = chain(dve, "dve_decode1")
                dve.sem_inc(s_lhs, 4)
                dve.sem_inc(s_add, 4)
                with dve.Fori(0, SORT_BODIES // 2) as i_2:
                    i = i_2 * 2
                    for v in range(2):
                        lhs_and_add(dve, 0, i + v, 0, lambda u: one_hots(
                            dve, 1, (i + v) * SORTS_PER_BODY + SORT_AT[u], (v * SORTS_PER_BODY + SORT_AT[u]) % 2)
                            if u in SORT_AT else None)
                with dve.Fori(SORT_BODIES, TA // BODY) as i:
                    lhs_and_add(dve, 0, i, 0, lambda u: None)
                decode(dve, link, 1)

            @block.tensor
            def _(pe):
                pe.sem_inc(s_sum, 16)
                open_or_close(1, True)
                with pe.Fori(0, SORT_BODIES // 2) as i_2:
                    i = i_2 * 2
                    for v in range(2):
                        tile_sums(pe, 0, i + v, 0, lambda u: move(
                            pe, 1, (i + v) * SORTS_PER_BODY + SORT_AT[u], (v * SORTS_PER_BODY + SORT_AT[u]) % 2)
                            if u in SORT_AT else None)
                open_or_close(1, False)
                with pe.Fori(SORT_BODIES, TA // BODY) as i:
                    tile_sums(pe, 0, i, 0, lambda u: None)

        with nc.Block() as block:
            @block.gpsimd
            def _(pool):
                with pool.Fori(0, TB // BODY) as i:
                    gather(pool, 1, i, TA)

            @block.scalar
            def _(act):
                with act.Fori(0, TB // BODY) as i:
                    gates(act, 1, i, TA)

            @block.vector
            def _(dve):
                with dve.Fori(0, TB // BODY) as i:
                    lhs_and_add(dve, 1, i, TA, lambda u: None)

            @block.tensor
            def _(pe):
                with pe.Fori(0, TB // BODY) as i:
                    tile_sums(pe, 1, i, TA, lambda u: None)


        s_yn = sem("yn_ready")
        s_ynT = sem("yn_transposed")
        s_ynTc = sem("ynT_copied")
        s_logit = sem("logits_ready")
        s_b1 = sem("b1_transposed")
        s_b1c = sem("b1T_ready")
        s_top = sem("top_found")
        s_diff = sem("top_difference_ready")
        s_wk = sem("top_weights_ready")
        s_etot = sem("expert_counts_ready")
        s_eoff = sem("expert_offsets_ready")

        def normalized(slot, b):
            return nc.vector.tensor_scalar(yn[:, slot, :], flat(acc[:, b, :]), rstd[:, b], shift[:, b], ALU.mult, ALU.add)

        with nc.Block() as block:
            @block.vector
            def _(dve):
                link = chain(dve, "dve_route")
                dve.sem_inc(s_logit, 2)
                moments(dve, link, 1)
                with dve.Fori(0, NB // 2) as b_2:
                    b = b_2 * 2
                    for u in range(2):
                        dve.wait_ge(s_ynT, b + (u + 1))
                        normalized(u, bass.ds(b + u, 1)).then_inc(s_yn, 1)
                dve.wait_ge(s_logit, NB + 2)
                link(nc.vector.tensor_tensor(logits[:, :, :], banks[7][:, 0:NB * X].rearrange("p (b e) -> p b e", b=NB),
                                             bg[:, :].unsqueeze(1).to_broadcast([P, NB, X]), ALU.add))
                rest = row_f[:, 0:X].unsqueeze(1).to_broadcast([P, NB, X])
                for k in range(TOP_K):
                    link(nc.vector.tensor_reduce(top[:, k, :], logits[:, :, :], AX_X, ALU.max))
                    link(nc.vector.tensor_tensor(hit[:, :, :], logits[:, :, :],
                                                 top[:, k, :].unsqueeze(2).to_broadcast([P, NB, X]), ALU.is_equal))
                    link(nc.vector.tensor_scalar(lead[:, :, :], rest, -1.0, float(X), ALU.mult, ALU.add))
                    link(nc.vector.tensor_tensor(hit[:, :, :], hit[:, :, :], lead[:, :, :], ALU.mult))
                    link(nc.vector.tensor_reduce(idx[k][:, :], hit[:, :, :], AX_X, ALU.max))
                    link(nc.vector.tensor_scalar(idx[k][:, :], idx[k][:, :], -1.0, float(X), ALU.mult, ALU.add))
                    if k == 0:
                        link(nc.vector.tensor_tensor(hit[:, :, :], rest, idx[k][:, :].unsqueeze(2).to_broadcast([P, NB, X]),
                                                     ALU.is_equal))
                        link(nc.vector.scalar_tensor_tensor(out=logits[:, :, :], in0=hit[:, :, :], scalar=-3e38,
                                                            in1=logits[:, :, :], op0=ALU.mult, op1=ALU.add))
                nc.vector.tensor_tensor(diff[:, :], top[:, 0, :], top[:, 1, :], ALU.subtract).then_inc(s_diff, 1)
                experts_f = row_f[:, 0:X].unsqueeze(2).to_broadcast([P, X, NB])
                for k in range(TOP_K):
                    link(nc.vector.tensor_tensor(eh[k][:, :, :], experts_f, idx[k][:, :].unsqueeze(1).to_broadcast([P, X, NB]),
                                                 ALU.is_equal))
                    link(nc.vector.tensor_tensor(eh[k][:, :, :], eh[k][:, :, :],
                                                 valid[:, :].unsqueeze(1).to_broadcast([P, X, NB]), ALU.mult))
                link(nc.vector.tensor_tensor(ehs[:, :, :], eh[0][:, :, :], eh[1][:, :, :], ALU.add))
                for e in range(X):
                    last = nc.vector.tensor_tensor_scan(out=esc[:, e, :], data0=ones[:, 0:NB], data1=ehs[:, e, :],
                                                        initial=0.0, op0=ALU.mult, op1=ALU.add)
                link(last)
                nc.vector.tensor_copy(etot[:, :], esc[:, :, NB - 1]).then_inc(s_etot, 1)
                dve.wait_ge(s_etot, 1)
                link(nc.vector.tensor_tensor(esc[:, :, :], esc[:, :, :], ehs[:, :, :], ALU.subtract))
                dve.wait_ge(s_eoff, 1)
                link(nc.vector.tensor_scalar(eti[:, :], banks[6][:, X:2 * X], float(FFN_ROWS - 1), None, ALU.add))
                link(nc.vector.tensor_scalar(eti[:, :], eti[:, :], FFN_ROWS.bit_length() - 1, None, ALU.arith_shift_right))
                link(nc.vector.tensor_copy(et[:, 0, :], eti[:, :]))
                link(nc.vector.tensor_tensor_scan(out=et[:, 1, :], data0=ones[:, 0:X], data1=et[:, 0, :], initial=0.0,
                                                  op0=ALU.mult, op1=ALU.add))
                link(nc.vector.tensor_tensor(et[:, 2, :], et[:, 1, :], et[:, 0, :], ALU.subtract))
                link(nc.vector.scalar_tensor_tensor(out=et[:, 3, :], in0=et[:, 2, :], scalar=float(FFN_ROWS),
                                                    in1=banks[6][:, 0:X], op0=ALU.mult, op1=ALU.add))
                link(nc.vector.tensor_tensor(esc[:, :, :], esc[:, :, :], et[:, 3, :].unsqueeze(2).to_broadcast([P, X, NB]),
                                             ALU.add))
                for k in range(TOP_K):
                    link(nc.vector.tensor_tensor(eh[k][:, :, :], eh[k][:, :, :], esc[:, :, :], ALU.mult))
                    link(nc.vector.tensor_reduce(posk_f[:, :], eh[k][:, :, :].rearrange("p e b -> p b e"), AX_X, ALU.add))
                    link(nc.vector.tensor_copy(posk[:, :, k], posk_f[:, :]))
                link(nc.vector.tensor_tensor(ecmp[:, :, 0:X - 1], row_f[:, 0:FT].unsqueeze(2).to_broadcast([P, FT, X - 1]),
                                             et[:, 1, 0:X - 1].unsqueeze(1).to_broadcast([P, FT, X - 1]), ALU.is_ge))
                link(nc.vector.tensor_reduce(esum[:, :], ecmp[:, :, 0:X - 1], AX_X, ALU.add))
                link(nc.vector.tensor_copy(expert[:, :], esum[:, :]))

            @block.scalar
            def _(act):
                act.sem_inc(s_ynTc, 2)
                act.wait_ge(s_b1, 1)
                nc.scalar.copy(b1T[:, :], banks[5][:, 0:X * KH]).then_inc(s_b1c, 1)
                act.wait_ge(s_var, 2)
                nc.scalar.activation(rstd[:, :], rstd[:, :], ACT.Sqrt).then_inc(s_sd, 1)
                with act.Fori(0, NB // 2) as b_2:
                    b = b_2 * 2
                    for u in range(2):
                        act.wait_ge(s_ynT, b + (u + 3))
                        nc.scalar.copy(ynT[:, u * KD:(u + 1) * KD, :],
                                       banks[u][:, 0:KD * P].rearrange("p (k m) -> p k m", k=KD)).then_inc(s_ynTc, 1)
                act.wait_ge(s_diff, 1)
                nc.scalar.activation(wk[0][:, :], diff[:, :], ACT.Sigmoid)
                nc.scalar.activation(wk[1][:, :], diff[:, :], ACT.Sigmoid, scale=-1.0).then_inc(s_wk, 1)

            @block.tensor
            def _(pe):
                pe.sem_inc(s_ynT, 2)
                nc.tensor.transpose(banks[5][:, 0:X * KH], b1raw[:, :], ident[0:X * KH, 0:X * KH]).then_inc(s_b1, 1)
                with pe.Fori(0, NB // 2) as b_2:
                    b = b_2 * 2
                    for u in range(2):
                        pe.wait_ge(s_yn, b + (u + 1))
                        pe.wait_ge(s_ynTc, b + (u + 1))
                        for k in range(KD):
                            mm = nc.tensor.transpose(banks[u][:, k * P:(k + 1) * P], yn[:, u, k * P:(k + 1) * P], ident[:, :])
                        mm.then_inc(s_ynT, 1)
                    for u in range(2):
                        pe.wait_ge(s_ynTc, b + (u + 3))
                        for k in range(KD):
                            mm = nc.tensor.matmul(banks[7][:, bass.ds((b + u) * X, X)], ynT[:, u * KD + k, :], wg[:, k, :],
                                                  start=(k == 0), stop=(k == KD - 1))
                        mm.then_inc(s_logit, 1)
                pe.wait_ge(s_etot, 1)
                nc.tensor.matmul(banks[6][:, 0:X], below[:, :], etot[:, :], start=True, stop=True)
                nc.tensor.matmul(banks[6][:, X:2 * X], ones[:, :], etot[:, :], start=True, stop=True).then_inc(s_eoff, 1)

        s_tok = sem("token_rows_ready")
        s_sent = [sem(f"rows_sent{u}") for u in range(4)]
        s_sfree = sem("token_rows_free")

        with nc.Block() as block:
            @block.vector
            def _(dve):
                def stage(b, u):
                    dve.wait_ge(s_sfree, b + (u + 1))
                    nc.vector.tensor_copy(placesk[:, u, :], flat(posk[:, bass.ds(b + u, 1), :]))
                    normalized(u, bass.ds(b + u, 1)).then_inc(s_tok, 1)
                with dve.Fori(0, (REAL - 1) // 4) as b_4:
                    b = b_4 * 4
                    for u in range(4):
                        stage(b, u)
                dve.wait_ge(s_sfree, REAL)
                nc.vector.tensor_copy(placesk[:, 0, :], posk[:, REAL - 1, :])
                normalized(0, slice(REAL - 1, REAL)).then_inc(s_tok, 1)

            @block.gpsimd
            def _(pool):
                def send(u, rows):
                    for k in range(TOP_K):
                        pool.indirect_dma_start(out=xs[:, :],
                                                out_offset=bass.IndirectOffsetOnAxis(ap=placesk[0:rows, u, k:k + 1], axis=0),
                                                in_=yn[0:rows, u, :], in_offset=None).then_inc(s_sent[u], 16)
                with pool.Fori(0, (REAL - 1) // 4) as b_4:
                    b = b_4 * 4
                    for u in range(4):
                        pool.wait_ge(s_tok, b + (u + 1))
                        pool.sem_inc(s_dummy, 1)
                        send(u, P)
                pool.wait_ge(s_tok, REAL)
                send(0, LAST)

            @block.sync
            def _(sp):
                sp.sem_inc(s_sfree, 4)
                with sp.Fori(0, (REAL - 1) // 4) as b_4:
                    b = b_4 * 4
                    for u in range(4):
                        sp.wait_ge(s_sent[u], 8 * b + 16 * TOP_K)
                        sp.sem_inc(s_sfree, 1)
                sp.wait_ge(s_sent[0], (REAL - 1) // 4 * 16 * TOP_K + 16 * TOP_K)

        s_wl = [sem(f"expert_weights_loaded{u}") for u in range(2)]
        s_xg = [sem(f"expert_rows_loaded{u}") for u in range(2)]
        s_b2 = sem("b2_loaded")
        s_xT = sem("rows_transposed")
        s_xTc = sem("rows_T_ready")
        s_mm1 = sem("hidden_ready")
        s_gelu = sem("gelu_ready")
        HB = 4
        s_mm2 = sem("expert_out_ready")
        s_yo = sem("expert_rows_ready")
        s_st = sem("expert_rows_stored")
        s_yofree = sem("expert_rows_free")

        with nc.Block() as block:
            @block.sync
            def _(sp):
                sp.dma_start(flat(b2all), f_b2.rearrange("e d -> (e d)").partition_broadcast(P)).then_inc(s_b2, 16)
                with sp.Fori(0, FT // 2) as t_2:
                    t = t_2 * 2
                    for u in range(2):
                        e = sp.value_load(expert[0:1, bass.ds(t + u, 1)], min_val=0, max_val=X - 1)
                        sp.wait_ge(s_mm2, t + (u + 1))
                        sp.dma_start(xg[u], xs[bass.ds((t + u) * FFN_ROWS, FFN_ROWS), :].rearrange("(s p) d -> p s d", p=P)
                                     ).then_inc(s_xg[u], 16)
                        sp.dma_start(W1[u], f_w1[bass.ds(e, 1)].rearrange("a (k p) h -> p (a k) h", p=P)).then_inc(s_wl[u], 16)
                        sp.dma_start(W2[u], f_w2[bass.ds(e, 1)].rearrange("a (k p) d -> p (a k) d", p=P)).then_inc(s_wl[u], 16)

            @block.tensor
            def _(pe):
                pe.sem_inc(s_mm2, 2)

                def up(t, u, n):
                    pe.wait_ge(s_xg[u], 8 * t + 16 * (n // 2 + 1))
                    for k in range(KD):
                        for s in range(2):
                            mm = nc.tensor.transpose(banks[0][:, k * FFN_ROWS + s * P:k * FFN_ROWS + (s + 1) * P],
                                                     xg[u][:, s, k * P:(k + 1) * P], ident[:, :])
                    mm.then_inc(s_xT, 1)
                    pe.wait_ge(s_wl[u], 16 * t + 32 * (n // 2 + 1))
                    pe.wait_ge(s_xTc, t + (n + 1))
                    for h in range(KH):
                        pe.wait_ge(s_gelu, KH * t + (KH * n + h + 1))
                        for k in range(KD):
                            mm = nc.tensor.matmul(banks[1 + h % HB][:, 0:FFN_ROWS],
                                                  W1[u][:, k, h * P:(h + 1) * P], xgT[u][:, k, :],
                                                  start=(k == 0), stop=(k == KD - 1))
                        mm.then_inc(s_mm1, 1)

                def down(t, u, n):
                    pe.wait_ge(s_yo, t + (n + 1))
                    pe.wait_ge(s_gelu, KH * t + (KH * (n + 1) + HB))
                    for s in range(2):
                        for h in range(KH):
                            mm = nc.tensor.matmul(banks[5 + u][:, s * D:(s + 1) * D], hT[u][:, h, s * P:(s + 1) * P],
                                                  W2[u][:, h, :], start=(h == 0), stop=(h == KH - 1))
                    mm.then_inc(s_mm2, 1)

                up(0, 0, 0)
                with pe.Fori(0, (FT - 2) // 2) as t_2:
                    t = t_2 * 2
                    up(t, 1, 1)
                    down(t, 0, 0)
                    up(t, 0, 2)
                    down(t, 1, 1)
                up(FT - 2, 1, 1)
                down(FT - 2, 0, 0)
                down(FT - 2, 1, 1)

            @block.scalar
            def _(act):
                act.sem_inc(s_gelu, HB)
                with act.Fori(0, FT // 2) as t_2:
                    t = t_2 * 2
                    for u in range(2):
                        e = act.value_load(expert[0:1, bass.ds(t + u, 1)], min_val=0, max_val=X - 1)
                        act.wait_ge(s_mm2, t + (u + 1))
                        for h in range(KH):
                            act.wait_ge(s_mm1, KH * t + (KH * u + h + 1))
                            nc.scalar.activation(hT[u][:, h, :], banks[1 + h % HB][:, 0:FFN_ROWS],
                                                 ACT.Gelu, bias=b1T[:, bass.ds(e * KH + h, 1)]).then_inc(s_gelu, 1)

            @block.vector
            def _(dve):
                dve.sem_inc(s_yo, 2)
                dve.wait_ge(s_b2, 16)

                def turn(t, u, n):
                    dve.wait_ge(s_xT, t + (n + 1))
                    nc.vector.tensor_copy(flat(xgT[u]), banks[0][:, :]).then_inc(s_xTc, 1)

                def finish(t, u, n):
                    e = dve.value_load(expert[0:1, bass.ds(t + n, 1) if not isinstance(t, int) else slice(t + n, t + n + 1)],
                                       min_val=0, max_val=X - 1)
                    dve.wait_ge(s_mm2, t + (n + 3))
                    dve.wait_ge(s_yofree, t + (n + 1))
                    nc.vector.tensor_tensor(yo[u], banks[5 + u][:, :].rearrange("p (s d) -> p s d", s=2),
                                            b2all[:, bass.ds(e, 1), :].to_broadcast([P, 2, D]), ALU.add).then_inc(s_yo, 1)
                turn(0, 0, 0)
                with dve.Fori(0, (FT - 2) // 2) as t_2:
                    t = t_2 * 2
                    turn(t, 1, 1)
                    finish(t, 0, 0)
                    turn(t, 0, 2)
                    finish(t, 1, 1)
                turn(FT - 2, 1, 1)
                finish(FT - 2, 0, 0)
                finish(FT - 2, 1, 1)

            @block.gpsimd
            def _(pool):
                pool.sem_inc(s_yofree, 2)
                with pool.Fori(0, FT // 2) as t_2:
                    t = t_2 * 2
                    for u in range(2):
                        pool.wait_ge(s_yo, t + (u + 3))
                        pool.sem_inc(s_dummy, 1)
                        pool.dma_start(os[bass.ds((t + u) * FFN_ROWS, FFN_ROWS), :].rearrange("(s p) d -> p s d", p=P),
                                       yo[u]).then_inc(s_st, 16)
                        pool.wait_ge(s_st, 16 * t + (16 * u + 16))
                        pool.sem_inc(s_yofree, 1)

        s_stage = sem("places_back_staged")
        s_back = [sem(f"rows_back{u}") for u in range(4)]
        s_mix = sem("token_mixed")
        s_res = sem("results_ready")
        s_out = [sem(f"out_stored{u}") for u in range(4)]
        s_ofree = sem("result_buffers_free")

        with nc.Block() as block:
            @block.gpsimd
            def _(pool):
                def fetch(u, rows):
                    for k in range(TOP_K):
                        pool.indirect_dma_start(out=back[0:rows, u, k, :], out_offset=None, in_=os[:, :],
                                                in_offset=bass.IndirectOffsetOnAxis(ap=placesk[0:rows, u, k:k + 1], axis=0)
                                                ).then_inc(s_back[u], 16)
                with pool.Fori(0, (REAL - 1) // 4) as b_4:
                    b = b_4 * 4
                    for u in range(4):
                        pool.wait_ge(s_stage, b + (u + 1))
                        pool.sem_inc(s_dummy, 1)
                        fetch(u, P)
                pool.wait_ge(s_stage, REAL)
                fetch(0, LAST)

            @block.vector
            def _(dve):
                def stage(b, u):
                    dve.wait_ge(s_ofree, b + (u + 1))
                    nc.vector.tensor_copy(placesk[:, u, :], flat(posk[:, bass.ds(b + u, 1), :])).then_inc(s_stage, 1)

                def mix(u, rows, b, at, n):
                    dve.wait_ge(s_back[u], n)
                    a = flat(acc[0:rows, b, :])
                    nc.vector.scalar_tensor_tensor(out=back[0:rows, u, 0, :], in0=back[0:rows, u, 0, :], scalar=wk[0][0:rows, b],
                                                   in1=a, op0=ALU.mult, op1=ALU.add).then_inc(s_mix, 1)
                    dve.wait_ge(s_mix, at)
                    nc.vector.scalar_tensor_tensor(out=back[0:rows, u, 1, :], in0=back[0:rows, u, 1, :], scalar=wk[1][0:rows, b],
                                                   in1=back[0:rows, u, 0, :], op0=ALU.mult, op1=ALU.add).then_inc(s_res, 1)
                with dve.Fori(0, (REAL - 1) // 4) as b_4:
                    b = b_4 * 4
                    for u in range(4):
                        stage(b, u)
                    for u in range(4):
                        mix(u, P, bass.ds(b + u, 1), b + (u + 1), 8 * b + 16 * TOP_K)
                dve.wait_ge(s_ofree, REAL)
                nc.vector.tensor_copy(placesk[:, 0, :], posk[:, REAL - 1, :]).then_inc(s_stage, 1)
                mix(0, LAST, slice(REAL - 1, REAL), REAL, (REAL - 1) // 4 * 16 * TOP_K + 16 * TOP_K)

            @block.sync
            def _(sp):
                sp.sem_inc(s_ofree, 4)
                with sp.Fori(0, (REAL - 1) // 4) as b_4:
                    b = b_4 * 4
                    for u in range(4):
                        sp.wait_ge(s_res, b + (u + 1))
                        sp.dma_start(out[bass.ds((b + u) * P, P), :], back[:, u, 1, :]).then_inc(s_out[u], 16)
                    for u in range(4):
                        sp.wait_ge(s_out[u], 4 * b + 16)
                        sp.sem_inc(s_ofree, 1)
                sp.wait_ge(s_res, REAL)
                sp.dma_start(out[(REAL - 1) * P:N, :], back[0:LAST, 0, 1, :]).then_inc(s_out[0], 16)
                sp.wait_ge(s_out[0], 16 * ((REAL - 1) // 4 + 1))


_INS = ["x", "src", "dst", "L0_gnn_W1", "L0_gnn_b1", "L0_gnn_W2", "L0_gnn_b2", "L0_gnn_wa1", "L0_gnn_ba1",
        "L0_gnn_wa2", "L0_gnn_ba2", "L0_ffn_Wg", "L0_ffn_bg", "L0_ffn_W1", "L0_ffn_b1", "L0_ffn_W2", "L0_ffn_b2"]


def kernel(**inputs):
    import numpy as _np
    import concourse.bacc as _bacc
    from concourse import mybir as _mybir
    from concourse.bass_utils import run_bass_kernel_spmd as _run

    nc = _bacc.Bacc("TRN2", target_bir_lowering=False, num_devices=1)
    arrays, args = {}, []
    for name in _INS:
        a = _np.ascontiguousarray(inputs[name])
        arrays[f"in_{name}_dram"] = a
        args.append(nc.dram_tensor(f"in_{name}_dram", a.shape, _mybir.dt.from_np(a.dtype), kind="ExternalInput").ap())
    shape = inputs["x"].shape
    out = nc.dram_tensor("out_dram", shape, _mybir.dt.float32, kind="ExternalOutput").ap()
    gnn_moe_kernel(nc, *args, out)
    r = _run(nc, [arrays], core_ids=[0])
    return r.results[0]["out_dram"]
```

```python
from contextlib import ExitStack

import concourse.bass as bass
from concourse import mybir

ALU = mybir.AluOpType
ACT = mybir.ActivationFunctionType
AX_X = mybir.AxisListType.X
F32 = mybir.dt.float32
F16 = mybir.dt.float16
BF16 = mybir.dt.bfloat16
I32 = mybir.dt.int32
U16 = mybir.dt.uint16
U32 = mybir.dt.uint32

P = 128
EPS = 1e-5
SLOPE = 0.2
TOP_K = 2
FFN_ROWS = 256
SLOTS = 3
RUN = 2 * SLOTS
GROUP = 8
BODY = 16
QUARTER = 4
QUARTERS = BODY // QUARTER
SLOTS_G = 8
LEAD = 4
SORTS_PER_BODY = 3


def ceil_div(a, b):
    return -(-a // b)


def gnn_moe_kernel(nc, x, src, dst, g_w1, g_b1, g_w2, g_b2, wa1, ba1, wa2, ba2,
                   w_gate, b_gate, f_w1, f_b1, f_w2, f_b2, out):
    N, D = x.shape
    (E,) = src.shape
    X, _, H = f_w1.shape
    KD, KH = D // P, H // P
    REAL = ceil_div(N, P)
    LAST = N - (REAL - 1) * P
    NB = ceil_div(REAL, 2) * 2
    EC = ceil_div(E, P)
    FULL = E // P
    TAIL = E - FULL * P
    COLS = ceil_div(EC, GROUP) * GROUP

    def tiles_for(cols):
        return (cols * P + REAL * (P - 1)) // P

    WA = 304
    WB = COLS - WA
    WB_REAL = EC - WA
    TA = ceil_div(tiles_for(WA), BODY) * BODY
    TB = ceil_div(tiles_for(WB_REAL), BODY) * BODY
    TMAX = max(TA, TB)
    SORT_BODIES = WB // GROUP // SORTS_PER_BODY
    assert WB % (GROUP * SORTS_PER_BODY) == 0 and SORT_BODIES <= TA // BODY
    assert TB % 2 == 0 and TB // 2 <= 512 and TA <= 512 and max(WA, WB) <= 512
    PARTS = ((0, WA, TA), (WA, WB, TB))
    CUTS = (((0, TA),), ((0, TB // 2), (TB // 2, TB)))
    FT = (TOP_K * N + X * (FFN_ROWS - 1)) // FFN_ROWS
    DEAD = 1 << 14
    ROW = D + 1

    table = nc.dram_tensor("table", (NB * P, ROW), F32).ap()
    xs = nc.dram_tensor("xs", (FT * FFN_ROWS, D), F32).ap()
    os = nc.dram_tensor("os", (FT * FFN_ROWS, D), F32).ap()

    with ExitStack() as ctx:
        def sb(name, shape, dt=F32):
            return ctx.enter_context(nc.sbuf_tensor(name, shape, dt))

        def sem(name):
            return ctx.enter_context(nc.semaphore(name))

        banks = [ctx.enter_context(nc.psum_tensor(f"bank{i}", [P, 512], F32)) for i in range(8)]

        acc = sb("acc", [P, NB, D])
        ident = sb("ident", [P, P])
        ones = sb("ones", [P, P])
        iota_1 = sb("iota_1", [P, P])
        iota_16 = sb("iota_16", [P, TMAX], F16)
        below = sb("below", [P, P])
        mean2 = sb("mean2", [P, NB])
        spread = sb("spread", [P, NB])
        rstd = sb("rstd", [P, NB])
        shift = sb("shift", [P, NB])
        row_f = sb("row_f", [P, TMAX])
        part = [dict(
            sender=sb(f"sender{n}", [P, t + BODY], I32), receiver=sb(f"receiver{n}", [P, t]),
            block=sb(f"block{n}", [P, t], I32)) for n, (_, _, t) in enumerate(PARTS)]
        a1row = sb("a1row", [P, NB, P])
        ring = sb("ring", [P, BODY, ROW])
        gate = sb("gate", [P, SLOTS_G, P])
        lhs = sb("lhs", [P, SLOTS_G, P])
        places = sb("places", [P, QUARTERS, QUARTER], I32)


        ARENA = 18448
        arena = sb("arena", [P, ARENA])
        used = [0]

        def cut(shape, dt=F32, region=None):
            n = 1
            for m in shape:
                n *= m
            words = ceil_div(n * (2 if dt in (F16, BF16) else 4), 32) * 8
            if region is None:
                region, at = arena, used
            else:
                region, at = region
            a = region[:, at[0]:at[0] + words]
            at[0] += words
            a = (a if dt == F32 else a.bitcast(dt))[:, 0:n]
            if len(shape) == 2:
                a = a.rearrange("p (a b) -> p a b", a=shape[0])
            if len(shape) == 3:
                a = a.rearrange("p (a b c) -> p a b c", a=shape[0], b=shape[1])
            return a

        tmp_i = cut([COLS], I32)
        src_i = cut([COLS], I32)
        dst_i = cut([COLS], I32)
        block16 = cut([COLS], BF16)
        v1_16 = cut([COLS], F16)
        v2_16 = cut([COLS], F16)
        posl_16 = cut([COLS], F16)
        post_f = cut([COLS])
        pos_f = cut([COLS])
        unit = cut([2 * P], BF16)
        iota_m = cut([P, GROUP], F16)
        after_sort = used[0]
        sel = cut([NB, P], BF16)
        below16 = cut([P], BF16)
        mask = [cut([COLS], BF16) for _ in range(2)]
        a1flat = a1row[:, :, :].rearrange("p b m -> p (b m)")
        count_f, scan_f, ones_row = (a1flat[:, n * COLS:(n + 1) * COLS] for n in range(3))
        carry_i, digit_i = (a1flat[:, n * COLS:(n + 1) * COLS].bitcast(I32) for n in (3, 4))
        carry = [cut([COLS], BF16) for _ in range(3)]
        first_rows = cut([P], F16)
        after = cut([TMAX], F16)
        small = cut([16])
        small_i = cut([16], I32)
        wcat = cut([KD, 2 * D])
        bcat = cut([2 * D])
        brest = cut([2 * D])
        bias3 = cut([2 * D], BF16)
        bpart = cut([2 * D], BF16)
        ones16 = cut([P], BF16)
        wa = cut([2, D])
        ba = cut([2])
        xn = cut([2, D])
        xt = cut([2, KD, P])
        xij = cut([2, 2, ROW])
        junk = cut([2, 2, D])
        a1diag = cut([4, P])
        used[0] = after_sort
        hot = [cut([P, GROUP], F16) for _ in range(2)]
        hot1 = [cut([P, GROUP], F16) for _ in range(2)]
        hot2 = [cut([P, GROUP], F16) for _ in range(2)]
        tile_hot = [cut([GROUP, TMAX], F16) for _ in range(2)]
        out_v1 = cut([TMAX])
        out_v2 = cut([TMAX], I32)
        out_hi = cut([TMAX], I32)
        used[0] = 0
        W1 = [cut([KD, H]) for _ in range(3)]
        W2 = [cut([KH, D]) for _ in range(3)]
        b2all = cut([X, D])
        hT = [cut([KH, FFN_ROWS]) for _ in range(2)]
        tiles = (a1flat, [0])
        xg = [cut([2, D], region=tiles) for _ in range(2)]
        xgT = [cut([KD, FFN_ROWS], region=tiles) for _ in range(2)]
        yo = [cut([2, D], region=tiles) for _ in range(2)]
        back = cut([4, 2, D], region=tiles)

        b1T = sb("b1T", [P, X * KH])
        b1raw = sb("b1raw", [X * KH, P])
        wg = sb("wg", [P, KD, X])
        bg = sb("bg", [P, X])
        yn = ring[:, :, :].rearrange("p a b -> p (a b)")[:, 0:8 * D].rearrange("p (a b) -> p a b", a=8)
        ynT = gate[:, 0:4, :]
        logits = sb("logits", [P, NB, X])
        stats = logits[:, :, 0:6]
        top = sb("top", [P, TOP_K, NB])
        hit = sb("hit", [P, NB, X])
        lead = sb("lead", [P, NB, X])
        diff = sb("diff", [P, NB])
        wk = [sb(f"wk{k}", [P, NB]) for k in range(TOP_K)]
        idx = [sb(f"idx{k}", [P, NB]) for k in range(TOP_K)]
        eh = [sb(f"eh{k}", [P, X, NB]) for k in range(TOP_K)]
        ehs = sb("ehs", [P, X, NB])
        esc = sb("esc", [P, X, NB])
        valid = sb("valid", [P, NB])
        etot = sb("etot", [P, X])
        et = sb("et", [P, 6, X])
        eti = sb("eti", [P, X], I32)
        posk_f = sb("posk_f", [P, NB])
        posk = sb("posk", [P, NB, TOP_K], I32)
        placesk = sb("placesk", [P, 4, TOP_K], I32)
        zeros = ring[:, :, :].rearrange("p a b -> p (a b)")[:, 0:4 * D]
        ecmp = sb("ecmp", [P, FT, X])
        esum = sb("esum", [P, FT])
        expert = sb("expert", [P, FT], I32)
        fresh = sb("fresh", [P, FT], I32)

        def chain(eng, name):
            s, n = sem(name), [0]

            def link(ins):
                n[0] += 1
                ins.then_inc(s, 1)
                eng.wait_ge(s, n[0])
            return link


        def flat(ap):
            return ap.rearrange("p a b -> p (a b)")

        s_dummy = sem("carries_pool_waits")
        s_dve = sem("carries_dve_waits")
        s_pe = sem("carries_pe_waits")

        s_const = sem("constants_ready")
        s_x = [sem(f"x_loaded{n}") for n in range(5)]
        s_w = sem("weights_loaded")
        s_e = sem("edges_loaded")
        XG = [0, 12, 24, 36, REAL - 1]

        with nc.Block() as block:
            @block.vector
            def _(dve):
                nc.vector.memset(src_i[:, FULL:COLS], DEAD)
                nc.vector.memset(dst_i[:, FULL:COLS], 0)
                nc.vector.memset(acc[:, REAL - 1:NB, :], 0.0)
                nc.vector.memset(ones[:, :], 1.0)
                nc.vector.memset(zeros, 0.0)
                nc.vector.memset(ones_row, 1.0)
                nc.vector.memset(ones16, 1.0)
                nc.vector.memset(bias3, 0.0)
                nc.vector.memset(unit, 0.0)
                nc.vector.memset(pos_f, -1.0).then_inc(s_const, 1)
                dve.wait_ge(s_const, 1)
                nc.vector.memset(unit[:, P:P + 1], 1.0).then_inc(s_const, 1)

            @block.sync
            def _(sp):
                sp.wait_ge(s_const, 2)
                for dram, tile in ((src, src_i), (dst, dst_i)):
                    sp.dma_start(tile[:, 0:FULL], dram[0:FULL * P].rearrange("(p j) -> p j", p=P)).then_inc(s_e, 16)
                    sp.dma_start(tile[0:TAIL, FULL:FULL + 1],
                                 dram[FULL * P:E].rearrange("(p j) -> p j", j=1)).then_inc(s_e, 16)
                for n in range(4):
                    a, b = XG[n], XG[n + 1]
                    sp.dma_start(acc[:, a:b, :], x[a * P:b * P, :].rearrange("(b p) d -> p b d", p=P)).then_inc(s_x[n], 16)
                sp.dma_start(acc[0:LAST, REAL - 1, :], x[(REAL - 1) * P:N, :]).then_inc(s_x[4], 16)

            @block.scalar
            def _(act):
                for n, (w, b, wv, bv) in enumerate(((g_w2, g_b2, wa2, ba2), (g_w1, g_b1, wa1, ba1))):
                    act.dma_start(wcat[:, :, n * D:(n + 1) * D], w.rearrange("(k p) n -> p k n", p=P)).then_inc(s_w, 16)
                    act.dma_start(bcat[:, n * D:(n + 1) * D], b.partition_broadcast(P)).then_inc(s_w, 16)
                    act.dma_start(wa[:, n, :], wv.partition_broadcast(P)).then_inc(s_w, 16)
                    act.dma_start(ba[:, n:n + 1], bv.partition_broadcast(P)).then_inc(s_w, 16)
                act.dma_start(wg[:, :, :], w_gate.rearrange("(k p) e -> p k e", p=P)).then_inc(s_w, 16)
                act.dma_start(bg[:, :], b_gate.partition_broadcast(P)).then_inc(s_w, 16)
                act.dma_start(b1raw[:, :], f_b1.rearrange("e (k p) -> (e k) p", p=P)).then_inc(s_w, 16)

            @block.gpsimd
            def _(pool):
                link = chain(pool, "pool_constants")
                for n, (_, _, t) in enumerate(PARTS):
                    nc.gpsimd.memset(part[n]["sender"][:, t:t + BODY], 0)
                nc.gpsimd.memset(sel, 1.0)
                nc.gpsimd.memset(first_rows, 1.0)
                nc.gpsimd.memset(below[:, :], 1.0)
                nc.gpsimd.memset(below16, 1.0)
                nc.gpsimd.memset(valid[:, :], 1.0)
                nc.gpsimd.memset(ident[:, :], 1.0)
                link(nc.gpsimd.iota(tmp_i, [[1, COLS]], base=0, channel_multiplier=0))
                nc.gpsimd.tensor_copy(iota_16[:, :], tmp_i[:, 0:TMAX])
                nc.gpsimd.tensor_copy(row_f[:, :], tmp_i[:, 0:TMAX])
                nc.gpsimd.tensor_copy(iota_m, tmp_i[:, 0:P].unsqueeze(2).to_broadcast([P, P, GROUP]))
                nc.gpsimd.tensor_copy(iota_1[:, :], tmp_i[:, 1:P + 1])
                nc.gpsimd.affine_select(out=sel, in_=sel, pattern=[[-1, NB], [0, P]], base=0, channel_multiplier=1,
                                        compare_op=ALU.is_equal, fill=0.0)
                nc.gpsimd.affine_select(out=first_rows, in_=first_rows, pattern=[[0, P]], base=REAL - 1,
                                        channel_multiplier=-1, compare_op=ALU.is_gt, fill=0.0)
                nc.gpsimd.affine_select(out=below[:, :], in_=below[:, :], pattern=[[1, P]], base=0,
                                        channel_multiplier=-1, compare_op=ALU.is_gt, fill=0.0)
                nc.gpsimd.affine_select(out=below16, in_=below16, pattern=[[1, P]], base=0,
                                        channel_multiplier=-1, compare_op=ALU.is_gt, fill=0.0)
                nc.gpsimd.affine_select(out=valid[:, :], in_=valid[:, :], pattern=[[-P, NB]], base=N,
                                        channel_multiplier=-1, compare_op=ALU.is_gt, fill=0.0)
                link(nc.gpsimd.affine_select(out=ident[:, :], in_=ident[:, :], pattern=[[-1, P]], base=0,
                                             channel_multiplier=1, compare_op=ALU.is_equal, fill=0.0))

        s_mask = sem("mask_ready")
        s_counted = sem("mask_counted")
        s_cnt = sem("counts_ready")
        s_tiles = sem("tiles_ready")
        s_base = sem("bases_ready")
        s_cmp = sem("ends_compared")
        s_blk = sem("tile_blocks_ready")
        s_carry = sem("carries_ready")
        s_rank = sem("ranks_ready")
        s_ranked = sem("ranks_taken")
        s_bn = sem("moments_taken")
        s_var = sem("variance_ready")
        s_sd = sem("deviation_ready")
        s_xn = sem("xn_ready")
        s_acc = sem("xn_added")
        s_xnT = sem("xn_transposed")
        s_xt = sem("xt_ready")
        s_lin = sem("linear_ready")
        s_xij = sem("table_row_ready")
        s_dot = sem("dots_ready")
        s_tab = [sem(f"table_stored{u}") for u in range(2)]
        s_leaky = sem("leaky_and_dots")
        s_fifth = sem("fifth_ready")
        s_a1r = sem("a1_row_copied")
        s_a1b = sem("a1_broadcast")
        s_xs0 = sem("xs_zeroed")
        s_scaled = sem("scale_and_shift_ready")
        RANK_CUTS = ((0, WA), (WA, COLS))

        def moments(dve, link, done):
            with dve.Fori(0, NB) as b:
                nc.vector.bn_stats(flat(stats[:, bass.ds(b, 1), :]), flat(acc[:, bass.ds(b, 1), :])).then_inc(s_bn, 1)
            dve.wait_ge(s_bn, NB * (done + 1))
            nc.vector.tensor_tensor(mean2[:, :], stats[:, :, 1], stats[:, :, 4], ALU.add)
            nc.vector.tensor_tensor(rstd[:, :], stats[:, :, 2], stats[:, :, 5], ALU.add)
            link(nc.vector.tensor_tensor(spread[:, :], stats[:, :, 1], stats[:, :, 4], ALU.subtract))
            link(nc.vector.scalar_tensor_tensor(out=spread[:, :], in0=spread[:, :], scalar=0.25, in1=spread[:, :],
                                                op0=ALU.mult, op1=ALU.mult))
            link(nc.vector.scalar_tensor_tensor(out=rstd[:, :], in0=rstd[:, :], scalar=1.0 / D, in1=spread[:, :],
                                                op0=ALU.mult, op1=ALU.add))
            nc.vector.tensor_scalar(rstd[:, :], rstd[:, :], EPS, None, ALU.add).then_inc(s_var, 1)
            dve.wait_ge(s_sd, done + 1)
            link(nc.vector.reciprocal(rstd[:, :], rstd[:, :]))
            nc.vector.scalar_tensor_tensor(out=shift[:, :], in0=mean2[:, :], scalar=-0.5, in1=rstd[:, :],
                                           op0=ALU.mult, op1=ALU.mult).then_inc(s_scaled, 1)
            dve.wait_ge(s_scaled, done + 1)

        with nc.Block() as block:
            @block.gpsimd
            def _(pool):
                pool.sem_inc(s_acc, 2)
                with pool.Fori(0, NB // 2) as b_2:
                    b = b_2 * 2
                    for u in range(2):
                        pool.wait_ge(s_xn, b + (u + 1))
                        a = acc[:, bass.ds(b + u, 1), :].rearrange("p b d -> p (b d)")
                        nc.gpsimd.tensor_tensor(a, a, xn[:, u, :], ALU.add).then_inc(s_acc, 1)

            @block.vector
            def _(dve):
                link = chain(dve, "dve_keys")
                shift_and = nc.vector.tensor_scalar
                dve.sem_inc(s_ranked, 2)
                dve.sem_inc(s_xij, 2)
                dve.wait_ge(s_e, 64)
                link(shift_and(tmp_i, src_i, 7, None, ALU.arith_shift_right))
                link(nc.vector.tensor_copy(block16, tmp_i))
                link(shift_and(tmp_i, dst_i, 3, None, ALU.arith_shift_right))
                link(nc.vector.tensor_scalar(v1_16, tmp_i, 1.0, None, ALU.add))
                link(shift_and(src_i, src_i, P - 1, None, ALU.bitwise_and))
                link(shift_and(dst_i, dst_i, 7, 7, ALU.bitwise_and, ALU.arith_shift_left))
                link(nc.vector.tensor_tensor(v2_16, src_i, dst_i, ALU.add))

                def make_mask(b, slot):
                    nc.vector.tensor_scalar(mask[slot], block16, b, None, ALU.is_equal).then_inc(s_mask, 1)

                for n in range(5):
                    dve.wait_ge(s_x[n], 16)
                dve.wait_ge(s_w, 176)
                for row in (0, 32, 64):
                    src_of = bcat if row == 0 else brest
                    link(nc.vector.tensor_copy(bpart, src_of))
                    link(nc.vector.tensor_copy(bias3[row:row + 1, :], src_of[row:row + 1, :]))
                    link(nc.vector.tensor_tensor(brest, src_of, bpart, ALU.subtract))

                with dve.Fori(0, NB // 2) as b_2:
                    b = b_2 * 2
                    for u in range(2):
                        dve.wait_ge(s_counted, b + (u + 1))
                        make_mask(row_f[:, bass.ds(b + u, 1)], u)
                moments(dve, link, 0)
                dve.wait_ge(s_cnt, 1)
                nc.vector.tensor_copy(count_f[:, WA:COLS], banks[1][:, 0:WB])
                link(nc.vector.tensor_copy(count_f[:, 0:WA], banks[0][:, 0:WA]))
                for n, (c0, w, t) in enumerate(PARTS):
                    link(nc.vector.tensor_tensor_scan(out=scan_f[:, c0:c0 + w], data0=ones_row[:, 0:w],
                                                      data1=count_f[:, c0:c0 + w], initial=0.0,
                                                      op0=ALU.mult, op1=ALU.add))
                    link(nc.vector.tensor_scalar(small_i[:, n:n + 1], scan_f[:, c0 + w - 1:c0 + w], float(P - 1), None, ALU.add))
                    link(shift_and(small_i[:, n:n + 1], small_i[:, n:n + 1], 7, None, ALU.arith_shift_right))
                    link(nc.vector.tensor_copy(small[:, n:n + 1], small_i[:, n:n + 1]))
                nc.vector.memset(small[:, 15:16], 0.0).then_inc(s_tiles, 1)
                link(nc.vector.tensor_tensor(scan_f, scan_f, count_f, ALU.subtract))
                dve.wait_ge(s_base, 1)
                link(nc.vector.tensor_copy(small[:, 2:4], banks[2][:, 0:2]))
                link(nc.vector.tensor_tensor(small[:, 4:6], small[:, 2:4], small[:, 0:2], ALU.add))
                link(nc.vector.tensor_scalar(small[:, 6:8], small[:, 2:4], float(P), None, ALU.mult))
                for n, (c0, w, t) in enumerate(PARTS):
                    link(nc.vector.tensor_scalar(carry_i[:, c0:c0 + w], scan_f[:, c0:c0 + w], small[:, 6 + n:7 + n],
                                                 None, ALU.add))
                for d in range(3):
                    link(shift_and(digit_i, carry_i, 127 << (7 * d), None, ALU.bitwise_and))
                    link(nc.vector.tensor_copy(carry[d], digit_i))
                nc.vector.memset(small[:, 14:15], 0.0).then_inc(s_carry, 1)
                for n, (c0, w, t) in enumerate(PARTS):
                    nc.vector.tensor_scalar(after[:, 0:t], row_f[:, 0:t], small[:, 4 + n:5 + n], None,
                                            ALU.is_ge).then_inc(s_cmp, 1)
                    dve.wait_ge(s_blk, n + 1)
                    for k, (a, z) in enumerate(CUTS[n]):
                        link(nc.vector.tensor_copy(part[n]["block"][:, a:z], banks[2 + k][:, 0:z - a]))

                def take(k, slot):
                    dve.wait_ge(s_rank, k)
                    dve.wait_ge(s_mask, k + NB)
                    dve.sem_inc(s_dve, 1)
                    for c, (a, z) in enumerate(RANK_CUTS):
                        last = nc.vector.copy_predicated(pos_f[:, a:z], mask[slot][:, a:z].bitcast(U16),
                                                         banks[2 + 2 * slot + c][:, 0:z - a])
                    last.then_inc(s_ranked, 1)
                    dve.wait_ge(s_ranked, k + 2)

                def rows(b, u):
                    dve.wait_ge(s_fifth, b + (u + 1))
                    dve.wait_ge(s_dot, b + (u + 1))
                    o = banks[u][:, :].rearrange("p (s d) -> p s d", s=2)
                    nc.vector.tensor_tensor(xij[:, u, :, 0:D], o, junk[:, u, :, :], ALU.max).then_inc(s_leaky, 1)
                    dve.wait_ge(s_leaky, b * 2 + (2 * u + 1))
                    for side in range(2):
                        last = nc.vector.tensor_tensor_reduce(out=junk[:, u, side, :], in0=xij[:, u, side, 0:D],
                                                              in1=wa[:, side, :], scale=1.0, scalar=ba[:, side:side + 1],
                                                              op0=ALU.mult, op1=ALU.add, accum_out=xij[:, u, side, D:ROW])
                    last.then_inc(s_leaky, 1)
                    dve.wait_ge(s_leaky, b * 2 + (2 * u + 2))
                    dve.wait_ge(s_a1b, b + (u + 1))
                    nc.vector.tensor_scalar(a1diag[:, u, :], ident[:, :], xij[:, u, 1, D:ROW], None,
                                            ALU.mult).then_inc(s_xij, 1)

                def turn(b, last=False):
                    make_mask(row_f[:, bass.ds(b + 1, 1)], 1)
                    take(b + 1, 0)
                    if not last:
                        make_mask(row_f[:, bass.ds(b + 2, 1)], 0)
                    take(b + 2, 1)
                    for u in range(2):
                        rows(b, u)

                make_mask(row_f[:, 0:1], 0)
                with dve.Fori(0, (NB - 2) // 2) as b_2:
                    turn(b_2 * 2)
                turn(NB - 2, last=True)
                link(nc.vector.tensor_copy(tmp_i, pos_f))
                link(shift_and(src_i, tmp_i, P - 1, None, ALU.bitwise_and))
                link(shift_and(dst_i, tmp_i, 7, None, ALU.arith_shift_right))
                link(nc.vector.tensor_copy(posl_16, src_i))
                link(nc.vector.tensor_copy(post_f, dst_i))

            @block.scalar
            def _(act):
                act.sem_inc(s_xt, 2)
                act.sem_inc(s_a1r, 1)
                act.wait_ge(s_var, 1)
                nc.scalar.activation(rstd[:, :], rstd[:, :], ACT.Sqrt).then_inc(s_sd, 1)
                act.wait_ge(s_scaled, 1)

                def normalize(b, u):
                    act.wait_ge(s_acc, b + (u + 1))
                    act.wait_ge(s_xnT, b + (u + 1))
                    nc.scalar.activation(xn[:, u, :], flat(acc[:, bass.ds(b + u, 1), :]), ACT.Identity,
                                         scale=rstd[:, bass.ds(b + u, 1)], bias=shift[:, bass.ds(b + u, 1)]).then_inc(s_xn, 1)

                def copy_xt(b, u):
                    act.wait_ge(s_xnT, b + (u + 3))
                    nc.scalar.copy(xt[:, u, :, :], banks[6][:, u * D:(u + 1) * D].rearrange("p (k m) -> p k m", k=KD)
                                   ).then_inc(s_xt, 1)

                def fifth(b, u):
                    act.wait_ge(s_lin, b + (u + 1))
                    act.wait_ge(s_xij, b + (u + 1))
                    nc.scalar.mul(junk[:, u, :, :], banks[u][:, :].rearrange("p (s d) -> p s d", s=2), SLOPE).then_inc(s_fifth, 1)

                def copy_a1(b, u):
                    act.wait_ge(s_a1b, b + (u + 3))
                    nc.scalar.copy(flat(a1row[:, bass.ds(b + u, 1), :]), banks[7][:, 0:P]).then_inc(s_a1r, 1)

                def turn(b, first=False, last=False):
                    for u in range(2):
                        if not last:
                            normalize(b + 2, u)
                    for u in range(2):
                        fifth(b, u)
                        if not last:
                            copy_xt(b + 2, u)
                        if not first:
                            copy_a1(b - 2, u)
                for u in range(2):
                    normalize(0, u)
                for u in range(2):
                    copy_xt(0, u)
                turn(0, first=True)
                with act.Fori(0, (NB - 4) // 2) as b_2:
                    turn(b_2 * 2 + 2)
                turn(NB - 2, last=True)
                for u in range(2):
                    copy_a1(NB - 2, u)

            @block.tensor
            def _(pe):
                pe.sem_inc(s_counted, 2)
                pe.sem_inc(s_xnT, 2)
                pe.sem_inc(s_a1b, 2)
                for c, (a, z) in enumerate(RANK_CUTS):
                    nc.tensor.matmul(banks[c][:, 0:z - a], unit[:, 0:P], iota_16[:, 0:z - a], start=True, stop=False)
                with pe.Fori(0, NB // 2) as b_2:
                    b = b_2 * 2
                    for u in range(2):
                        pe.wait_ge(s_mask, b + (u + 1))
                        pe.sem_inc(s_pe, 1)
                        for c, (a, z) in enumerate(RANK_CUTS):
                            mm = nc.tensor.matmul(banks[c][:, 0:z - a], unit[:, bass.ds(P - u - b, P)], mask[u][:, a:z],
                                                  start=False, stop=False)
                        mm.then_inc(s_counted, 1)
                for c, (a, z) in enumerate(RANK_CUTS):
                    mm = nc.tensor.matmul(banks[c][:, 0:z - a], unit[:, 0:P], iota_16[:, 0:z - a], start=False, stop=True)
                mm.then_inc(s_cnt, 1)
                pe.wait_ge(s_tiles, 1)
                nc.tensor.matmul(banks[2][:, 0:2], below[:, :], small[:, 0:2], start=True, stop=True).then_inc(s_base, 1)
                pe.wait_ge(s_carry, 1)
                for n, (c0, w, t) in enumerate(PARTS):
                    pe.wait_ge(s_cmp, n + 1)
                    for k, (a, z) in enumerate(CUTS[n]):
                        mm = nc.tensor.matmul(banks[2 + k][:, 0:z - a], first_rows, after[:, a:z], start=True, stop=True)
                    mm.then_inc(s_blk, 1)
                def ranks(b, u):
                    pe.wait_ge(s_mask, b + (NB + u + 1))
                    pe.wait_ge(s_ranked, b + (u + 1))
                    for c, (a, z) in enumerate(RANK_CUTS):
                        o = banks[2 + 2 * u + c][:, 0:z - a]
                        nc.tensor.matmul(o, below16, mask[u][:, a:z], start=True, stop=False)
                        for d in range(3):
                            mm = nc.tensor.matmul(o, flat(sel[:, bass.ds(b + u, 1), :]), carry[d][:, a:z],
                                                  start=False, stop=(d == 2))
                    mm.then_inc(s_rank, 1)

                def transposes(b, u):
                    pe.wait_ge(s_xn, b + (u + 1))
                    pe.wait_ge(s_xt, b + (u + 2))
                    for k in range(KD):
                        mm = nc.tensor.transpose(banks[6][:, u * D + k * P:u * D + (k + 1) * P],
                                                 xn[:, u, k * P:(k + 1) * P], ident[:, :])
                    mm.then_inc(s_xnT, 1)

                def linears(b, u):
                    pe.wait_ge(s_xt, b + (u + 3))
                    pe.wait_ge(s_xij, b + (u + 1))
                    for k in range(KD):
                        nc.tensor.matmul(banks[u][:, :], xt[:, u, k, :], wcat[:, k, :], start=(k == 0), stop=False)
                    nc.tensor.matmul(banks[u][:, :], ones16[0:96, :], bias3[0:96, :], start=False, stop=True).then_inc(s_lin, 1)

                def spread_a1(b, u):
                    pe.wait_ge(s_xij, b + (u + 3))
                    pe.wait_ge(s_a1r, b + (u + 1))
                    nc.tensor.matmul(banks[7][:, 0:P], ones[:, :], a1diag[:, u, :], start=True, stop=True).then_inc(s_a1b, 1)

                def turn(b, first=False, last=False):
                    for u in range(2):
                        ranks(b, u)
                    for u in range(2):
                        linears(b, u)
                        if not last:
                            transposes(b + 2, u)
                        if not first:
                            spread_a1(b - 2, u)
                for u in range(2):
                    transposes(0, u)
                turn(0, first=True)
                with pe.Fori(0, (NB - 4) // 2) as b_2:
                    turn(b_2 * 2 + 2)
                turn(NB - 2, last=True)
                for u in range(2):
                    spread_a1(NB - 2, u)

            @block.sync
            def _(sp):
                per = FT * FFN_ROWS // P * D // (4 * D)
                sp.dma_start(xs.rearrange("(p a r) d -> p a (r d)", p=P, a=per),
                             zeros.unsqueeze(1).to_broadcast([P, per, 4 * D])).then_inc(s_xs0, 16)
                sp.sem_inc(s_dot, 2)
                with sp.Fori(0, NB // 2) as b_2:
                    b = b_2 * 2
                    for u in range(2):
                        sp.wait_ge(s_xij, b + (u + 3))
                        sp.dma_start(table[bass.ds((b + u) * P, P), :], xij[:, u, 0, :]).then_inc(s_tab[u], 16)
                    for u in range(2):
                        sp.wait_ge(s_tab[u], 8 * b + 16)
                        sp.sem_inc(s_dot, 1)
                sp.wait_ge(s_xs0, 16)

        s_hot = sem("one_hots_ready")
        s_lone = sem("plain_one_hot_ready")
        s_moved = sem("one_hots_used")
        s_sorted = sem("sorted")
        s_opened = sem("sort_banks_opened")
        SORT_BANKS = ((0, 1), (2, 4))

        def one_hots(dve, n, g, slot, step=None):
            c0, w, t = PARTS[n]
            at = g + ((PARTS[0][1] // GROUP if n else 0) + 1)
            cols = g * GROUP + c0

            def rep(a):
                return a[:, bass.ds(cols, GROUP)].unsqueeze(1).to_broadcast([P, P, GROUP])
            if step in (0, None):
                dve.wait_ge(s_moved, at)
                nc.vector.tensor_tensor(hot[slot], iota_m, rep(posl_16), ALU.is_equal).then_inc(s_lone, 1)
            for c in {0: range(0, 1), 1: range(1, 4), 2: range(4, 7), 3: range(7, 8), 4: (), None: range(GROUP)}[step]:
                nc.vector.tensor_scalar(tile_hot[slot][:, c, 0:t], iota_16[:, 0:t], post_f[:, bass.ds(cols + c, 1)], None,
                                        ALU.is_equal)
            if step in (3, None):
                dve.wait_ge(s_lone, at)
                nc.vector.tensor_tensor(hot1[slot], hot[slot], rep(v1_16), ALU.mult)
            if step in (4, None):
                nc.vector.tensor_tensor(hot2[slot], hot[slot], rep(v2_16), ALU.mult).then_inc(s_hot, 1)

        def move(pe, n, g, slot, cs=range(GROUP)):
            done = PARTS[0][1] // GROUP if n else 0
            if cs[0] == 0:
                pe.wait_ge(s_hot, g + (done + 1))
            for c in cs:
                for v, h in enumerate((hot1, hot2)):
                    for k, (a, z) in enumerate(CUTS[n]):
                        mm = nc.tensor.matmul(banks[SORT_BANKS[n][v] + k][:, 0:z - a], h[slot][:, :, c],
                                              tile_hot[slot][:, c, a:z], start=False, stop=False)
            if cs[-1] == GROUP - 1:
                mm.then_inc(s_moved, 1)

        def open_or_close(n, first):
            for v in range(2):
                for k, (a, z) in enumerate(CUTS[n]):
                    mm = nc.tensor.matmul(banks[SORT_BANKS[n][v] + k][:, 0:z - a], unit[:, 0:P], iota_16[:, 0:z - a],
                                          start=first, stop=not first)
            mm.then_inc(s_opened if first else s_sorted, 1)

        def decode(dve, link, n):
            dve.wait_ge(s_sorted, n + 1)
            t = PARTS[n][2]
            for k, (a, z) in enumerate(CUTS[n]):
                link(nc.vector.tensor_copy(out_v1[:, a:z], banks[SORT_BANKS[n][0] + k][:, 0:z - a]))
                link(nc.vector.tensor_copy(out_v2[:, a:z], banks[SORT_BANKS[n][1] + k][:, 0:z - a]))
            link(nc.vector.tensor_scalar(out_hi[:, 0:t], out_v2[:, 0:t], 7, None, ALU.arith_shift_right))
            link(nc.vector.tensor_scalar(out_v2[:, 0:t], out_v2[:, 0:t], P - 1, None, ALU.bitwise_and))
            link(nc.vector.scalar_tensor_tensor(out=part[n]["receiver"][:, :], in0=out_v1[:, 0:t], scalar=1.0,
                                                in1=out_v2[:, 0:t], op0=ALU.min, op1=ALU.add))
            link(nc.vector.tensor_scalar(out_v1[:, 0:t], out_v1[:, 0:t], -1.0, 0.0, ALU.add, ALU.max))
            link(nc.vector.scalar_tensor_tensor(out=part[n]["sender"][:, 0:t], in0=out_v1[:, 0:t], scalar=8.0,
                                                in1=out_hi[:, 0:t], op0=ALU.mult, op1=ALU.add))

        with nc.Block() as block:
            @block.vector
            def _(dve):
                link = chain(dve, "dve_decode0")
                with dve.Fori(0, (WA // GROUP) // 2) as g_2:
                    g = g_2 * 2
                    for u in range(2):
                        one_hots(dve, 0, g + u, u)
                decode(dve, link, 0)

            @block.tensor
            def _(pe):
                pe.sem_inc(s_moved, 2)
                open_or_close(0, True)
                with pe.Fori(0, (WA // GROUP) // 2) as g_2:
                    g = g_2 * 2
                    for u in range(2):
                        move(pe, 0, g + u, u)
                open_or_close(0, False)

        s_place = sem("places_staged")
        s_row = [sem(f"rows_gathered{q}") for q in range(QUARTERS)]
        s_gate = sem("gates_ready")
        s_lhs = sem("gated_one_hots_ready")
        s_sum = sem("tile_sums_ready")
        s_add = sem("tile_sums_added")

        sums = [banks[n] for n in (0, 1, 6, 7)]

        def loaded(eng, regs, n, t0):
            eng.load(regs, part[n]["block"][0:1, bass.ds(t0, QUARTER)])
            return [eng.snap(reg, min_val=0, max_val=NB - 1) for reg in regs]

        def gather(pool, n, i, done):
            for q in range(QUARTERS):
                pool.wait_ge(s_sum, i * BODY + (q * QUARTER + done + QUARTER))
                pool.wait_ge(s_place, i * QUARTERS + (q + done // QUARTER + 1 + QUARTERS * n))
                pool.sem_inc(s_dummy, 1)
                for u in range(QUARTER):
                    pool.indirect_dma_start(out=ring[:, q * QUARTER + u, :], out_offset=None, in_=table[:, :],
                                            in_offset=bass.IndirectOffsetOnAxis(ap=places[:, q, u:u + 1], axis=0)
                                            ).then_inc(s_row[q], 16)

        def stage_places(n, q, t0):
            nc.scalar.copy(places[:, q, :], part[n]["sender"][:, bass.ds(t0, QUARTER)]).then_inc(s_place, 1)

        def gates(act, regs, n, i, done):
            for q in range(QUARTERS):
                t0 = i * BODY + q * QUARTER
                blocks = loaded(act, regs, n, t0)
                act.wait_ge(s_row[q], i * (16 * QUARTER) + (16 * QUARTER * (done // BODY + 1)))
                for u in range(QUARTER):
                    act.wait_ge(s_lhs, t0 + (done + u + 1))
                    nc.scalar.activation(gate[:, (q * QUARTER + u) % SLOTS_G, :], flat(a1row[:, bass.ds(blocks[u], 1), :]),
                                         ACT.Sigmoid, bias=ring[:, q * QUARTER + u, D:ROW]).then_inc(s_gate, 1)
                stage_places(n, q, t0 + BODY)

        def gated(dve, n, t, j, done):
            dve.wait_ge(s_gate, t + (done + j + 1))
            dve.wait_ge(s_sum, t + (done + j + 1 + BODY - SLOTS_G))
            nc.vector.scalar_tensor_tensor(out=lhs[:, j % SLOTS_G, :], in0=iota_1[:, :],
                                           scalar=part[n]["receiver"][:, bass.ds(t + j, 1)], in1=gate[:, j % SLOTS_G, :],
                                           op0=ALU.is_equal, op1=ALU.mult).then_inc(s_lhs, 1)

        def lhs_and_add(dve, regs, n, i, done, between=None, last=False):
            t = i * BODY
            for j in range(BODY):
                u = j % QUARTER
                if u == 0:
                    blocks = loaded(dve, regs, n, t + j)
                if not last or j + LEAD < BODY:
                    gated(dve, n, t, j + LEAD, done)
                dve.wait_ge(s_sum, t + (done + j + 1 + BODY))
                dve.wait_ge(s_add, t + (done + j + 4))
                a = flat(acc[:, bass.ds(blocks[u], 1), :])
                nc.vector.tensor_tensor(a, a, sums[u][:, 0:D], ALU.add).then_inc(s_add, 1)
                if between:
                    between(j)

        def tile_sums(pe, n, i, done, between):
            for q in range(QUARTERS):
                t0 = i * BODY + q * QUARTER
                for u in range(QUARTER):
                    pe.wait_ge(s_lhs, t0 + (done + u + SLOTS_G + 1))
                    pe.wait_ge(s_add, t0 + (done + u + 1))
                    nc.tensor.matmul(sums[u][:, 0:D], lhs[:, (q * QUARTER + u) % SLOTS_G, :], ring[:, q * QUARTER + u, 0:D],
                                     start=True, stop=True).then_inc(s_sum, 1)
                    between(q * QUARTER + u)

        PERIOD = 5
        assert SORTS_PER_BODY * PERIOD < BODY
        MOVES = (range(0, 2), range(2, 4), range(4, 6), range(6, 7), range(7, 8))

        with nc.Block() as block:
            @block.gpsimd
            def _(pool):
                with pool.Fori(0, TA // BODY) as i:
                    gather(pool, 0, i, 0)

            @block.scalar
            def _(act):
                for q in range(QUARTERS):
                    stage_places(0, q, q * QUARTER)
                regs = [act.alloc_register(f"act_block{u}") for u in range(QUARTER)]
                with act.Fori(0, TA // BODY) as i:
                    gates(act, regs, 0, i, 0)

            @block.vector
            def _(dve):
                link = chain(dve, "dve_decode1")
                regs = [dve.alloc_register(f"dve_block{u}") for u in range(QUARTER)]
                dve.sem_inc(s_lhs, SLOTS_G)
                dve.sem_inc(s_add, 4)
                for j in range(LEAD):
                    gated(dve, 0, 0, j, 0)
                one_hots(dve, 1, 0, 0)

                def sort_body(i, v):
                    def step(j):
                        group = v * SORTS_PER_BODY + j // PERIOD + 1
                        if j < SORTS_PER_BODY * PERIOD and not (isinstance(i, int) and i * SORTS_PER_BODY + group == WB // GROUP):
                            one_hots(dve, 1, i * SORTS_PER_BODY + group, group % 2, j % PERIOD)
                    lhs_and_add(dve, regs, 0, i + v, 0, step)
                with dve.Fori(0, SORT_BODIES // 2 - 1) as i_2:
                    for v in range(2):
                        sort_body(i_2 * 2, v)
                for v in range(2):
                    sort_body(SORT_BODIES - 2, v)
                with dve.Fori(SORT_BODIES, TA // BODY - 1) as i:
                    lhs_and_add(dve, regs, 0, i, 0)
                lhs_and_add(dve, regs, 0, TA // BODY - 1, 0, last=True)
                decode(dve, link, 1)

            @block.tensor
            def _(pe):
                pe.sem_inc(s_sum, 16)
                open_or_close(1, True)
                with pe.Fori(0, SORT_BODIES // 2) as i_2:
                    i = i_2 * 2
                    for v in range(2):
                        def step(j, v=v):
                            group = v * SORTS_PER_BODY + j // PERIOD
                            if j < SORTS_PER_BODY * PERIOD:
                                move(pe, 1, i * SORTS_PER_BODY + group, group % 2, MOVES[j % PERIOD])
                        tile_sums(pe, 0, i + v, 0, step)
                open_or_close(1, False)
                with pe.Fori(SORT_BODIES, TA // BODY) as i:
                    tile_sums(pe, 0, i, 0, lambda u: None)

        with nc.Block() as block:
            @block.gpsimd
            def _(pool):
                with pool.Fori(0, TB // BODY) as i:
                    gather(pool, 1, i, TA)

            @block.scalar
            def _(act):
                for q in range(QUARTERS):
                    stage_places(1, q, q * QUARTER)
                regs = [act.alloc_register(f"act_block{u}_") for u in range(QUARTER)]
                with act.Fori(0, TB // BODY) as i:
                    gates(act, regs, 1, i, TA)

            @block.vector
            def _(dve):
                regs = [dve.alloc_register(f"dve_block{u}_") for u in range(QUARTER)]
                for j in range(LEAD):
                    gated(dve, 1, 0, j, TA)
                with dve.Fori(0, TB // BODY - 1) as i:
                    lhs_and_add(dve, regs, 1, i, TA)
                lhs_and_add(dve, regs, 1, TB // BODY - 1, TA, last=True)

            @block.tensor
            def _(pe):
                with pe.Fori(0, TB // BODY) as i:
                    tile_sums(pe, 1, i, TA, lambda u: None)


        s_yn = sem("yn_ready")
        s_ynT = sem("yn_transposed")
        s_ynTc = sem("ynT_copied")
        s_logit = sem("logits_ready")
        s_b1 = sem("b1_transposed")
        s_b1c = sem("b1T_ready")
        s_top = sem("top_found")
        s_diff = sem("top_difference_ready")
        s_wk = sem("top_weights_ready")
        s_etot = sem("expert_counts_ready")
        s_eoff = sem("expert_offsets_ready")

        def normalized(slot, b):
            return nc.vector.tensor_scalar(yn[:, slot, :], flat(acc[:, b, :]), rstd[:, b], shift[:, b], ALU.mult, ALU.add)

        with nc.Block() as block:
            @block.vector
            def _(dve):
                link = chain(dve, "dve_route")
                dve.sem_inc(s_logit, 2)
                moments(dve, link, 1)
                with dve.Fori(0, NB // 2) as b_2:
                    b = b_2 * 2
                    for u in range(2):
                        dve.wait_ge(s_ynT, b + (u + 1))
                        normalized(u, bass.ds(b + u, 1)).then_inc(s_yn, 1)
                dve.wait_ge(s_logit, NB + 2)
                link(nc.vector.tensor_tensor(logits[:, :, :], banks[7][:, 0:NB * X].rearrange("p (b e) -> p b e", b=NB),
                                             bg[:, :].unsqueeze(1).to_broadcast([P, NB, X]), ALU.add))
                rest = row_f[:, 0:X].unsqueeze(1).to_broadcast([P, NB, X])
                for k in range(TOP_K):
                    link(nc.vector.tensor_reduce(top[:, k, :], logits[:, :, :], AX_X, ALU.max))
                    link(nc.vector.tensor_tensor(hit[:, :, :], logits[:, :, :],
                                                 top[:, k, :].unsqueeze(2).to_broadcast([P, NB, X]), ALU.is_equal))
                    link(nc.vector.tensor_scalar(lead[:, :, :], rest, -1.0, float(X), ALU.mult, ALU.add))
                    link(nc.vector.tensor_tensor(hit[:, :, :], hit[:, :, :], lead[:, :, :], ALU.mult))
                    link(nc.vector.tensor_reduce(idx[k][:, :], hit[:, :, :], AX_X, ALU.max))
                    link(nc.vector.tensor_scalar(idx[k][:, :], idx[k][:, :], -1.0, float(X), ALU.mult, ALU.add))
                    if k == 0:
                        link(nc.vector.tensor_tensor(hit[:, :, :], rest, idx[k][:, :].unsqueeze(2).to_broadcast([P, NB, X]),
                                                     ALU.is_equal))
                        link(nc.vector.scalar_tensor_tensor(out=logits[:, :, :], in0=hit[:, :, :], scalar=-3e38,
                                                            in1=logits[:, :, :], op0=ALU.mult, op1=ALU.add))
                nc.vector.tensor_tensor(diff[:, :], top[:, 0, :], top[:, 1, :], ALU.subtract).then_inc(s_diff, 1)
                experts_f = row_f[:, 0:X].unsqueeze(2).to_broadcast([P, X, NB])
                for k in range(TOP_K):
                    link(nc.vector.tensor_tensor(eh[k][:, :, :], experts_f, idx[k][:, :].unsqueeze(1).to_broadcast([P, X, NB]),
                                                 ALU.is_equal))
                    link(nc.vector.tensor_tensor(eh[k][:, :, :], eh[k][:, :, :],
                                                 valid[:, :].unsqueeze(1).to_broadcast([P, X, NB]), ALU.mult))
                link(nc.vector.tensor_tensor(ehs[:, :, :], eh[0][:, :, :], eh[1][:, :, :], ALU.add))
                for e in range(X):
                    last = nc.vector.tensor_tensor_scan(out=esc[:, e, :], data0=ones[:, 0:NB], data1=ehs[:, e, :],
                                                        initial=0.0, op0=ALU.mult, op1=ALU.add)
                link(last)
                nc.vector.tensor_copy(etot[:, :], esc[:, :, NB - 1]).then_inc(s_etot, 1)
                dve.wait_ge(s_etot, 1)
                link(nc.vector.tensor_tensor(esc[:, :, :], esc[:, :, :], ehs[:, :, :], ALU.subtract))
                dve.wait_ge(s_eoff, 1)
                link(nc.vector.tensor_scalar(eti[:, :], banks[6][:, X:2 * X], float(FFN_ROWS - 1), None, ALU.add))
                link(nc.vector.tensor_scalar(eti[:, :], eti[:, :], FFN_ROWS.bit_length() - 1, None, ALU.arith_shift_right))
                link(nc.vector.tensor_copy(et[:, 0, :], eti[:, :]))
                link(nc.vector.tensor_tensor_scan(out=et[:, 1, :], data0=ones[:, 0:X], data1=et[:, 0, :], initial=0.0,
                                                  op0=ALU.mult, op1=ALU.add))
                link(nc.vector.tensor_tensor(et[:, 2, :], et[:, 1, :], et[:, 0, :], ALU.subtract))
                link(nc.vector.scalar_tensor_tensor(out=et[:, 3, :], in0=et[:, 2, :], scalar=float(FFN_ROWS),
                                                    in1=banks[6][:, 0:X], op0=ALU.mult, op1=ALU.add))
                link(nc.vector.tensor_tensor(esc[:, :, :], esc[:, :, :], et[:, 3, :].unsqueeze(2).to_broadcast([P, X, NB]),
                                             ALU.add))
                for k in range(TOP_K):
                    link(nc.vector.tensor_tensor(eh[k][:, :, :], eh[k][:, :, :], esc[:, :, :], ALU.mult))
                    link(nc.vector.tensor_reduce(posk_f[:, :], eh[k][:, :, :].rearrange("p e b -> p b e"), AX_X, ALU.add))
                    link(nc.vector.tensor_copy(posk[:, :, k], posk_f[:, :]))
                link(nc.vector.tensor_tensor(ecmp[:, :, 0:X - 1], row_f[:, 0:FT].unsqueeze(2).to_broadcast([P, FT, X - 1]),
                                             et[:, 1, 0:X - 1].unsqueeze(1).to_broadcast([P, FT, X - 1]), ALU.is_ge))
                link(nc.vector.tensor_reduce(esum[:, :], ecmp[:, :, 0:X - 1], AX_X, ALU.add))
                link(nc.vector.tensor_copy(expert[:, :], esum[:, :]))
                nc.vector.memset(fresh[:, 0:SLOTS], 1)
                link(nc.vector.tensor_tensor(fresh[:, SLOTS:FT], esum[:, SLOTS:FT], esum[:, 0:FT - SLOTS], ALU.not_equal))

            @block.scalar
            def _(act):
                act.sem_inc(s_ynTc, 2)
                act.wait_ge(s_b1, 1)
                nc.scalar.copy(b1T[:, :], banks[5][:, 0:X * KH]).then_inc(s_b1c, 1)
                act.wait_ge(s_var, 2)
                nc.scalar.activation(rstd[:, :], rstd[:, :], ACT.Sqrt).then_inc(s_sd, 1)
                with act.Fori(0, NB // 2) as b_2:
                    b = b_2 * 2
                    for u in range(2):
                        act.wait_ge(s_ynT, b + (u + 3))
                        nc.scalar.copy(ynT[:, u * KD:(u + 1) * KD, :],
                                       banks[u][:, 0:KD * P].rearrange("p (k m) -> p k m", k=KD)).then_inc(s_ynTc, 1)
                act.wait_ge(s_diff, 1)
                nc.scalar.activation(wk[0][:, :], diff[:, :], ACT.Sigmoid)
                nc.scalar.activation(wk[1][:, :], diff[:, :], ACT.Sigmoid, scale=-1.0).then_inc(s_wk, 1)

            @block.tensor
            def _(pe):
                pe.sem_inc(s_ynT, 2)
                nc.tensor.transpose(banks[5][:, 0:X * KH], b1raw[:, :], ident[0:X * KH, 0:X * KH]).then_inc(s_b1, 1)
                with pe.Fori(0, NB // 2) as b_2:
                    b = b_2 * 2
                    for u in range(2):
                        pe.wait_ge(s_yn, b + (u + 1))
                        pe.wait_ge(s_ynTc, b + (u + 1))
                        for k in range(KD):
                            mm = nc.tensor.transpose(banks[u][:, k * P:(k + 1) * P], yn[:, u, k * P:(k + 1) * P], ident[:, :])
                        mm.then_inc(s_ynT, 1)
                    for u in range(2):
                        pe.wait_ge(s_ynTc, b + (u + 3))
                        for k in range(KD):
                            mm = nc.tensor.matmul(banks[7][:, bass.ds((b + u) * X, X)], ynT[:, u * KD + k, :], wg[:, k, :],
                                                  start=(k == 0), stop=(k == KD - 1))
                        mm.then_inc(s_logit, 1)
                pe.wait_ge(s_etot, 1)
                nc.tensor.matmul(banks[6][:, 0:X], below[:, :], etot[:, :], start=True, stop=True)
                nc.tensor.matmul(banks[6][:, X:2 * X], ones[:, :], etot[:, :], start=True, stop=True).then_inc(s_eoff, 1)

        s_tok = sem("token_rows_ready")
        s_sent = [sem(f"rows_sent{u}") for u in range(4)]
        s_sfree = sem("token_rows_free")

        with nc.Block() as block:
            @block.vector
            def _(dve):
                def stage(b, u):
                    dve.wait_ge(s_sfree, b + (u + 1))
                    nc.vector.tensor_copy(placesk[:, u, :], flat(posk[:, bass.ds(b + u, 1), :]))
                    normalized(u, bass.ds(b + u, 1)).then_inc(s_tok, 1)
                with dve.Fori(0, (REAL - 1) // 4) as b_4:
                    b = b_4 * 4
                    for u in range(4):
                        stage(b, u)
                dve.wait_ge(s_sfree, REAL)
                nc.vector.tensor_copy(placesk[:, 0, :], posk[:, REAL - 1, :])
                normalized(0, slice(REAL - 1, REAL)).then_inc(s_tok, 1)

            @block.gpsimd
            def _(pool):
                def send(u, rows):
                    for k in range(TOP_K):
                        pool.indirect_dma_start(out=xs[:, :],
                                                out_offset=bass.IndirectOffsetOnAxis(ap=placesk[0:rows, u, k:k + 1], axis=0),
                                                in_=yn[0:rows, u, :], in_offset=None).then_inc(s_sent[u], 16)
                with pool.Fori(0, (REAL - 1) // 4) as b_4:
                    b = b_4 * 4
                    for u in range(4):
                        pool.wait_ge(s_tok, b + (u + 1))
                        pool.sem_inc(s_dummy, 1)
                        send(u, P)
                pool.wait_ge(s_tok, REAL)
                send(0, LAST)

            @block.sync
            def _(sp):
                sp.sem_inc(s_sfree, 4)
                with sp.Fori(0, (REAL - 1) // 4) as b_4:
                    b = b_4 * 4
                    for u in range(4):
                        sp.wait_ge(s_sent[u], 8 * b + 16 * TOP_K)
                        sp.sem_inc(s_sfree, 1)
                sp.wait_ge(s_sent[0], (REAL - 1) // 4 * 16 * TOP_K + 16 * TOP_K)

        s_wl = [sem(f"expert_weights_loaded{w}") for w in range(SLOTS)]
        s_xg = [sem(f"expert_rows_loaded{u}") for u in range(2)]
        s_b2 = sem("b2_loaded")
        s_xT = sem("rows_transposed")
        s_xTc = sem("rows_T_ready")
        s_mm1 = sem("hidden_ready")
        s_gelu = sem("gelu_ready")
        HB = 4
        s_mm2 = sem("expert_out_ready")
        s_yo = sem("expert_rows_ready")
        s_st = [sem(f"expert_rows_stored{u}") for u in range(2)]
        s_yofree = sem("expert_rows_free")

        def each_tile(eng, step, first=0):
            count = (FT - first) // RUN
            with eng.Fori(0, count) as i:
                for j in range(RUN):
                    step(i * RUN, j + first)
            for j in range(count * RUN + first, FT):
                step(count * RUN, j - count * RUN)

        def at(t, j):
            return bass.ds(t + j, 1) if not isinstance(t, int) else slice(t + j, t + j + 1)

        with nc.Block() as block:
            @block.sync
            def _(sp):
                sp.dma_start(flat(b2all), f_b2.rearrange("e d -> (e d)").partition_broadcast(P)).then_inc(s_b2, 16)

                def load(t, j):
                    rows, w = j % 2, j % SLOTS
                    row0 = (t + j) * FFN_ROWS
                    e = sp.value_load(expert[0:1, at(t, j)], min_val=0, max_val=X - 1)
                    new = sp.value_load(fresh[0:1, at(t, j)], min_val=0, max_val=1)
                    sp.wait_ge(s_mm2, t + (j + 1))
                    sp.dma_start(W1[w], f_w1[bass.ds(e, 1)].rearrange("a (k p) h -> p (a k) h", p=P), cond=new
                                 ).then_inc(s_wl[w], 16)
                    sp.dma_start(W2[w], f_w2[bass.ds(e, 1)].rearrange("a (k p) d -> p (a k) d", p=P), cond=new
                                 ).then_inc(s_wl[w], 16)
                    sp.wait_ge(s_mm2, t + (j + 2))
                    rows_of = xs[bass.ds(row0, FFN_ROWS), :] if not isinstance(row0, int) else xs[row0:row0 + FFN_ROWS, :]
                    sp.dma_start(xg[rows], rows_of.rearrange("(s p) d -> p s d", p=P)).then_inc(s_xg[rows], 16)
                each_tile(sp, load)

            @block.tensor
            def _(pe):
                pe.sem_inc(s_mm2, SLOTS)

                def up(t, j):
                    u, w = j % 2, j % SLOTS
                    pe.wait_ge(s_xg[u], t * 8 + 16 * (j // 2 + 1))
                    for k in range(KD):
                        for s in range(2):
                            mm = nc.tensor.transpose(banks[0][:, k * FFN_ROWS + s * P:k * FFN_ROWS + (s + 1) * P],
                                                     xg[u][:, s, k * P:(k + 1) * P], ident[:, :])
                    mm.then_inc(s_xT, 1)
                    pe.wait_ge(s_wl[w], t // SLOTS * 32 + 32 * (j // SLOTS + 1))
                    pe.wait_ge(s_xTc, t + (j + 1))
                    for h in range(KH):
                        pe.wait_ge(s_gelu, t * KH + (KH * j + h + 1))
                        for k in range(KD):
                            mm = nc.tensor.matmul(banks[1 + h % HB][:, 0:FFN_ROWS],
                                                  W1[w][:, k, h * P:(h + 1) * P], xgT[u][:, k, :],
                                                  start=(k == 0), stop=(k == KD - 1))
                        mm.then_inc(s_mm1, 1)

                def down(t, j):
                    u, w = j % 2, j % SLOTS
                    pe.wait_ge(s_yo, t + (j + 1))
                    pe.wait_ge(s_gelu, t * KH + (KH * (j + 1) + HB))
                    for s in range(2):
                        for h in range(KH):
                            mm = nc.tensor.matmul(banks[5 + u][:, s * D:(s + 1) * D], hT[u][:, h, s * P:(s + 1) * P],
                                                  W2[w][:, h, :], start=(h == 0), stop=(h == KH - 1))
                    mm.then_inc(s_mm2, 1)

                def step(t, j):
                    up(t, j)
                    down(t, j - 1)
                up(0, 0)
                each_tile(pe, step, 1)
                down(FT - 1 - (FT - 1) % RUN, (FT - 1) % RUN)

            @block.scalar
            def _(act):
                act.sem_inc(s_gelu, HB)

                def gelus(t, j):
                    e = act.value_load(expert[0:1, at(t, j)], min_val=0, max_val=X - 1)
                    act.wait_ge(s_mm2, t + (j + 2))
                    for h in range(KH):
                        act.wait_ge(s_mm1, t * KH + (KH * j + h + 1))
                        nc.scalar.activation(hT[j % 2][:, h, :], banks[1 + h % HB][:, 0:FFN_ROWS],
                                             ACT.Gelu, bias=b1T[:, bass.ds(e * KH + h, 1)]).then_inc(s_gelu, 1)
                each_tile(act, gelus)

            @block.vector
            def _(dve):
                dve.sem_inc(s_yo, 2)
                dve.wait_ge(s_b2, 16)

                def turn(t, j):
                    dve.wait_ge(s_xT, t + (j + 1))
                    nc.vector.tensor_copy(flat(xgT[j % 2]), banks[0][:, :]).then_inc(s_xTc, 1)

                def finish(t, j):
                    e = dve.value_load(expert[0:1, at(t, j)], min_val=0, max_val=X - 1)
                    dve.wait_ge(s_mm2, t + (j + 1 + SLOTS))
                    dve.wait_ge(s_yofree, t + (j + 1))
                    nc.vector.tensor_tensor(yo[j % 2], banks[5 + j % 2][:, :].rearrange("p (s d) -> p s d", s=2),
                                            b2all[:, bass.ds(e, 1), :].to_broadcast([P, 2, D]), ALU.add).then_inc(s_yo, 1)

                def step(t, j):
                    turn(t, j)
                    finish(t, j - 1)
                turn(0, 0)
                each_tile(dve, step, 1)
                finish(FT - 1 - (FT - 1) % RUN, (FT - 1) % RUN)

            @block.gpsimd
            def _(pool):
                pool.sem_inc(s_yofree, 2)
                with pool.Fori(0, FT // 2) as t_2:
                    t = t_2 * 2
                    for u in range(2):
                        pool.wait_ge(s_yo, t + (u + 3))
                        pool.sem_inc(s_dummy, 1)
                        pool.dma_start(os[bass.ds((t + u) * FFN_ROWS, FFN_ROWS), :].rearrange("(s p) d -> p s d", p=P),
                                       yo[u]).then_inc(s_st[u], 16)
                    for u in range(2):
                        pool.wait_ge(s_st[u], t * 8 + 16)
                        pool.sem_inc(s_yofree, 1)

        s_stage = sem("places_back_staged")
        s_back = [sem(f"rows_back{u}") for u in range(4)]
        s_mix = sem("token_mixed")
        s_res = sem("results_ready")
        s_out = [sem(f"out_stored{u}") for u in range(4)]
        s_ofree = sem("result_buffers_free")

        with nc.Block() as block:
            @block.gpsimd
            def _(pool):
                def fetch(u, rows):
                    for k in range(TOP_K):
                        pool.indirect_dma_start(out=back[0:rows, u, k, :], out_offset=None, in_=os[:, :],
                                                in_offset=bass.IndirectOffsetOnAxis(ap=placesk[0:rows, u, k:k + 1], axis=0)
                                                ).then_inc(s_back[u], 16)
                with pool.Fori(0, (REAL - 1) // 4) as b_4:
                    b = b_4 * 4
                    for u in range(4):
                        pool.wait_ge(s_stage, b + (u + 1))
                        pool.sem_inc(s_dummy, 1)
                        fetch(u, P)
                pool.wait_ge(s_stage, REAL)
                fetch(0, LAST)

            @block.vector
            def _(dve):
                def stage(b, u):
                    dve.wait_ge(s_ofree, b + (u + 1))
                    nc.vector.tensor_copy(placesk[:, u, :], flat(posk[:, bass.ds(b + u, 1), :])).then_inc(s_stage, 1)

                def mix(u, rows, b, at, n):
                    dve.wait_ge(s_back[u], n)
                    a = flat(acc[0:rows, b, :])
                    nc.vector.scalar_tensor_tensor(out=back[0:rows, u, 0, :], in0=back[0:rows, u, 0, :], scalar=wk[0][0:rows, b],
                                                   in1=a, op0=ALU.mult, op1=ALU.add).then_inc(s_mix, 1)
                    dve.wait_ge(s_mix, at)
                    nc.vector.scalar_tensor_tensor(out=back[0:rows, u, 1, :], in0=back[0:rows, u, 1, :], scalar=wk[1][0:rows, b],
                                                   in1=back[0:rows, u, 0, :], op0=ALU.mult, op1=ALU.add).then_inc(s_res, 1)
                with dve.Fori(0, (REAL - 1) // 4) as b_4:
                    b = b_4 * 4
                    for u in range(4):
                        stage(b, u)
                    for u in range(4):
                        mix(u, P, bass.ds(b + u, 1), b + (u + 1), 8 * b + 16 * TOP_K)
                dve.wait_ge(s_ofree, REAL)
                nc.vector.tensor_copy(placesk[:, 0, :], posk[:, REAL - 1, :]).then_inc(s_stage, 1)
                mix(0, LAST, slice(REAL - 1, REAL), REAL, (REAL - 1) // 4 * 16 * TOP_K + 16 * TOP_K)

            @block.sync
            def _(sp):
                sp.sem_inc(s_ofree, 4)
                with sp.Fori(0, (REAL - 1) // 4) as b_4:
                    b = b_4 * 4
                    for u in range(4):
                        sp.wait_ge(s_res, b + (u + 1))
                        sp.dma_start(out[bass.ds((b + u) * P, P), :], back[:, u, 1, :]).then_inc(s_out[u], 16)
                    for u in range(4):
                        sp.wait_ge(s_out[u], 4 * b + 16)
                        sp.sem_inc(s_ofree, 1)
                sp.wait_ge(s_res, REAL)
                sp.dma_start(out[(REAL - 1) * P:N, :], back[0:LAST, 0, 1, :]).then_inc(s_out[0], 16)
                sp.wait_ge(s_out[0], 16 * ((REAL - 1) // 4 + 1))


_INS = ["x", "src", "dst", "L0_gnn_W1", "L0_gnn_b1", "L0_gnn_W2", "L0_gnn_b2", "L0_gnn_wa1", "L0_gnn_ba1",
        "L0_gnn_wa2", "L0_gnn_ba2", "L0_ffn_Wg", "L0_ffn_bg", "L0_ffn_W1", "L0_ffn_b1", "L0_ffn_W2", "L0_ffn_b2"]


def kernel(**inputs):
    import numpy as _np
    import concourse.bacc as _bacc
    from concourse import mybir as _mybir
    from concourse.bass_utils import run_bass_kernel_spmd as _run

    nc = _bacc.Bacc("TRN2", target_bir_lowering=False, num_devices=1)
    arrays, args = {}, []
    for name in _INS:
        a = _np.ascontiguousarray(inputs[name])
        arrays[f"in_{name}_dram"] = a
        args.append(nc.dram_tensor(f"in_{name}_dram", a.shape, _mybir.dt.from_np(a.dtype), kind="ExternalInput").ap())
    shape = inputs["x"].shape
    out = nc.dram_tensor("out_dram", shape, _mybir.dt.float32, kind="ExternalOutput").ap()
    gnn_moe_kernel(nc, *args, out)
    r = _run(nc, [arrays], core_ids=[0])
    return r.results[0]["out_dram"]
```

```python
from contextlib import ExitStack

import concourse.bass as bass
from concourse import mybir

ALU = mybir.AluOpType
ACT = mybir.ActivationFunctionType
AX_X = mybir.AxisListType.X
F32 = mybir.dt.float32
F32R = mybir.dt.float32r
F16 = mybir.dt.float16
BF16 = mybir.dt.bfloat16
I32 = mybir.dt.int32
U16 = mybir.dt.uint16

P = 128
EPS = 1e-5
SLOPE = 0.2
TOP_K = 2
TURN = 10
BACKS = 8
FFN_ROWS = 256
RUN = 6
GROUP = 8
HOTS = 3
SORT_RUN = 2 * HOTS
BODY = 16
QUARTER = 4
QUARTERS = BODY // QUARTER
SLOTS_G = 8
LEAD = 4
SORTS_PER_BODY = 2
PERIOD = BODY // SORTS_PER_BODY


def ceil_div(a, b):
    return -(-a // b)


def gnn_moe_kernel(nc, x, src, dst, g_w1, g_b1, g_w2, g_b2, wa1, ba1, wa2, ba2,
                   w_gate, b_gate, f_w1, f_b1, f_w2, f_b2, out):
    N, D = x.shape
    (E,) = src.shape
    X, _, H = f_w1.shape
    KD, KH = D // P, H // P
    REAL = ceil_div(N, P)
    LAST = N - (REAL - 1) * P
    NB = ceil_div(REAL, 2) * 2
    EC = ceil_div(E, P)
    FULL = E // P
    CENTRE = 1 << 15
    TAIL = E - FULL * P
    COLS = ceil_div(EC, GROUP) * GROUP

    def tiles_for(cols):
        return (cols * P + REAL * (P - 1)) // P

    WA = 384
    WB = COLS - WA
    WB_REAL = EC - WA
    TA = ceil_div(tiles_for(WA), BODY) * BODY
    TB = ceil_div(tiles_for(WB_REAL), BODY) * BODY
    TMAX = max(TA, TB)
    SORT_BODIES = WB // GROUP // SORTS_PER_BODY
    assert WB % (GROUP * SORTS_PER_BODY) == 0 and SORT_BODIES < TA // BODY
    assert TMAX <= 512 and max(WA, WB) <= 512
    PARTS = ((0, WA, TA), (WA, WB, TB))
    FT = (TOP_K * N + X * (FFN_ROWS - 1)) // FFN_ROWS
    DEAD = 1 << 14
    ROW = D + 1

    table = nc.dram_tensor("table", (NB * P, ROW), F32).ap()
    xs = nc.dram_tensor("xs", (FT * FFN_ROWS, D), F32).ap()
    os = nc.dram_tensor("os", (FT * FFN_ROWS, D), F32).ap()

    with ExitStack() as ctx:
        def sb(name, shape, dt=F32):
            return ctx.enter_context(nc.sbuf_tensor(name, shape, dt))

        def sem(name):
            return ctx.enter_context(nc.semaphore(name))

        banks = [ctx.enter_context(nc.psum_tensor(f"bank{i}", [P, 512], F32)) for i in range(8)]

        acc = sb("acc", [P, NB, D])
        ident = sb("ident", [P, P])
        ones = sb("ones", [P, P])
        iota_1 = sb("iota_1", [P, P])
        iota_16 = sb("iota_16", [P, TMAX], F16)
        below = sb("below", [P, P])
        mean2 = sb("mean2", [P, NB])
        spread = sb("spread", [P, NB])
        rstd = sb("rstd", [P, NB])
        shift = sb("shift", [P, NB])
        row_f = sb("row_f", [P, TMAX])
        b1T = sb("b1T", [P, X * KH])
        b1raw = sb("b1raw", [X * KH, P])
        wg = sb("wg", [P, KD, X])
        bg = sb("bg", [P, X])
        logits = sb("logits", [P, NB, X])
        stats = logits[:, :, 0:6]
        top = sb("top", [P, TOP_K, NB])
        hit = sb("hit", [P, NB, X])
        lead = sb("lead", [P, NB, X])
        diff = sb("diff", [P, NB])
        wk = [sb(f"wk{k}", [P, NB]) for k in range(TOP_K)]
        idx = [sb(f"idx{k}", [P, NB]) for k in range(TOP_K)]
        eh = [sb(f"eh{k}", [P, X, NB]) for k in range(TOP_K)]
        ehs = sb("ehs", [P, X, NB])
        esc = sb("esc", [P, X, NB])
        valid = sb("valid", [P, NB])
        etot = sb("etot", [P, X])
        et = sb("et", [P, 6, X])
        eti = sb("eti", [P, X], I32)
        posk_f = sb("posk_f", [P, NB])
        posk = sb("posk", [P, NB, TOP_K], I32)
        placesk = sb("placesk", [P, 4, TOP_K], I32)
        ecmp = sb("ecmp", [P, FT, X])
        esum = sb("esum", [P, FT])
        expert = sb("expert", [P, FT], I32)
        fresh = sb("fresh", [P, FT], I32)

        edges = ctx.enter_context(ExitStack())

        def sbe(name, shape, dt=F32):
            return edges.enter_context(nc.sbuf_tensor(name, shape, dt))
        part = [dict(
            sender=sbe(f"sender{n}", [P, t + BODY], I32), receiver=sbe(f"receiver{n}", [P, t]),
            block=sbe(f"block{n}", [P, t], I32)) for n, (_, _, t) in enumerate(PARTS)]
        a1row = sbe("a1row", [P, NB, P])
        ring = sbe("ring", [P, BODY, ROW])
        gate = sbe("gate", [P, SLOTS_G, P])
        lhs = sbe("lhs", [P, SLOTS_G, P])
        places = sbe("places", [P, QUARTERS, QUARTER], I32)
        ringflat = ring[:, :, :].rearrange("p a b -> p (a b)")
        yn = ringflat[:, 0:8 * D].rearrange("p (a b) -> p a b", a=8)
        ynT = gate[:, 0:4, :]

        ARENA = 18448
        arena = sbe("arena", [P, ARENA])
        used = [0]

        def cut(shape, dt=F32, region=None):
            n = 1
            for m in shape:
                n *= m
            words = ceil_div(n * (2 if dt in (F16, BF16) else 4), 32) * 8
            if region is None:
                region, at = arena, used
            else:
                region, at = region
            a = region[:, at[0]:at[0] + words]
            at[0] += words
            a = (a if dt == F32 else a.bitcast(dt))[:, 0:n]
            if len(shape) == 2:
                a = a.rearrange("p (a b) -> p a b", a=shape[0])
            if len(shape) == 3:
                a = a.rearrange("p (a b c) -> p a b c", a=shape[0], b=shape[1])
            return a

        zeros = cut([4 * D])
        tmp_i = cut([COLS], I32)
        src_i = cut([COLS], I32)
        dst_i = cut([COLS], I32)
        block16 = cut([COLS], F16)
        v1_16 = cut([COLS], F16)
        v2_16 = cut([COLS], F16)
        v2_f = cut([COLS])
        posl_16 = cut([COLS], F16)
        post_f = cut([COLS])
        pos_f = cut([COLS])
        unit = cut([2 * P], F16)
        iota_m = cut([P, GROUP], F16)
        after_sort = used[0]
        sel = cut([NB, P], F16)
        below16 = cut([P], F16)
        mask = [cut([COLS], F16) for _ in range(2)]
        a1flat = a1row[:, :, :].rearrange("p b m -> p (b m)")
        count_f, scan_f, ones_row = (a1flat[:, n * COLS:(n + 1) * COLS] for n in range(3))
        carry_i, digit_i = (a1flat[:, n * COLS:(n + 1) * COLS].bitcast(I32) for n in (3, 4))
        carry = [cut([COLS], F16) for _ in range(2)]
        early = (a1flat, [5 * COLS])
        first_rows = cut([P], F16, early)
        after = cut([TMAX], F16, early)
        small = cut([16])
        small_i = cut([16], I32)
        wcat = cut([KD, 2 * D])
        bcat = cut([2 * D], F32, early)
        brest = cut([2 * D], F32, early)
        bias3 = cut([2 * D], BF16)
        bpart = cut([2 * D], BF16, early)
        ones16 = cut([P], BF16)
        wa = cut([2, D])
        ba = cut([2])
        xn = cut([2, D])
        xt = cut([2, KD, P])
        xij = cut([2, 2, ROW])
        junk = cut([2, 2, D])
        a1diag = cut([4, P])
        used[0] = after_sort
        hot = [cut([P, GROUP], F16) for _ in range(HOTS)]
        hot1 = [cut([P, GROUP], F16) for _ in range(HOTS)]
        hot2 = [cut([P, GROUP], F16) for _ in range(HOTS)]
        tile_hot = [cut([GROUP, TMAX], F16) for _ in range(2)]
        out_v1 = cut([TMAX])
        out_v2 = cut([TMAX], I32)
        out_hi = cut([TMAX], I32)
        def chain(eng, name):
            s, n = sem(name), [0]

            def link(ins):
                n[0] += 1
                ins.then_inc(s, 1)
                eng.wait_ge(s, n[0])
            return link


        def flat(ap):
            return ap.rearrange("p a b -> p (a b)")

        s_dummy = sem("carries_pool_waits")
        s_dve = sem("carries_dve_waits")
        s_pe = sem("carries_pe_waits")

        s_const = sem("constants_ready")
        s_iota = sem("tables_ready")
        s_x = [sem(f"x_loaded{n}") for n in range(NB // TURN)]
        s_w = sem("weights_loaded")
        s_e = sem("edges_loaded")

        def set_constants(dve):
            nc.vector.memset(src_i[:, FULL:COLS], DEAD)
            nc.vector.memset(dst_i[:, FULL:COLS], 0)
            nc.vector.memset(acc[:, REAL - 1:NB, :], 0.0)
            nc.vector.memset(zeros, 0.0)
            nc.vector.memset(unit, 0.0).then_inc(s_const, 1)
            dve.wait_ge(s_const, 1)
            nc.vector.memset(ones[:, :], 1.0)
            nc.vector.memset(ones_row, 1.0)
            nc.vector.memset(ones16, 1.0)
            nc.vector.memset(bias3, 0.0)
            nc.vector.memset(pos_f, -1.0 - CENTRE)
            nc.vector.memset(unit[:, P:P + 1], 1.0).then_inc(s_const, 1)

        def load_nodes(sp):
            sp.wait_ge(s_const, 1)
            for dram, tile in ((src, src_i), (dst, dst_i)):
                sp.dma_start(tile[:, 0:FULL], dram[0:FULL * P].rearrange("(p j) -> p j", p=P)).then_inc(s_e, 16)
                sp.dma_start(tile[0:TAIL, FULL:FULL + 1],
                             dram[FULL * P:E].rearrange("(p j) -> p j", j=1)).then_inc(s_e, 16)
            for n in range(NB // TURN):
                a, b = n * TURN, min((n + 1) * TURN, REAL - 1)
                sp.dma_start(acc[:, a:b, :], x[a * P:b * P, :].rearrange("(b p) d -> p b d", p=P)).then_inc(s_x[n], 16)
            sp.dma_start(acc[0:LAST, REAL - 1, :], x[(REAL - 1) * P:N, :]).then_inc(s_x[-1], 16)

        def load_weights(act):
            for n, (w, b, wv, bv) in enumerate(((g_w2, g_b2, wa2, ba2), (g_w1, g_b1, wa1, ba1))):
                act.dma_start(wcat[:, :, n * D:(n + 1) * D], w.rearrange("(k p) n -> p k n", p=P)).then_inc(s_w, 16)
                act.dma_start(bcat[:, n * D:(n + 1) * D], b.partition_broadcast(P)).then_inc(s_w, 16)
                act.dma_start(wa[:, n, :], wv.partition_broadcast(P)).then_inc(s_w, 16)
                act.dma_start(ba[:, n:n + 1], bv.partition_broadcast(P)).then_inc(s_w, 16)
            act.dma_start(wg[:, :, :], w_gate.rearrange("(k p) e -> p k e", p=P)).then_inc(s_w, 16)
            act.dma_start(bg[:, :], b_gate.partition_broadcast(P)).then_inc(s_w, 16)
            act.dma_start(b1raw[:, :], f_b1.rearrange("e (k p) -> (e k) p", p=P)).then_inc(s_w, 16)

        def set_tables(pool):
            numbers = carry_i
            nc.gpsimd.iota(numbers, [[1, COLS]], base=0, channel_multiplier=0).then_inc(s_iota, 1)
            pool.wait_ge(s_iota, 1)
            nc.gpsimd.tensor_copy(row_f[:, :], numbers[:, 0:TMAX])
            nc.gpsimd.tensor_copy(iota_16[:, :], numbers[:, 0:TMAX]).then_inc(s_iota, 1)
            for n, (_, _, t) in enumerate(PARTS):
                nc.gpsimd.memset(part[n]["sender"][:, t:t + BODY], 0)
            for tile in (first_rows, below[:, :], below16, ident[:, :], valid[:, :]):
                nc.gpsimd.memset(tile, 1.0)
            nc.gpsimd.memset(sel, 1.0).then_inc(s_iota, 1)
            pool.wait_ge(s_iota, 3)
            nc.gpsimd.affine_select(out=first_rows, in_=first_rows, pattern=[[0, P]], base=REAL - 1,
                                    channel_multiplier=-1, compare_op=ALU.is_gt, fill=0.0)
            for tile in (below[:, :], below16):
                nc.gpsimd.affine_select(out=tile, in_=tile, pattern=[[1, P]], base=0,
                                        channel_multiplier=-1, compare_op=ALU.is_gt, fill=0.0)
            nc.gpsimd.affine_select(out=ident[:, :], in_=ident[:, :], pattern=[[-1, P]], base=0,
                                    channel_multiplier=1, compare_op=ALU.is_equal, fill=0.0)
            nc.gpsimd.affine_select(out=valid[:, :], in_=valid[:, :], pattern=[[-P, NB]], base=N,
                                    channel_multiplier=-1, compare_op=ALU.is_gt, fill=0.0)
            nc.gpsimd.affine_select(out=sel, in_=sel, pattern=[[-1, NB], [0, P]], base=0, channel_multiplier=1,
                                    compare_op=ALU.is_equal, fill=0.0)
            nc.gpsimd.tensor_copy(iota_m, numbers[:, 0:P].unsqueeze(2).to_broadcast([P, P, GROUP]))
            nc.gpsimd.tensor_copy(iota_1[:, :], numbers[:, 1:P + 1]).then_inc(s_iota, 1)

        s_mask = sem("mask_ready")
        s_counted = sem("mask_counted")
        s_cnt = sem("counts_ready")
        s_tiles = sem("tiles_ready")
        s_base = sem("bases_ready")
        s_cmp = sem("ends_compared")
        s_blk = sem("tile_blocks_ready")
        s_carry = sem("carries_ready")
        s_rank = sem("ranks_ready")
        s_ranked = sem("ranks_taken")
        s_bn = sem("moments_taken")
        s_var = sem("variance_ready")
        s_sd = sem("deviation_ready")
        s_xn = sem("xn_ready")
        s_acc = sem("xn_added")
        s_xnT = sem("xn_transposed")
        s_xt = sem("xt_ready")
        s_lin = sem("linear_ready")
        s_xij = sem("table_row_ready")
        s_dot = sem("table_rows_stored")
        s_tab = [sem(f"table_stored{u}") for u in range(2)]
        s_leaky = sem("leaky_and_dots")
        s_fifth = sem("fifth_ready")
        s_a1r = sem("a1_row_copied")
        s_a1b = sem("a1_broadcast")
        s_xs0 = sem("xs_zeroed")
        s_scaled = sem("scale_and_shift_ready")
        RANK_CUTS = ((0, WA), (WA, COLS))

        def moments(dve, link, done):
            def some(i):
                for u in range(TURN):
                    b = bass.ds(i * TURN + u, 1)
                    nc.vector.bn_stats(flat(stats[:, b, :]), flat(acc[:, b, :])).then_inc(s_bn, 1)
            if done:
                with dve.Fori(0, NB // TURN) as i:
                    some(i)
            else:
                for i in range(NB // TURN):
                    dve.wait_ge(s_x[i], 32 if i == NB // TURN - 1 else 16)
                    some(i)
            dve.wait_ge(s_bn, NB * (done + 1))
            nc.vector.tensor_tensor(mean2[:, :], stats[:, :, 1], stats[:, :, 4], ALU.add)
            nc.vector.tensor_tensor(rstd[:, :], stats[:, :, 2], stats[:, :, 5], ALU.add)
            link(nc.vector.tensor_tensor(spread[:, :], stats[:, :, 1], stats[:, :, 4], ALU.subtract))
            link(nc.vector.scalar_tensor_tensor(out=spread[:, :], in0=spread[:, :], scalar=0.25, in1=spread[:, :],
                                                op0=ALU.mult, op1=ALU.mult))
            link(nc.vector.scalar_tensor_tensor(out=rstd[:, :], in0=rstd[:, :], scalar=1.0 / D, in1=spread[:, :],
                                                op0=ALU.mult, op1=ALU.add))
            nc.vector.tensor_scalar(rstd[:, :], rstd[:, :], EPS, None, ALU.add).then_inc(s_var, 1)
            dve.wait_ge(s_sd, done + 1)
            link(nc.vector.reciprocal(rstd[:, :], rstd[:, :]))
            nc.vector.scalar_tensor_tensor(out=shift[:, :], in0=mean2[:, :], scalar=-0.5, in1=rstd[:, :],
                                           op0=ALU.mult, op1=ALU.mult).then_inc(s_scaled, 1)
            dve.wait_ge(s_scaled, done + 1)

        with nc.Block() as block:
            @block.gpsimd
            def _(pool):
                set_tables(pool)
                pool.sem_inc(s_acc, 2)
                with pool.Fori(0, NB // 2) as b_2:
                    b = b_2 * 2
                    for u in range(2):
                        pool.wait_ge(s_xn, b + (u + 1))
                        a = acc[:, bass.ds(b + u, 1), :].rearrange("p b d -> p (b d)")
                        nc.gpsimd.tensor_tensor(a, a, xn[:, u, :], ALU.add).then_inc(s_acc, 1)

            @block.vector
            def _(dve):
                link = chain(dve, "dve_keys")
                set_constants(dve)
                bits = nc.vector.tensor_scalar
                dve.sem_inc(s_ranked, 2)
                dve.sem_inc(s_xij, 2)
                dve.wait_ge(s_e, 64)
                link(bits(tmp_i, src_i, 7, None, ALU.arith_shift_right))
                link(nc.vector.tensor_copy(block16, tmp_i))
                link(bits(tmp_i, dst_i, 3, None, ALU.arith_shift_right))
                link(nc.vector.tensor_scalar(v1_16, tmp_i, 1.0, None, ALU.add))
                link(bits(src_i, src_i, P - 1, None, ALU.bitwise_and))
                link(bits(dst_i, dst_i, 7, 7, ALU.bitwise_and, ALU.arith_shift_left))
                link(nc.vector.tensor_tensor(v2_f, src_i, dst_i, ALU.add))
                link(nc.vector.tensor_copy(v2_16, v2_f))

                def make_mask(b, slot):
                    nc.vector.tensor_scalar(mask[slot], block16, b, None, ALU.is_equal).then_inc(s_mask, 1)

                dve.wait_ge(s_iota, 2)
                with dve.Fori(0, NB // TURN) as i:
                    for u in range(TURN):
                        dve.wait_ge(s_counted, i * TURN + (u + 1))
                        make_mask(row_f[:, bass.ds(i * TURN + u, 1)], u % 2)
                dve.wait_ge(s_w, 176)
                for row in (0, 32, 64):
                    src_of = bcat if row == 0 else brest
                    link(nc.vector.tensor_copy(bpart, src_of))
                    link(nc.vector.tensor_copy(bias3[row:row + 1, :], src_of[row:row + 1, :]))
                    link(nc.vector.tensor_tensor(brest, src_of, bpart, ALU.subtract))

                moments(dve, link, 0)
                dve.wait_ge(s_cnt, 1)
                nc.vector.tensor_copy(count_f[:, WA:COLS], banks[1][:, 0:WB])
                link(nc.vector.tensor_copy(count_f[:, 0:WA], banks[0][:, 0:WA]))
                for n, (c0, w, t) in enumerate(PARTS):
                    link(nc.vector.tensor_tensor_scan(out=scan_f[:, c0:c0 + w], data0=ones_row[:, 0:w],
                                                      data1=count_f[:, c0:c0 + w], initial=0.0,
                                                      op0=ALU.mult, op1=ALU.add))
                    link(nc.vector.tensor_scalar(small_i[:, n:n + 1], scan_f[:, c0 + w - 1:c0 + w], float(P - 1), None, ALU.add))
                    link(bits(small_i[:, n:n + 1], small_i[:, n:n + 1], 7, None, ALU.arith_shift_right))
                    link(nc.vector.tensor_copy(small[:, n:n + 1], small_i[:, n:n + 1]))
                nc.vector.memset(small[:, 15:16], 0.0).then_inc(s_tiles, 1)
                link(nc.vector.tensor_tensor(scan_f, scan_f, count_f, ALU.subtract))
                dve.wait_ge(s_base, 1)
                link(nc.vector.tensor_copy(small[:, 2:4], banks[2][:, 0:2]))
                link(nc.vector.tensor_tensor(small[:, 4:6], small[:, 2:4], small[:, 0:2], ALU.add))
                link(nc.vector.tensor_scalar(small[:, 6:8], small[:, 2:4], float(P), None, ALU.mult))
                for n, (c0, w, t) in enumerate(PARTS):
                    link(nc.vector.tensor_scalar(carry_i[:, c0:c0 + w], scan_f[:, c0:c0 + w], small[:, 6 + n:7 + n],
                                                 None, ALU.add))
                link(bits(digit_i, carry_i, 2047, None, ALU.bitwise_and))
                link(nc.vector.tensor_copy(carry[0], digit_i))
                link(nc.vector.scalar_tensor_tensor(out=carry[1], in0=carry_i, scalar=-float(CENTRE), in1=digit_i,
                                                    op0=ALU.add, op1=ALU.subtract))
                nc.vector.memset(small[:, 14:15], 0.0).then_inc(s_carry, 1)
                for n, (c0, w, t) in enumerate(PARTS):
                    nc.vector.tensor_scalar(after[:, 0:t], row_f[:, 0:t], small[:, 4 + n:5 + n], None,
                                            ALU.is_ge).then_inc(s_cmp, 1)
                    dve.wait_ge(s_blk, n + 1)
                    link(nc.vector.tensor_copy(part[n]["block"][:, :], banks[2][:, 0:t]))

                def take(k, slot):
                    dve.wait_ge(s_rank, k)
                    dve.wait_ge(s_mask, k + NB)
                    dve.sem_inc(s_dve, 1)
                    for c, (a, z) in enumerate(RANK_CUTS):
                        last = nc.vector.copy_predicated(pos_f[:, a:z], mask[slot][:, a:z].bitcast(U16),
                                                         banks[2 + 2 * slot + c][:, 0:z - a])
                    last.then_inc(s_ranked, 1)
                    dve.wait_ge(s_ranked, k + 2)

                def rows(b, u):
                    dve.wait_ge(s_fifth, b + (u + 1))
                    dve.wait_ge(s_dot, b + (u + 1))
                    o = banks[u][:, :].rearrange("p (s d) -> p s d", s=2)
                    nc.vector.tensor_tensor(xij[:, u, :, 0:D], o, junk[:, u, :, :], ALU.max).then_inc(s_leaky, 1)
                    dve.wait_ge(s_leaky, b * 2 + (2 * u + 1))
                    for side in range(2):
                        last = nc.vector.tensor_tensor_reduce(out=junk[:, u, side, :], in0=xij[:, u, side, 0:D],
                                                              in1=wa[:, side, :], scale=1.0, scalar=ba[:, side:side + 1],
                                                              op0=ALU.mult, op1=ALU.add, accum_out=xij[:, u, side, D:ROW])
                    last.then_inc(s_leaky, 1)
                    dve.wait_ge(s_leaky, b * 2 + (2 * u + 2))
                    dve.wait_ge(s_a1b, b + (u + 1))
                    nc.vector.tensor_scalar(a1diag[:, u, :], ident[:, :], xij[:, u, 1, D:ROW], None,
                                            ALU.mult).then_inc(s_xij, 1)

                def turn(b, last=False):
                    for u in range(2):
                        take(b + (u + 1), u)
                        if not last:
                            make_mask(row_f[:, bass.ds(b + (u + 2), 1)], u)
                    for u in range(2):
                        rows(b, u)

                for u in range(2):
                    make_mask(row_f[:, u:u + 1], u)
                with dve.Fori(0, NB // 2 - 1) as b_2:
                    turn(b_2 * 2)
                turn(NB - 2, last=True)
                link(nc.vector.tensor_scalar(tmp_i, pos_f, float(CENTRE), None, ALU.add))
                link(bits(src_i, tmp_i, P - 1, None, ALU.bitwise_and))
                link(bits(dst_i, tmp_i, 7, None, ALU.arith_shift_right))
                link(nc.vector.tensor_copy(posl_16, src_i))
                link(nc.vector.tensor_copy(post_f, dst_i))

            @block.scalar
            def _(act):
                load_weights(act)
                act.sem_inc(s_xt, 2)
                act.sem_inc(s_a1r, 1)
                act.wait_ge(s_var, 1)
                nc.scalar.activation(rstd[:, :], rstd[:, :], ACT.Sqrt).then_inc(s_sd, 1)
                act.wait_ge(s_scaled, 1)

                def normalize(b, u):
                    act.wait_ge(s_acc, b + (u + 1))
                    act.wait_ge(s_xnT, b + (u + 1))
                    nc.scalar.activation(xn[:, u, :], flat(acc[:, bass.ds(b + u, 1), :]), ACT.Identity,
                                         scale=rstd[:, bass.ds(b + u, 1)], bias=shift[:, bass.ds(b + u, 1)]).then_inc(s_xn, 1)

                def copy_xt(b, u):
                    act.wait_ge(s_xnT, b + (u + 3))
                    nc.scalar.copy(xt[:, u, :, :], banks[6][:, u * D:(u + 1) * D].rearrange("p (k m) -> p k m", k=KD)
                                   ).then_inc(s_xt, 1)

                def fifth(b, u):
                    act.wait_ge(s_lin, b + (u + 1))
                    act.wait_ge(s_xij, b + (u + 1))
                    nc.scalar.mul(junk[:, u, :, :], banks[u][:, :].rearrange("p (s d) -> p s d", s=2), SLOPE).then_inc(s_fifth, 1)

                def copy_a1(b, u):
                    act.wait_ge(s_a1b, b + (u + 3))
                    nc.scalar.copy(flat(a1row[:, bass.ds(b + u, 1), :]), banks[7][:, 0:P]).then_inc(s_a1r, 1)

                def turn(b, first=False, last=False):
                    for u in range(2):
                        if not last:
                            normalize(b + 2, u)
                    for u in range(2):
                        fifth(b, u)
                        if not last:
                            copy_xt(b + 2, u)
                        if not first:
                            copy_a1(b - 2, u)
                for u in range(2):
                    normalize(0, u)
                for u in range(2):
                    copy_xt(0, u)
                turn(0, first=True)
                with act.Fori(0, (NB - 4) // 2) as b_2:
                    turn(b_2 * 2 + 2)
                turn(NB - 2, last=True)
                for u in range(2):
                    copy_a1(NB - 2, u)

            @block.tensor
            def _(pe):
                pe.sem_inc(s_counted, 2)
                pe.sem_inc(s_xnT, 2)
                pe.sem_inc(s_a1b, 2)
                pe.wait_ge(s_const, 2)
                pe.wait_ge(s_iota, 2)
                for c, (a, z) in enumerate(RANK_CUTS):
                    nc.tensor.matmul(banks[c][:, 0:z - a], unit[:, 0:P], iota_16[:, 0:z - a], start=True, stop=False)
                with pe.Fori(0, NB // TURN) as i:
                    for u in range(TURN):
                        pe.wait_ge(s_mask, i * TURN + (u + 1))
                        pe.sem_inc(s_pe, 1)
                        for c, (a, z) in enumerate(RANK_CUTS):
                            mm = nc.tensor.matmul(banks[c][:, 0:z - a], unit[:, bass.ds(P - u - i * TURN, P)], mask[u % 2][:, a:z],
                                                  start=False, stop=False)
                        mm.then_inc(s_counted, 1)
                for c, (a, z) in enumerate(RANK_CUTS):
                    mm = nc.tensor.matmul(banks[c][:, 0:z - a], unit[:, 0:P], iota_16[:, 0:z - a], start=False, stop=True)
                mm.then_inc(s_cnt, 1)
                pe.wait_ge(s_tiles, 1)
                pe.wait_ge(s_iota, 4)
                nc.tensor.matmul(banks[2][:, 0:2], below[:, :], small[:, 0:2], start=True, stop=True).then_inc(s_base, 1)
                pe.wait_ge(s_carry, 1)
                for n, (c0, w, t) in enumerate(PARTS):
                    pe.wait_ge(s_cmp, n + 1)
                    nc.tensor.matmul(banks[2][:, 0:t], first_rows, after[:, 0:t], start=True, stop=True).then_inc(s_blk, 1)

                def ranks(b, u):
                    pe.wait_ge(s_mask, b + (NB + u + 1))
                    pe.wait_ge(s_ranked, b + (u + 1))
                    for c, (a, z) in enumerate(RANK_CUTS):
                        o = banks[2 + 2 * u + c][:, 0:z - a]
                        nc.tensor.matmul(o, below16, mask[u][:, a:z], start=True, stop=False)
                        for d in range(2):
                            mm = nc.tensor.matmul(o, flat(sel[:, bass.ds(b + u, 1), :]), carry[d][:, a:z],
                                                  start=False, stop=(d == 1))
                    mm.then_inc(s_rank, 1)

                def transposes(b, u):
                    pe.wait_ge(s_xn, b + (u + 1))
                    pe.wait_ge(s_xt, b + (u + 2))
                    for k in range(KD):
                        mm = nc.tensor.transpose(banks[6][:, u * D + k * P:u * D + (k + 1) * P],
                                                 xn[:, u, k * P:(k + 1) * P], ident[:, :])
                    mm.then_inc(s_xnT, 1)

                def linears(b, u):
                    pe.wait_ge(s_xt, b + (u + 3))
                    pe.wait_ge(s_xij, b + (u + 1))
                    for k in range(KD):
                        nc.tensor.matmul(banks[u][:, :], xt[:, u, k, :], wcat[:, k, :], start=(k == 0), stop=False)
                    nc.tensor.matmul(banks[u][:, :], ones16[0:96, :], bias3[0:96, :], start=False, stop=True).then_inc(s_lin, 1)

                def spread_a1(b, u):
                    pe.wait_ge(s_xij, b + (u + 3))
                    pe.wait_ge(s_a1r, b + (u + 1))
                    nc.tensor.matmul(banks[7][:, 0:P], ones[:, :], a1diag[:, u, :], start=True, stop=True).then_inc(s_a1b, 1)

                def turn(b, first=False, last=False):
                    for u in range(2):
                        ranks(b, u)
                    for u in range(2):
                        linears(b, u)
                        if not last:
                            transposes(b + 2, u)
                        if not first:
                            spread_a1(b - 2, u)
                for u in range(2):
                    transposes(0, u)
                turn(0, first=True)
                with pe.Fori(0, (NB - 4) // 2) as b_2:
                    turn(b_2 * 2 + 2)
                turn(NB - 2, last=True)
                for u in range(2):
                    spread_a1(NB - 2, u)

            @block.sync
            def _(sp):
                load_nodes(sp)
                sp.sem_inc(s_dot, 2)
                with sp.Fori(0, NB // 2) as b_2:
                    b = b_2 * 2
                    for u in range(2):
                        sp.wait_ge(s_xij, b + (u + 3))
                        sp.dma_start(table[bass.ds((b + u) * P, P), :], xij[:, u, 0, :]).then_inc(s_tab[u], 16)
                    for u in range(2):
                        sp.wait_ge(s_tab[u], 8 * b + 16)
                        sp.sem_inc(s_dot, 1)

        s_hot = sem("one_hots_ready")
        s_lone = sem("plain_one_hot_ready")
        s_hot1 = sem("first_number_ready")
        s_hot2 = sem("second_number_ready")
        s_moved = sem("one_hots_used")
        s_sorted = sem("sorted")
        s_decoded = sem("edges_decoded")
        SORT_BANKS = ((0, 1), (2, 4))

        def rep(a, cols):
            return a[:, bass.ds(cols, GROUP)].unsqueeze(1).to_broadcast([P, P, GROUP])

        def rows_hot(cols, slot):
            nc.vector.tensor_tensor(hot[slot], iota_m, rep(posl_16, cols), ALU.is_equal).then_inc(s_lone, 1)

        def column_hot(n, cols, slot, c):
            t = PARTS[n][2]
            last = nc.vector.tensor_scalar(tile_hot[slot][:, c, 0:t], iota_16[:, 0:t], post_f[:, bass.ds(cols + c, 1)],
                                           None, ALU.is_equal)
            if c == GROUP - 1:
                last.then_inc(s_hot, 1)

        def second_sort(dve, g, slot, step):
            at = g + (PARTS[0][1] // GROUP + 1)
            cols = g * GROUP + PARTS[1][0]
            if step == 0:
                dve.wait_ge(s_moved, at)
                rows_hot(cols, slot)
            if step == 3:
                dve.wait_ge(s_lone, at)
                nc.vector.tensor_tensor(hot1[slot], hot[slot], rep(v1_16, cols), ALU.mult)
            if step == 5:
                nc.vector.tensor_tensor(hot2[slot], hot[slot], rep(v2_16, cols), ALU.mult)
            column_hot(1, cols, slot, step)

        GROUPS_A = WA // GROUP

        def each_group(eng, step):
            count = (GROUPS_A - 1) // SORT_RUN
            with eng.Fori(0, count) as i:
                for j in range(SORT_RUN):
                    step(i * SORT_RUN, j)
            for j in range(GROUPS_A - count * SORT_RUN):
                step(count * SORT_RUN, j)

        def first_number(pool, g, j):
            slot = j % HOTS
            pool.wait_ge(s_lone, g + (j + 1))
            nc.gpsimd.tensor_tensor(hot1[slot], hot[slot], rep(v1_16, g * GROUP + j * GROUP), ALU.mult).then_inc(s_hot1, 1)

        def second_number(act, g, j):
            slot = j % HOTS
            act.wait_ge(s_lone, g + (j + 1))
            for c in range(GROUP):
                last = nc.scalar.activation(hot2[slot][:, :, c], hot[slot][:, :, c], ACT.Copy,
                                            scale=v2_f[:, bass.ds(g * GROUP + (j * GROUP + c), 1)])
            last.then_inc(s_hot2, 1)

        def move(pe, n, g, slot, tile_slot, cs=range(GROUP)):
            t = PARTS[n][2]
            done = PARTS[0][1] // GROUP if n else 0
            if cs[0] == 0:
                pe.wait_ge(s_hot, g + (done + 1))
                if n == 0:
                    pe.wait_ge(s_hot1, g + 1)
                    pe.wait_ge(s_hot2, g + 1)
            for c in cs:
                for v, h in enumerate((hot1, hot2)):
                    mm = nc.tensor.matmul(banks[SORT_BANKS[n][v]][:, 0:t], h[slot][:, :, c],
                                          tile_hot[tile_slot][:, c, 0:t], start=False, stop=False)
            if cs[-1] == GROUP - 1:
                mm.then_inc(s_moved, 1)

        def open_or_close(n, first):
            for v in range(2):
                t = PARTS[n][2]
                mm = nc.tensor.matmul(banks[SORT_BANKS[n][v]][:, 0:t], unit[:, 0:P], iota_16[:, 0:t],
                                      start=first, stop=not first)
            if not first:
                mm.then_inc(s_sorted, 1)

        def decode(dve, link, n):
            dve.wait_ge(s_sorted, n + 1)
            t = PARTS[n][2]
            link(nc.vector.tensor_copy(out_v1[:, 0:t], banks[SORT_BANKS[n][0]][:, 0:t]))
            link(nc.vector.tensor_copy(out_v2[:, 0:t], banks[SORT_BANKS[n][1]][:, 0:t]))
            link(nc.vector.tensor_scalar(out_hi[:, 0:t], out_v2[:, 0:t], 7, None, ALU.arith_shift_right))
            link(nc.vector.tensor_scalar(out_v2[:, 0:t], out_v2[:, 0:t], P - 1, None, ALU.bitwise_and))
            link(nc.vector.scalar_tensor_tensor(out=part[n]["receiver"][:, :], in0=out_v1[:, 0:t], scalar=1.0,
                                                in1=out_v2[:, 0:t], op0=ALU.min, op1=ALU.add))
            link(nc.vector.tensor_scalar(out_v1[:, 0:t], out_v1[:, 0:t], -1.0, 0.0, ALU.add, ALU.max))
            nc.vector.scalar_tensor_tensor(out=part[n]["sender"][:, 0:t], in0=out_v1[:, 0:t], scalar=8.0,
                                           in1=out_hi[:, 0:t], op0=ALU.mult, op1=ALU.add).then_inc(s_decoded, 1)
            dve.wait_ge(s_decoded, n + 1)

        s_place = sem("places_staged")
        s_row = [sem(f"rows_gathered{q}") for q in range(QUARTERS)]
        s_gate = sem("gates_ready")
        s_lhs = sem("gated_one_hots_ready")
        s_sum = sem("tile_sums_ready")
        s_add = sem("tile_sums_added")

        sums = [banks[n] for n in (0, 1, 6, 7)]

        def loaded(eng, regs, n, t0):
            eng.load(regs, part[n]["block"][0:1, bass.ds(t0, QUARTER)])
            return [eng.snap(reg, min_val=0, max_val=NB - 1) for reg in regs]

        def gather(pool, i, done):
            for q in range(QUARTERS):
                pool.wait_ge(s_sum, i * BODY + (q * QUARTER + done + QUARTER))
                pool.wait_ge(s_place, i * QUARTERS + (q + done // QUARTER + 1))
                pool.sem_inc(s_dummy, 1)
                for u in range(QUARTER):
                    pool.indirect_dma_start(out=ring[:, q * QUARTER + u, :], out_offset=None, in_=table[:, :],
                                            in_offset=bass.IndirectOffsetOnAxis(ap=places[:, q, u:u + 1], axis=0)
                                            ).then_inc(s_row[q], 16)

        def stage_places(n, q, t0):
            nc.scalar.copy(places[:, q, :], part[n]["sender"][:, bass.ds(t0, QUARTER)]).then_inc(s_place, 1)

        def gates(act, regs, n, i, done, last=False):
            for q in range(QUARTERS):
                t0 = i * BODY + q * QUARTER
                blocks = loaded(act, regs, n, t0)
                act.wait_ge(s_row[q], i * (16 * QUARTER) + (16 * QUARTER * (done // BODY + 1)))
                for u in range(QUARTER):
                    act.wait_ge(s_lhs, t0 + (done + u + 1))
                    nc.scalar.activation(gate[:, (q * QUARTER + u) % SLOTS_G, :], flat(a1row[:, bass.ds(blocks[u], 1), :]),
                                         ACT.Sigmoid, bias=ring[:, q * QUARTER + u, D:ROW]).then_inc(s_gate, 1)
                stage_places(*((1, q, q * QUARTER) if last else (n, q, t0 + BODY)))

        def gated(dve, n, t, j, done):
            dve.wait_ge(s_gate, t + (done + j + 1))
            dve.wait_ge(s_sum, t + (done + j + 1 + BODY - SLOTS_G))
            nc.vector.scalar_tensor_tensor(out=lhs[:, j % SLOTS_G, :], in0=iota_1[:, :],
                                           scalar=part[n]["receiver"][:, bass.ds(t + j, 1)], in1=gate[:, j % SLOTS_G, :],
                                           op0=ALU.is_equal, op1=ALU.mult).then_inc(s_lhs, 1)

        def lhs_and_add(dve, regs, n, i, done, between=None, last=False):
            t = i * BODY
            for j in range(BODY):
                u = j % QUARTER
                if u == 0:
                    blocks = loaded(dve, regs, n, t + j)
                if not last or j + LEAD < BODY:
                    gated(dve, n, t, j + LEAD, done)
                dve.wait_ge(s_sum, t + (done + j + 1 + BODY))
                dve.wait_ge(s_add, t + (done + j + 4))
                a = flat(acc[:, bass.ds(blocks[u], 1), :])
                nc.vector.tensor_tensor(a, a, sums[u][:, 0:D], ALU.add).then_inc(s_add, 1)
                if between:
                    between(j)

        def tile_sums(pe, i, done, between=None):
            for q in range(QUARTERS):
                t0 = i * BODY + q * QUARTER
                for u in range(QUARTER):
                    pe.wait_ge(s_lhs, t0 + (done + u + SLOTS_G + 1))
                    pe.wait_ge(s_add, t0 + (done + u + 1))
                    nc.tensor.matmul(sums[u][:, 0:D], lhs[:, (q * QUARTER + u) % SLOTS_G, :], ring[:, q * QUARTER + u, 0:D],
                                     start=True, stop=True).then_inc(s_sum, 1)
                    if between:
                        between(q * QUARTER + u)

        assert PERIOD == GROUP

        BODIES_A, BODIES_B = TA // BODY, TB // BODY

        with nc.Block() as block:
            @block.sync
            def _(sp):
                per = FT * FFN_ROWS // P * D // (4 * D)
                sp.dma_start(xs.rearrange("(p a r) d -> p a (r d)", p=P, a=per),
                             zeros.unsqueeze(1).to_broadcast([P, per, 4 * D])).then_inc(s_xs0, 16)
                sp.wait_ge(s_xs0, 16)

            @block.gpsimd
            def _(pool):
                each_group(pool, lambda g, j: first_number(pool, g, j))
                with pool.Fori(0, BODIES_A) as i:
                    gather(pool, i, 0)
                with pool.Fori(0, BODIES_B) as i:
                    gather(pool, i, TA)

            @block.scalar
            def _(act):
                each_group(act, lambda g, j: second_number(act, g, j))
                regs = [act.alloc_register(f"act_block{u}") for u in range(QUARTER)]
                act.wait_ge(s_decoded, 1)
                for q in range(QUARTERS):
                    stage_places(0, q, q * QUARTER)
                with act.Fori(0, BODIES_A - 1) as i:
                    gates(act, regs, 0, i, 0)
                act.wait_ge(s_decoded, 2)
                gates(act, regs, 0, BODIES_A - 1, 0, last=True)
                with act.Fori(0, BODIES_B) as i:
                    gates(act, regs, 1, i, TA)

            @block.vector
            def _(dve):
                link = chain(dve, "dve_decode")

                def group(g, j):
                    dve.wait_ge(s_moved, g + (j + 1))
                    if not (isinstance(g, int) and g + j + 1 == GROUPS_A):
                        rows_hot(g * GROUP + (j + 1) * GROUP, (j + 1) % HOTS)
                    for c in range(GROUP):
                        column_hot(0, g * GROUP + j * GROUP, j % 2, c)
                rows_hot(0, 0)
                each_group(dve, group)
                decode(dve, link, 0)

                regs = [dve.alloc_register(f"dve_block{u}") for u in range(QUARTER)]
                dve.sem_inc(s_lhs, SLOTS_G)
                dve.sem_inc(s_add, 4)
                for step in range(GROUP):
                    second_sort(dve, 0, 0, step)
                for j in range(LEAD):
                    gated(dve, 0, 0, j, 0)

                def sort_body(i, last=False):
                    def step(j):
                        group = j // PERIOD + 1
                        if not (last and group == SORTS_PER_BODY):
                            second_sort(dve, i * SORTS_PER_BODY + group, group % 2, j % PERIOD)
                    lhs_and_add(dve, regs, 0, i, 0, step)
                with dve.Fori(0, SORT_BODIES - 1) as i:
                    sort_body(i)
                sort_body(SORT_BODIES - 1, last=True)
                decode(dve, link, 1)
                with dve.Fori(SORT_BODIES, BODIES_A - 1) as i:
                    lhs_and_add(dve, regs, 0, i, 0)
                lhs_and_add(dve, regs, 0, BODIES_A - 1, 0, last=True)
                for j in range(LEAD):
                    gated(dve, 1, 0, j, TA)
                with dve.Fori(0, BODIES_B - 1) as i:
                    lhs_and_add(dve, regs, 1, i, TA)
                lhs_and_add(dve, regs, 1, BODIES_B - 1, TA, last=True)

            @block.tensor
            def _(pe):
                pe.sem_inc(s_moved, 2)
                pe.sem_inc(s_sum, BODY)
                open_or_close(0, True)
                each_group(pe, lambda g, j: move(pe, 0, g + j, j % HOTS, j % 2))
                open_or_close(0, False)
                open_or_close(1, True)
                with pe.Fori(0, SORT_BODIES) as i:
                    tile_sums(pe, i, 0, lambda j: move(pe, 1, i * SORTS_PER_BODY + j // PERIOD, j // PERIOD % 2,
                                                       j // PERIOD % 2, (j % PERIOD,)))
                open_or_close(1, False)
                with pe.Fori(SORT_BODIES, BODIES_A) as i:
                    tile_sums(pe, i, 0)
                with pe.Fori(0, BODIES_B) as i:
                    tile_sums(pe, i, TA)

        s_yn = sem("yn_ready")
        s_ynT = sem("yn_transposed")
        s_ynTc = sem("ynT_copied")
        s_logit = sem("logits_ready")
        s_b1 = sem("b1_transposed")
        s_diff = sem("top_difference_ready")
        s_etot = sem("expert_counts_ready")
        s_eoff = sem("expert_offsets_ready")

        def normalized(slot, b):
            return nc.vector.tensor_scalar(yn[:, slot, :], flat(acc[:, b, :]), rstd[:, b], shift[:, b], ALU.mult, ALU.add)

        with nc.Block() as block:
            @block.vector
            def _(dve):
                link = chain(dve, "dve_route")
                dve.sem_inc(s_logit, 2)
                moments(dve, link, 1)
                with dve.Fori(0, NB // 2) as b_2:
                    b = b_2 * 2
                    for u in range(2):
                        dve.wait_ge(s_ynT, b + (u + 1))
                        normalized(u, bass.ds(b + u, 1)).then_inc(s_yn, 1)
                dve.wait_ge(s_logit, NB + 2)
                link(nc.vector.tensor_tensor(logits[:, :, :], banks[7][:, 0:NB * X].rearrange("p (b e) -> p b e", b=NB),
                                             bg[:, :].unsqueeze(1).to_broadcast([P, NB, X]), ALU.add))
                rest = row_f[:, 0:X].unsqueeze(1).to_broadcast([P, NB, X])
                for k in range(TOP_K):
                    link(nc.vector.tensor_reduce(top[:, k, :], logits[:, :, :], AX_X, ALU.max))
                    link(nc.vector.tensor_tensor(hit[:, :, :], logits[:, :, :],
                                                 top[:, k, :].unsqueeze(2).to_broadcast([P, NB, X]), ALU.is_equal))
                    link(nc.vector.tensor_scalar(lead[:, :, :], rest, -1.0, float(X), ALU.mult, ALU.add))
                    link(nc.vector.tensor_tensor(hit[:, :, :], hit[:, :, :], lead[:, :, :], ALU.mult))
                    link(nc.vector.tensor_reduce(idx[k][:, :], hit[:, :, :], AX_X, ALU.max))
                    link(nc.vector.tensor_scalar(idx[k][:, :], idx[k][:, :], -1.0, float(X), ALU.mult, ALU.add))
                    if k == 0:
                        link(nc.vector.tensor_tensor(hit[:, :, :], rest, idx[k][:, :].unsqueeze(2).to_broadcast([P, NB, X]),
                                                     ALU.is_equal))
                        link(nc.vector.scalar_tensor_tensor(out=logits[:, :, :], in0=hit[:, :, :], scalar=-3e38,
                                                            in1=logits[:, :, :], op0=ALU.mult, op1=ALU.add))
                nc.vector.tensor_tensor(diff[:, :], top[:, 0, :], top[:, 1, :], ALU.subtract).then_inc(s_diff, 1)
                experts_f = row_f[:, 0:X].unsqueeze(2).to_broadcast([P, X, NB])
                for k in range(TOP_K):
                    link(nc.vector.tensor_tensor(eh[k][:, :, :], experts_f, idx[k][:, :].unsqueeze(1).to_broadcast([P, X, NB]),
                                                 ALU.is_equal))
                    link(nc.vector.tensor_tensor(eh[k][:, :, :], eh[k][:, :, :],
                                                 valid[:, :].unsqueeze(1).to_broadcast([P, X, NB]), ALU.mult))
                link(nc.vector.tensor_tensor(ehs[:, :, :], eh[0][:, :, :], eh[1][:, :, :], ALU.add))
                for e in range(X):
                    last = nc.vector.tensor_tensor_scan(out=esc[:, e, :], data0=ones[:, 0:NB], data1=ehs[:, e, :],
                                                        initial=0.0, op0=ALU.mult, op1=ALU.add)
                link(last)
                nc.vector.tensor_copy(etot[:, :], esc[:, :, NB - 1]).then_inc(s_etot, 1)
                dve.wait_ge(s_etot, 1)
                link(nc.vector.tensor_tensor(esc[:, :, :], esc[:, :, :], ehs[:, :, :], ALU.subtract))
                dve.wait_ge(s_eoff, 1)
                link(nc.vector.tensor_scalar(eti[:, :], banks[6][:, X:2 * X], float(FFN_ROWS - 1), None, ALU.add))
                link(nc.vector.tensor_scalar(eti[:, :], eti[:, :], FFN_ROWS.bit_length() - 1, None, ALU.arith_shift_right))
                link(nc.vector.tensor_copy(et[:, 0, :], eti[:, :]))
                link(nc.vector.tensor_tensor_scan(out=et[:, 1, :], data0=ones[:, 0:X], data1=et[:, 0, :], initial=0.0,
                                                  op0=ALU.mult, op1=ALU.add))
                link(nc.vector.tensor_tensor(et[:, 2, :], et[:, 1, :], et[:, 0, :], ALU.subtract))
                link(nc.vector.scalar_tensor_tensor(out=et[:, 3, :], in0=et[:, 2, :], scalar=float(FFN_ROWS),
                                                    in1=banks[6][:, 0:X], op0=ALU.mult, op1=ALU.add))
                link(nc.vector.tensor_tensor(esc[:, :, :], esc[:, :, :], et[:, 3, :].unsqueeze(2).to_broadcast([P, X, NB]),
                                             ALU.add))
                for k in range(TOP_K):
                    link(nc.vector.tensor_tensor(eh[k][:, :, :], eh[k][:, :, :], esc[:, :, :], ALU.mult))
                    link(nc.vector.tensor_reduce(posk_f[:, :], eh[k][:, :, :].rearrange("p e b -> p b e"), AX_X, ALU.add))
                    link(nc.vector.tensor_copy(posk[:, :, k], posk_f[:, :]))
                link(nc.vector.tensor_tensor(ecmp[:, :, 0:X - 1], row_f[:, 0:FT].unsqueeze(2).to_broadcast([P, FT, X - 1]),
                                             et[:, 1, 0:X - 1].unsqueeze(1).to_broadcast([P, FT, X - 1]), ALU.is_ge))
                link(nc.vector.tensor_reduce(esum[:, :], ecmp[:, :, 0:X - 1], AX_X, ALU.add))
                link(nc.vector.tensor_copy(expert[:, :], esum[:, :]))
                nc.vector.memset(fresh[:, 0:2], 1)
                link(nc.vector.tensor_tensor(fresh[:, 2:FT], esum[:, 2:FT], esum[:, 0:FT - 2], ALU.not_equal))

            @block.scalar
            def _(act):
                act.sem_inc(s_ynTc, 2)
                act.wait_ge(s_b1, 1)
                nc.scalar.copy(b1T[:, :], banks[5][:, 0:X * KH])
                act.wait_ge(s_var, 2)
                nc.scalar.activation(rstd[:, :], rstd[:, :], ACT.Sqrt).then_inc(s_sd, 1)
                with act.Fori(0, NB // 2) as b_2:
                    b = b_2 * 2
                    for u in range(2):
                        act.wait_ge(s_ynT, b + (u + 3))
                        nc.scalar.copy(ynT[:, u * KD:(u + 1) * KD, :],
                                       banks[u][:, 0:KD * P].rearrange("p (k m) -> p k m", k=KD)).then_inc(s_ynTc, 1)
                act.wait_ge(s_diff, 1)
                nc.scalar.activation(wk[0][:, :], diff[:, :], ACT.Sigmoid)
                nc.scalar.activation(wk[1][:, :], diff[:, :], ACT.Sigmoid, scale=-1.0)

            @block.tensor
            def _(pe):
                pe.sem_inc(s_ynT, 2)
                nc.tensor.transpose(banks[5][:, 0:X * KH], b1raw[:, :], ident[0:X * KH, 0:X * KH]).then_inc(s_b1, 1)
                def transposes(b, u):
                    pe.wait_ge(s_yn, b + (u + 1))
                    pe.wait_ge(s_ynTc, b + (u + 1))
                    for k in range(KD):
                        mm = nc.tensor.transpose(banks[u][:, k * P:(k + 1) * P], yn[:, u, k * P:(k + 1) * P], ident[:, :])
                    mm.then_inc(s_ynT, 1)

                def products(b, u):
                    pe.wait_ge(s_ynTc, b + (u + 3))
                    for k in range(KD):
                        mm = nc.tensor.matmul(banks[7][:, bass.ds((b + u) * X, X)], ynT[:, u * KD + k, :], wg[:, k, :],
                                              start=(k == 0), stop=(k == KD - 1))
                    mm.then_inc(s_logit, 1)
                for u in range(2):
                    transposes(0, u)
                with pe.Fori(0, NB // 2 - 1) as b_2:
                    for u in range(2):
                        products(b_2 * 2, u)
                        transposes(b_2 * 2 + 2, u)
                for u in range(2):
                    products(NB - 2, u)
                pe.wait_ge(s_etot, 1)
                nc.tensor.matmul(banks[6][:, 0:X], below[:, :], etot[:, :], start=True, stop=True)
                nc.tensor.matmul(banks[6][:, X:2 * X], ones[:, :], etot[:, :], start=True, stop=True).then_inc(s_eoff, 1)

        s_tok = sem("token_rows_ready")
        s_sent = [sem(f"rows_sent{u}") for u in range(4)]
        s_sfree = sem("token_rows_free")

        with nc.Block() as block:
            @block.vector
            def _(dve):
                def stage(b, u):
                    dve.wait_ge(s_sfree, b + (u + 1))
                    nc.vector.tensor_copy(placesk[:, u, :], flat(posk[:, bass.ds(b + u, 1), :]))
                    normalized(u, bass.ds(b + u, 1)).then_inc(s_tok, 1)
                with dve.Fori(0, (REAL - 1) // 4) as b_4:
                    b = b_4 * 4
                    for u in range(4):
                        stage(b, u)
                dve.wait_ge(s_sfree, REAL)
                nc.vector.tensor_copy(placesk[:, 0, :], posk[:, REAL - 1, :])
                normalized(0, slice(REAL - 1, REAL)).then_inc(s_tok, 1)

            @block.gpsimd
            def _(pool):
                def send(u, rows):
                    for k in range(TOP_K):
                        pool.indirect_dma_start(out=xs[:, :],
                                                out_offset=bass.IndirectOffsetOnAxis(ap=placesk[0:rows, u, k:k + 1], axis=0),
                                                in_=yn[0:rows, u, :], in_offset=None).then_inc(s_sent[u], 16)
                with pool.Fori(0, (REAL - 1) // 4) as b_4:
                    b = b_4 * 4
                    for u in range(4):
                        pool.wait_ge(s_tok, b + (u + 1))
                        pool.sem_inc(s_dummy, 1)
                        send(u, P)
                pool.wait_ge(s_tok, REAL)
                send(0, LAST)

            @block.sync
            def _(sp):
                sp.sem_inc(s_sfree, 4)
                with sp.Fori(0, (REAL - 1) // 4) as b_4:
                    b = b_4 * 4
                    for u in range(4):
                        sp.wait_ge(s_sent[u], 8 * b + 16 * TOP_K)
                        sp.sem_inc(s_sfree, 1)
                sp.wait_ge(s_sent[0], (REAL - 1) // 4 * 16 * TOP_K + 16 * TOP_K)

        edges.close()
        experts = ctx.enter_context(ExitStack())

        def buffers(name, shape, dt=F32, count=2):
            tiles = [experts.enter_context(nc.sbuf_tensor(f"{name}{n}", [P] + shape, dt)) for n in range(count)]
            return [t[:, :, :] for t in tiles]

        W1 = buffers("W1_", [KD, H])
        W2 = buffers("W2_", [KH, D])
        b2all = buffers("b2all", [X, D], count=1)[0]
        hidden = buffers("hidden", [KH, FFN_ROWS], count=1)[0]
        xg = buffers("xg", [2, D])
        yo = buffers("yo", [2, D])
        xgh = buffers("xgh", [KD, FFN_ROWS], F32R)
        xgl = buffers("xgl", [KD, FFN_ROWS], F32R)
        W1h, W1l = buffers("W1part", [KD, H], F32R)
        W2h, W2l = buffers("W2part", [KH, D], F32R)
        hh = buffers("hidden_hi", [KH, FFN_ROWS], F32R)
        hl = buffers("hidden_lo", [KH, FFN_ROWS], F32R)
        s_wl1 = [sem(f"first_weights_loaded{w}") for w in range(2)]
        s_wl2 = [sem(f"second_weights_loaded{w}") for w in range(2)]
        s_xg = [sem(f"expert_rows_loaded{u}") for u in range(2)]
        s_b2 = sem("b2_loaded")
        s_xT = sem("rows_transposed")
        s_xTc = sem("rows_T_ready")
        s_xh = sem("rows_hi_ready")
        s_w1h = sem("first_weights_hi_ready")
        s_w2h = sem("second_weights_hi_ready")
        s_w2l = sem("second_weights_lo_ready")
        s_hl = sem("hidden_lo_ready")
        s_w1l = sem("first_weights_lo_ready")
        s_mm1 = sem("hidden_ready")
        s_gelu = sem("gelu_ready")
        HB = 4
        s_mm2 = sem("expert_out_ready")
        s_yo = sem("expert_rows_ready")
        s_st = [sem(f"expert_rows_stored{u}") for u in range(2)]
        s_yofree = sem("expert_rows_free")

        def each_tile(eng, step, first=0):
            count = (FT - first) // RUN
            with eng.Fori(0, count) as i:
                for j in range(RUN):
                    step(i * RUN, j + first)
            for j in range(count * RUN + first, FT):
                step(count * RUN, j - count * RUN)

        def at(t, j):
            return bass.ds(t + j, 1) if not isinstance(t, int) else slice(t + j, t + j + 1)

        with nc.Block() as block:
            @block.sync
            def _(sp):
                def load(t, j):
                    u = j % 2
                    row0 = (t + j) * FFN_ROWS
                    e = sp.value_load(expert[0:1, at(t, j)], min_val=0, max_val=X - 1)
                    new = sp.value_load(fresh[0:1, at(t, j)], min_val=0, max_val=1)
                    sp.wait_ge(s_xT, t + (j + 1))
                    rows_of = xs[bass.ds(row0, FFN_ROWS), :] if not isinstance(row0, int) else xs[row0:row0 + FFN_ROWS, :]
                    sp.dma_start(xg[u], rows_of.rearrange("(s p) d -> p s d", p=P)).then_inc(s_xg[u], 16)
                    sp.wait_ge(s_w1l, t + (j + 1))
                    sp.dma_start(W1[u], f_w1[bass.ds(e, 1)].rearrange("a (k p) h -> p (a k) h", p=P), cond=new
                                 ).then_inc(s_wl1[u], 16)
                    sp.wait_ge(s_w2l, t + (j + 1))
                    sp.dma_start(W2[u], f_w2[bass.ds(e, 1)].rearrange("a (k p) d -> p (a k) d", p=P), cond=new
                                 ).then_inc(s_wl2[u], 16)
                each_tile(sp, load)

            @block.tensor
            def _(pe):
                pe.sem_inc(s_mm2, 2)
                pe.sem_inc(s_xT, 2)

                def turn_rows(t, j):
                    u = j % 2
                    pe.wait_ge(s_xg[u], t * 8 + 16 * (j // 2 + 1))
                    pe.wait_ge(s_xTc, t + (j + 1))
                    for k in range(KD):
                        for s in range(2):
                            mm = nc.tensor.transpose(banks[0][:, k * FFN_ROWS + s * P:k * FFN_ROWS + (s + 1) * P],
                                                     xg[u][:, s, k * P:(k + 1) * P], ident[:, :])
                    mm.then_inc(s_xT, 1)

                def up(t, j):
                    u = j % 2
                    pe.wait_ge(s_w1l, t + (j + 3))
                    pe.wait_ge(s_xTc, t + (j + 2))
                    for h in range(KH):
                        pe.wait_ge(s_gelu, t * KH + (KH * j + h + 1))
                        products = [(w_, x_, k) for k in range(KD) for w_, x_ in ((W1h, xgh), (W1h, xgl), (W1l, xgh))]
                        for n, (w_, x_, k) in enumerate(products):
                            mm = nc.tensor.matmul(banks[1 + h % HB][:, 0:FFN_ROWS], w_[:, k, h * P:(h + 1) * P],
                                                  x_[u][:, k, :], start=(n == 0), stop=(n == len(products) - 1))
                        mm.then_inc(s_mm1, 1)

                def down(t, j):
                    u = j % 2
                    pe.wait_ge(s_yo, t + (j + 1))
                    pe.wait_ge(s_w2l, t + (j + 3))
                    pe.wait_ge(s_hl, t * KH + KH * (j + 2))
                    for s in range(2):
                        products = [(h_, w_, h) for h in range(KH) for h_, w_ in ((hh, W2h), (hh, W2l), (hl, W2h))]
                        for n, (h_, w_, h) in enumerate(products):
                            mm = nc.tensor.matmul(banks[5 + u][:, s * D:(s + 1) * D], h_[u][:, h, s * P:(s + 1) * P],
                                                  w_[:, h, :], start=(n == 0), stop=(n == len(products) - 1))
                    mm.then_inc(s_mm2, 1)

                def step(t, j):
                    up(t, j)
                    if not (isinstance(t, int) and t + j + 1 == FT):
                        turn_rows(t, j + 1)
                    down(t, j - 1)
                turn_rows(0, 0)
                up(0, 0)
                turn_rows(0, 1)
                each_tile(pe, step, 1)
                down(FT - 1 - (FT - 1) % RUN, (FT - 1) % RUN)

            @block.scalar
            def _(act):
                act.sem_inc(s_gelu, HB)
                act.wait_ge(s_w1l, 3)
                act.dma_start(flat(b2all), f_b2.rearrange("e d -> (e d)").partition_broadcast(P)).then_inc(s_b2, 16)

                def gelus(t, j):
                    e = act.value_load(expert[0:1, at(t, j)], min_val=0, max_val=X - 1)
                    act.wait_ge(s_mm2, t + (j + 1))
                    for h in range(KH):
                        act.wait_ge(s_mm1, t * KH + (KH * j + h + 1))
                        act.wait_ge(s_hl, t * KH + (KH * j + h + 1))
                        for to in (hidden, hh[j % 2]):
                            last = nc.scalar.activation(to[:, h, :], banks[1 + h % HB][:, 0:FFN_ROWS],
                                                        ACT.Gelu, bias=b1T[:, bass.ds(e * KH + h, 1)])
                        last.then_inc(s_gelu, 1)
                each_tile(act, gelus)

            @block.vector
            def _(dve):
                dve.sem_inc(s_yo, 2)

                def turn(t, j):
                    dve.wait_ge(s_xT, t + (j + 3))
                    nc.vector.tensor_copy(flat(xgh[j % 2]), banks[0][:, :]).then_inc(s_xh, 1)
                    dve.wait_ge(s_xh, t + (j + 1))
                    nc.vector.tensor_tensor(flat(xgl[j % 2]), banks[0][:, :], flat(xgh[j % 2]).bitcast(F32), ALU.subtract
                                            ).then_inc(s_xTc, 1)

                def first_hi(t, j):
                    dve.wait_ge(s_wl1[j % 2], t * 8 + 16 * (j // 2 + 1))
                    if not (isinstance(t, int) and t + j == 0):
                        dve.wait_ge(s_mm1, t * KH + KH * j)
                    nc.vector.tensor_copy(W1h, W1[j % 2]).then_inc(s_w1h, 1)

                def first_lo(t, j):
                    dve.wait_ge(s_w1h, t + (j + 1))
                    nc.vector.tensor_tensor(W1l, W1[j % 2], W1h.bitcast(F32), ALU.subtract).then_inc(s_w1l, 1)

                def second_weights(t, j):
                    dve.wait_ge(s_wl2[j % 2], t * 8 + 16 * (j // 2 + 1))
                    dve.wait_ge(s_mm2, t + (j + 2))
                    nc.vector.tensor_copy(W2h, W2[j % 2]).then_inc(s_w2h, 1)
                    dve.wait_ge(s_w2h, t + (j + 1))
                    nc.vector.tensor_tensor(W2l, W2[j % 2], W2h.bitcast(F32), ALU.subtract).then_inc(s_w2l, 1)

                def finish(t, j):
                    e = dve.value_load(expert[0:1, at(t, j)], min_val=0, max_val=X - 1)
                    dve.wait_ge(s_mm2, t + (j + 3))
                    dve.wait_ge(s_yofree, t + (j + 1))
                    nc.vector.tensor_tensor(yo[j % 2], banks[5 + j % 2][:, :].rearrange("p (s d) -> p s d", s=2),
                                            b2all[:, bass.ds(e, 1), :].to_broadcast([P, 2, D]), ALU.add).then_inc(s_yo, 1)

                def step(t, j):
                    if not (isinstance(t, int) and t + j + 1 == FT):
                        first_hi(t, j + 1)
                        turn(t, j + 1)
                        first_lo(t, j + 1)
                    finish(t, j - 1)
                    second_weights(t, j)
                dve.sem_inc(s_xTc, 1)
                dve.sem_inc(s_w1l, 2)
                dve.sem_inc(s_w2l, 2)
                first_hi(0, 0)
                turn(0, 0)
                first_lo(0, 0)
                second_weights(0, 0)
                turn(0, 1)
                first_hi(0, 1)
                first_lo(0, 1)
                dve.wait_ge(s_b2, 16)
                each_tile(dve, step, 1)
                finish(FT - 1 - (FT - 1) % RUN, (FT - 1) % RUN)

            @block.gpsimd
            def _(pool):
                pool.sem_inc(s_yofree, 2)
                pool.sem_inc(s_hl, KH)

                def hidden_lo(t, j):
                    for h in range(KH):
                        pool.wait_ge(s_gelu, t * KH + (KH * j + HB + h + 1))
                        nc.gpsimd.tensor_tensor(hl[j % 2][:, h, :], hidden[:, h, :], hh[j % 2][:, h, :].bitcast(F32),
                                                ALU.subtract).then_inc(s_hl, 1)

                def store(t, j):
                    u = j % 2
                    row0 = (t + j) * FFN_ROWS
                    pool.wait_ge(s_yo, t + (j + 3))
                    pool.sem_inc(s_dummy, 1)
                    rows_of = os[bass.ds(row0, FFN_ROWS), :] if not isinstance(row0, int) else os[row0:row0 + FFN_ROWS, :]
                    pool.dma_start(rows_of.rearrange("(s p) d -> p s d", p=P), yo[u]).then_inc(s_st[u], 16)

                def release(t, j):
                    pool.wait_ge(s_st[j % 2], t * 8 + 16 * (j // 2 + 1))
                    pool.sem_inc(s_yofree, 1)

                def step(t, j):
                    hidden_lo(t, j)
                    if not (isinstance(t, int) and t + j == 1):
                        release(t, j - 2)
                    store(t, j - 1)
                hidden_lo(0, 0)
                step(0, 1)
                each_tile(pool, step, 2)
                last = FT - 1
                release(last - last % RUN, last % RUN - 1)
                store(last - last % RUN, last % RUN)
                release(last - last % RUN, last % RUN)

        s_stage = sem("places_back_staged")
        s_back = [sem(f"rows_back{u}") for u in range(BACKS)]
        s_mix = sem("token_mixed")
        s_res = sem("results_ready")
        s_out = [sem(f"out_stored{u}") for u in range(BACKS)]
        s_ofree = sem("result_buffers_free")
        experts.close()
        back = sb("back", [P, BACKS, 2, D])
        placesb = sb("placesb", [P, BACKS, TOP_K], I32)
        AHEAD = BACKS // 2
        WHOLE = REAL - 1
        assert WHOLE % BACKS == 0

        with nc.Block() as block:
            @block.gpsimd
            def _(pool):
                def fetch(b, u, rows=P):
                    pool.wait_ge(s_stage, b + (u + 1))
                    pool.sem_inc(s_dummy, 1)
                    for k in range(TOP_K):
                        pool.indirect_dma_start(out=back[0:rows, u, k, :], out_offset=None, in_=os[:, :],
                                                in_offset=bass.IndirectOffsetOnAxis(ap=placesb[0:rows, u, k:k + 1], axis=0)
                                                ).then_inc(s_back[u], 16)
                with pool.Fori(0, WHOLE // BACKS) as i:
                    for u in range(BACKS):
                        fetch(i * BACKS, u)
                fetch(WHOLE, 0, LAST)

            @block.vector
            def _(dve):
                def stage(b, u):
                    dve.wait_ge(s_ofree, b + (u + 1))
                    nc.vector.tensor_copy(placesb[:, u % BACKS, :], flat(posk[:, bass.ds(b + u, 1), :])).then_inc(s_stage, 1)

                def mix(b, u, rows=P):
                    dve.wait_ge(s_back[u], b * (16 * TOP_K // BACKS) + 16 * TOP_K)
                    block = bass.ds(b + u, 1)
                    nc.vector.scalar_tensor_tensor(out=back[0:rows, u, 0, :], in0=back[0:rows, u, 0, :],
                                                   scalar=wk[0][0:rows, block], in1=flat(acc[0:rows, block, :]),
                                                   op0=ALU.mult, op1=ALU.add).then_inc(s_mix, 1)
                    dve.wait_ge(s_mix, b + (u + 1))
                    nc.vector.scalar_tensor_tensor(out=back[0:rows, u, 1, :], in0=back[0:rows, u, 1, :],
                                                   scalar=wk[1][0:rows, block], in1=back[0:rows, u, 0, :],
                                                   op0=ALU.mult, op1=ALU.add).then_inc(s_res, 1)
                for u in range(AHEAD):
                    stage(0, u)
                with dve.Fori(0, WHOLE // BACKS - 1) as i:
                    for u in range(BACKS):
                        stage(i * BACKS, u + AHEAD)
                        mix(i * BACKS, u)
                for u in range(BACKS):
                    if u + AHEAD <= BACKS:
                        stage(WHOLE - BACKS, u + AHEAD)
                    mix(WHOLE - BACKS, u)
                mix(WHOLE, 0, LAST)

            @block.sync
            def _(sp):
                sp.sem_inc(s_ofree, BACKS)

                def store(b, u, rows=P):
                    sp.wait_ge(s_res, b + (u + 1))
                    to = out[bass.ds((b + u) * P, P), :] if rows == P else out[WHOLE * P:N, :]
                    sp.dma_start(to, back[0:rows, u, 1, :]).then_inc(s_out[u], 16)

                def release(b, u):
                    sp.wait_ge(s_out[u], b * (16 // BACKS) + 16)
                    sp.sem_inc(s_ofree, 1)
                with sp.Fori(0, WHOLE // BACKS) as i:
                    b = i * BACKS
                    for u in range(BACKS):
                        store(b, u)
                        if u >= 2:
                            release(b, u - 2)
                    for u in range(BACKS - 2, BACKS):
                        release(b, u)
                store(WHOLE, 0, LAST)
                sp.wait_ge(s_out[0], 16 * (WHOLE // BACKS + 1))


_INS = ["x", "src", "dst", "L0_gnn_W1", "L0_gnn_b1", "L0_gnn_W2", "L0_gnn_b2", "L0_gnn_wa1", "L0_gnn_ba1",
        "L0_gnn_wa2", "L0_gnn_ba2", "L0_ffn_Wg", "L0_ffn_bg", "L0_ffn_W1", "L0_ffn_b1", "L0_ffn_W2", "L0_ffn_b2"]


def kernel(**inputs):
    import numpy as _np
    import concourse.bacc as _bacc
    from concourse import mybir as _mybir
    from concourse.bass_utils import run_bass_kernel_spmd as _run

    nc = _bacc.Bacc("TRN2", target_bir_lowering=False, num_devices=1)
    arrays, args = {}, []
    for name in _INS:
        a = _np.ascontiguousarray(inputs[name])
        arrays[f"in_{name}_dram"] = a
        args.append(nc.dram_tensor(f"in_{name}_dram", a.shape, _mybir.dt.from_np(a.dtype), kind="ExternalInput").ap())
    shape = inputs["x"].shape
    out = nc.dram_tensor("out_dram", shape, _mybir.dt.float32, kind="ExternalOutput").ap()
    gnn_moe_kernel(nc, *args, out)
    r = _run(nc, [arrays], core_ids=[0])
    return r.results[0]["out_dram"]
```
